# Optimizing a Trainium2 kernel written in Bass

```python
import numpy as np
import jax
import jax.numpy as jnp

def _softmax(x, axis=-1):
    return jax.nn.softmax(x, axis=axis)

def _gelu(x):
    return jax.nn.gelu(x, approximate=True)

def _silu(x):
    return jax.nn.silu(x)

def _sigmoid(x):
    return jax.nn.sigmoid(x)

def _layernorm(x, axis=-1, eps=1e-05):
    m = jnp.mean(x, axis=axis, keepdims=True)
    v = jnp.var(x, axis=axis, keepdims=True)
    return (x - m) / jnp.sqrt(v + eps)

def _scatter_add(tgt, idx, src, axis=0):
    return tgt.at[idx].add(src)

def _segment_sum(src, seg, n):
    return jax.ops.segment_sum(src, seg, n)
kernel_name = 'mk_adj_preln_d4_adj_r2_131708'

def setup_inputs(seed: int=0):
    np.random.seed(seed)
    _w = jnp.asarray

    def _rec_inputs():
        import jax
        import jax.numpy as jnp
        _gk = jax.random.key(seed)
        x = -0.003407 + 1.001 * jax.random.normal(jax.random.fold_in(_gk, 1), (2048, 64), jnp.float32)
        _a = jax.random.bernoulli(jax.random.fold_in(_gk, 2), 0.0078125, (2048, 2048))
        adj = _a.astype(jnp.int32)
        return (x, adj)
    x, adj = _rec_inputs()

    def _L0_gnn_setup():
        import jax, jax.numpy as jnp
        import numpy as np
        N = 1024
        ATOM_D = 64
        H = 8
        NB = 8
        D = ATOM_D * H
        NEG_SLOPE = 0.2
        key = jax.random.key(seed)
        ks = jax.random.split(key, 12)
        inp = {'atom_embeddings': jax.random.normal(ks[0], (N, ATOM_D), dtype=jnp.float32), 'edges': jax.random.randint(ks[1], (N, N), -1, NB, dtype=jnp.int32), 'Qw': jax.random.normal(ks[2], (ATOM_D, D), dtype=jnp.float32) / np.sqrt(ATOM_D), 'Qb': jnp.zeros((D,), dtype=jnp.float32), 'Kw': jax.random.normal(ks[3], (ATOM_D, D), dtype=jnp.float32) / np.sqrt(ATOM_D), 'Kb': jnp.zeros((D,), dtype=jnp.float32), 'Vw': jax.random.normal(ks[4], (ATOM_D, D), dtype=jnp.float32) / np.sqrt(ATOM_D), 'Vb': jnp.zeros((D,), dtype=jnp.float32), 'a': jax.random.normal(ks[5], (NB, 2 * D, H), dtype=jnp.float32) * np.sqrt(2.0 / (2 * D + H)) * 1.414, 'Pw': jax.random.normal(ks[6], (D, ATOM_D), dtype=jnp.float32) / np.sqrt(D), 'Pb': jnp.zeros((ATOM_D,), dtype=jnp.float32)}
        return inp
    _L0_gnn_all = _L0_gnn_setup()
    _L0_gnn_in = {k: v for k, v in _L0_gnn_all.items() if k in ('Qw', 'Qb', 'Kw', 'Kb', 'Vw', 'Vb', 'a', 'Pw', 'Pb')}
    del _L0_gnn_all

    def _L1_gnn_setup():
        import jax, jax.numpy as jnp
        import numpy as np
        N = 2048
        OUT = 64
        EMB = 8
        K_TAYLOR = 4
        EPS = 1e-12
        key = jax.random.key(seed)
        k1, k2, k3, k4 = jax.random.split(key, 4)
        h = jax.random.normal(k1, (N, OUT), dtype=jnp.float32)
        adj = jax.random.randint(k2, (N, N), 0, 2, dtype=jnp.int32)
        w_k = jax.random.normal(k3, (OUT, EMB), dtype=jnp.float32)
        w_q = jax.random.normal(k4, (OUT, EMB), dtype=jnp.float32)
        return {'h': h, 'adj': adj, 'w_k': w_k, 'w_q': w_q}
    _L1_gnn_all = _L1_gnn_setup()
    _L1_gnn_in = {k: v for k, v in _L1_gnn_all.items() if k in ('w_k', 'w_q')}
    del _L1_gnn_all

    def _L2_gnn_setup():
        import jax, jax.numpy as jnp
        import numpy as np
        ALPHA = 0.2
        NEG_INF = -9000000000000000.0
        key = jax.random.key(seed)
        k1, k2, k3, k4 = jax.random.split(key, 4)
        N, F_IN, F_OUT = (512, 64, 64)
        h = jax.random.normal(k1, (N, F_IN), dtype=jnp.float32)
        adj = jax.random.randint(k2, (N, N), 0, 2, dtype=jnp.int32)
        lim_W = 1.414 * np.sqrt(6.0 / (F_IN + F_OUT))
        W = jax.random.uniform(k3, (F_IN, F_OUT), minval=-lim_W, maxval=lim_W, dtype=jnp.float32)
        lim_a = 1.414 * np.sqrt(6.0 / (2 * F_OUT + 1))
        a = jax.random.uniform(k4, (2 * F_OUT, 1), minval=-lim_a, maxval=lim_a, dtype=jnp.float32)
        return {'h': h, 'adj': adj, 'W': W, 'a': a}
    _L2_gnn_all = _L2_gnn_setup()
    _L2_gnn_in = {k: v for k, v in _L2_gnn_all.items() if k in ('W', 'a')}
    del _L2_gnn_all

    def _L3_gnn_setup():
        import jax, jax.numpy as jnp
        import numpy as np
        EPS = 1e-07

        def _mobius_add(x, y):
            x2 = jnp.sum(x * x, axis=-1, keepdims=True)
            y2 = jnp.sum(y * y, axis=-1, keepdims=True)
            xy = jnp.sum(x * y, axis=-1, keepdims=True)
            num = (1.0 + 2.0 * xy + y2) * x + (1.0 - x2) * y
            den = 1.0 + 2.0 * xy + x2 * y2
            return num / jnp.maximum(den, EPS)

        def _lambda_x(x):
            return 2.0 / jnp.clip(1.0 - jnp.sum(x * x, axis=-1, keepdims=True), EPS, None)

        def _logmap(y, x):
            u = _mobius_add(-x, y)
            un = jnp.clip(jnp.linalg.norm(u, axis=-1, keepdims=True), EPS, 1.0 - 1e-05)
            return 2.0 / _lambda_x(x) * jnp.arctanh(un) * (u / un)

        def _expmap(v, x):
            vn = jnp.clip(jnp.linalg.norm(v, axis=-1, keepdims=True), EPS, None)
            second = jnp.tanh(_lambda_x(x) * vn * 0.5) * (v / vn)
            return _mobius_add(x, second)
        key = jax.random.key(seed)
        k1, k2 = jax.random.split(key)
        N, D = (512, 64)
        u = jax.random.normal(k1, (N, D), dtype=jnp.float32)
        x = 0.5 * u / (1.0 + jnp.linalg.norm(u, axis=-1, keepdims=True))
        adj = jax.random.randint(k2, (N, N), 0, 2, dtype=jnp.int32)
        return {'x': x, 'adj': adj}
    _L3_gnn_all = _L3_gnn_setup()
    _L3_gnn_in = {k: v for k, v in _L3_gnn_all.items() if k in ()}
    del _L3_gnn_all
    return {'x': x, 'adj': adj, 'L0_gnn_Qw': _L0_gnn_in['Qw'], 'L0_gnn_Qb': _L0_gnn_in['Qb'], 'L0_gnn_Kw': _L0_gnn_in['Kw'], 'L0_gnn_Kb': _L0_gnn_in['Kb'], 'L0_gnn_Vw': _L0_gnn_in['Vw'], 'L0_gnn_Vb': _L0_gnn_in['Vb'], 'L0_gnn_a': _L0_gnn_in['a'], 'L0_gnn_Pw': _L0_gnn_in['Pw'], 'L0_gnn_Pb': _L0_gnn_in['Pb'], 'L1_gnn_w_k': _L1_gnn_in['w_k'], 'L1_gnn_w_q': _L1_gnn_in['w_q'], 'L2_gnn_W': _L2_gnn_in['W'], 'L2_gnn_a': _L2_gnn_in['a']}

def reference(x, adj, L0_gnn_Qw, L0_gnn_Qb, L0_gnn_Kw, L0_gnn_Kb, L0_gnn_Vw, L0_gnn_Vb, L0_gnn_a, L0_gnn_Pw, L0_gnn_Pb, L1_gnn_w_k, L1_gnn_w_q, L2_gnn_W, L2_gnn_a):
    import jax
    import jax.numpy as jnp

    def _L0_gnn_ref(atom_embeddings, edges, Qw, Qb, Kw, Kb, Vw, Vb, a, Pw, Pb):
        import jax, jax.numpy as jnp
        import numpy as np
        N = 1024
        ATOM_D = 64
        H = 8
        NB = 8
        D = ATOM_D * H
        NEG_SLOPE = 0.2
        n, d = atom_embeddings.shape
        nb, two_d, h = a.shape
        D_ = two_d // 2
        Q = atom_embeddings @ Qw + Qb
        K = atom_embeddings @ Kw + Kb
        V = atom_embeddings @ Vw + Vb
        A1 = a[:, :D_, :]
        A2 = a[:, D_:, :]
        S1 = jnp.einsum('id,kdh->ikh', Q, A1)
        S2 = jnp.einsum('jd,kdh->jkh', K, A2)
        kidx = jnp.clip(edges, 0, nb - 1)
        rows = jnp.arange(n)
        e = S1[rows[:, None], kidx] + S2[rows[None, :], kidx]
        valid = (edges >= 0)[..., None]
        e = jnp.where(valid, jax.nn.leaky_relu(e, negative_slope=NEG_SLOPE), 0.0)
        attn = jax.nn.softmax(e, axis=1)
        Vh = V.reshape(n, h, d)
        out = jnp.einsum('ijh,jhd->ihd', attn, Vh).reshape(n, h * d)
        return out @ Pw + Pb

    def _L1_gnn_ref(h, adj, w_k, w_q):
        import jax, jax.numpy as jnp
        import numpy as np
        N = 2048
        OUT = 64
        EMB = 8
        K_TAYLOR = 4
        EPS = 1e-12
        h = h - h.mean(axis=-1, keepdims=True)
        h = h / jnp.maximum(jnp.linalg.norm(h, axis=-1, keepdims=True), EPS)
        k = h @ w_k
        q = h @ w_q
        scores = k @ q.T / jnp.sqrt(jnp.float32(EMB))
        a_att = jax.nn.softmax(scores, axis=-1)
        a = adj.astype(jnp.float32) * a_att
        a = a / a.sum(axis=-1, keepdims=True)
        result = a
        fact = 1.0
        for i in range(2, K_TAYLOR):
            a = a @ a
            fact = fact * i
            result = result + a / fact
        return result @ h

    def _L2_gnn_ref(h, adj, W, a):
        import jax, jax.numpy as jnp
        import numpy as np
        ALPHA = 0.2
        NEG_INF = -9000000000000000.0
        F_OUT = W.shape[1]
        Wh = h @ W
        a1, a2 = (a[:F_OUT, 0], a[F_OUT:, 0])
        e = (Wh @ a1)[:, None] + (Wh @ a2)[None, :]
        e = jax.nn.leaky_relu(e, negative_slope=ALPHA)
        scores = jnp.where(adj > 0, e, jnp.float32(NEG_INF))
        attention = jax.nn.softmax(scores, axis=1)
        h_prime = attention @ Wh
        return jax.nn.elu(h_prime)

    def _L3_gnn_ref(x, adj):
        import jax, jax.numpy as jnp
        import numpy as np
        EPS = 1e-07

        def _mobius_add(x, y):
            x2 = jnp.sum(x * x, axis=-1, keepdims=True)
            y2 = jnp.sum(y * y, axis=-1, keepdims=True)
            xy = jnp.sum(x * y, axis=-1, keepdims=True)
            num = (1.0 + 2.0 * xy + y2) * x + (1.0 - x2) * y
            den = 1.0 + 2.0 * xy + x2 * y2
            return num / jnp.maximum(den, EPS)

        def _lambda_x(x):
            return 2.0 / jnp.clip(1.0 - jnp.sum(x * x, axis=-1, keepdims=True), EPS, None)

        def _logmap(y, x):
            u = _mobius_add(-x, y)
            un = jnp.clip(jnp.linalg.norm(u, axis=-1, keepdims=True), EPS, 1.0 - 1e-05)
            return 2.0 / _lambda_x(x) * jnp.arctanh(un) * (u / un)

        def _expmap(v, x):
            vn = jnp.clip(jnp.linalg.norm(v, axis=-1, keepdims=True), EPS, None)
            second = jnp.tanh(_lambda_x(x) * vn * 0.5) * (v / vn)
            return _mobius_add(x, second)
        mask = adj > 0
        logs = jax.vmap(lambda xi: _logmap(x, xi))(x)
        v = jnp.sum(jnp.where(mask[..., None], logs, 0.0), axis=1)
        return _expmap(v, x)
    h = jnp.maximum(_layernorm(x, axis=-1), 0.0)
    x = x + _L0_gnn_ref(h, adj, L0_gnn_Qw, L0_gnn_Qb, L0_gnn_Kw, L0_gnn_Kb, L0_gnn_Vw, L0_gnn_Vb, L0_gnn_a, L0_gnn_Pw, L0_gnn_Pb)
    h = jnp.maximum(_layernorm(x, axis=-1), 0.0)
    x = x + _L1_gnn_ref(h, adj, L1_gnn_w_k, L1_gnn_w_q)
    h = jnp.maximum(_layernorm(x, axis=-1), 0.0)
    x = x + _L2_gnn_ref(h, adj, L2_gnn_W, L2_gnn_a)
    h = jnp.maximum(_layernorm(x, axis=-1), 0.0)
    x = x + _L3_gnn_ref(h, adj)
    return x

_drawn_inputs = setup_inputs


def setup_inputs(seed=0):
    import zlib

    import numpy as np

    out = dict(_drawn_inputs(seed))
    spreads = {'L0_gnn_Qb': (0.0, 2.0),
     'L0_gnn_Kb': (0.0, 2.0),
     'L0_gnn_Vb': (0.0, 0.1),
     'L0_gnn_Pb': (0.0, 0.1)}
    factors = {'L0_gnn_Qw': 3.097}
    for name, (base, spread) in spreads.items():
        noise = np.random.default_rng([zlib.crc32(name.encode()), seed]).standard_normal(out[name].shape)
        drawn = base * np.exp(spread * noise) if base else spread * noise
        out[name] = jnp.asarray(drawn.astype(out[name].dtype))
    for name, factor in factors.items():
        out[name] = (out[name] * factor).astype(out[name].dtype)
    return out
```

```python
import math
from contextlib import ExitStack

import concourse.bass as bass
from concourse import mybir

P = 128
ALU = mybir.AluOpType
ACT = mybir.ActivationFunctionType
AX = mybir.AxisListType
F32 = mybir.dt.float32
BF16 = mybir.dt.bfloat16
U8 = mybir.dt.uint8
I32 = mybir.dt.int32

LN_EPS = 1e-5
NORM_EPS = 1e-12
BALL_EPS = 1e-7
SLOPE = 0.2
MASKED = -9e15


def gnn_stack(nc, x_d, adj_d, Qw, Qb, Kw, Kb, Vw, Vb, a_rel, Pw, Pb, w_k, w_q, W2, a2, out_d):
    N, D = x_d.shape
    NT = N // P
    H = a_rel.shape[2]
    DM = Qw.shape[1]
    DC = DM // P
    REL = 2
    E = w_k.shape[1]
    HALF = 512
    TW = 2 * HALF
    NB = N // TW
    PARTS = 3
    DA = D + 1
    DX = D + 2
    RING = 16
    BLOCKS = N // HALF
    PER_HEAD = BLOCKS * NT
    PAIR = 2 * PER_HEAD
    SLOTS = 4
    NQ = 2 * REL * H

    ctx = ExitStack()
    with ctx:
        def sb(name, shape, dt=F32):
            return ctx.enter_context(nc.sbuf_tensor(name, shape, dt))

        big = sb("big", [P, NT * N])
        mask = sb("mask", [P, NT, N], U8)
        x = sb("x_nat", [P, NT, D])
        h = sb("h_nat", [P, NT, DX])
        hT = sb("hT", [P, N])
        work = sb("work", [P, NT, D])
        ident = sb("ident", [P, P])
        identb = sb("identb", [P, P], BF16)
        onesf = sb("onesf", [P, P])
        stat = sb("stat", [P, 8, NT])
        small = sb("small", [P, 64])
        op_l = sb("op_l", [P, 2, N], BF16)
        op_r = sb("op_r", [P, 2, N], BF16)
        wall = sb("wall", [DA, NQ])
        arel = sb("arel", [P, REL, 2 * DC, H])
        pb = sb("pb", [P, D])
        wkq = sb("wkq", [D, 2 * E])
        w2 = sb("w2", [D, D])
        w2T = sb("w2T", [D, D])
        a12 = sb("a12", [D, 2])
        w2a = sb("w2a", [D, 2])

        at = [0]

        def part(n, shape=None):
            v = big[:, at[0]:at[0] + n]
            at[0] += n
            return v
        outT = part(H * N).rearrange("p (h n) -> p h n", h=H)
        ring = part(RING * HALF).rearrange("p (r n) -> p r n", r=RING)
        mrow = part(2 * N).rearrange("p (b n) -> p b n", b=2)
        vst = part(2 * NT * DA).rearrange("p (b t d) -> p b t d", b=2, t=NT)
        used0 = at[0]
        assert used0 <= NT * N
        at[0] = 0
        vp = part(NT * H * DA).rearrange("p (h t d) -> p h t d", h=H, t=NT)
        s_nat = part(NQ * NT).rearrange("p (q t) -> p q t", q=NQ)
        s_rem = part(NQ * NT).rearrange("p (q t) -> p q t", q=NQ)
        split = part(NQ * PARTS * NT // 2).bitcast(BF16).rearrange("p (q c t) -> p q c t", q=NQ, c=PARTS)
        splitT = part(NQ * PARTS * NT // 2).bitcast(BF16)
        m_nat = part(REL * H * NT).rearrange("p (q t) -> p q t", q=REL * H)
        m_tmp = part(REL * H * NT).rearrange("p (q t) -> p q t", q=REL * H)
        mT = part(P)
        wload = part(3 * DM).rearrange("p (w n) -> p w n", w=3)[0:DA, :, :]
        wT = part(3 * DC * DA).rearrange("p (w c n) -> p w c n", w=3, c=DC)
        pw = part(DC * D).rearrange("p (c n) -> p c n", c=DC)
        assert at[0] <= H * N
        adjb = ring.rearrange("p r n -> p (r n)").bitcast(BF16).rearrange("p (r n) -> p r n", n=N)
        NADJ = RING * HALF * 2 // N
        eT = big[:, :].rearrange("p (t n) -> p t n", t=NT)
        kqT = op_l[:, :, :].rearrange("p b n -> p (b n)").bitcast(F32)
        qT = op_r[:, :, :].rearrange("p b n -> p (b n)").bitcast(F32)
        y = sb("y_nat", [P, NT, D])
        yT = hT
        at[0] = 0
        lhs3 = part(N)
        rden = part(N)
        rdis = part(N)
        g3 = part(2 * NT * DX).rearrange("p (v t d) -> p v t d", v=2, t=NT)
        NW = 5
        wA = part(NW * TW).rearrange("p (r n) -> p r n", r=NW)
        wB = part(NW * TW).rearrange("p (r n) -> p r n", r=NW)
        wC = part(NW * TW).rearrange("p (r n) -> p r n", r=NW)
        wD = part(NW * TW).rearrange("p (r n) -> p r n", r=NW)
        z = part(NT * DX).rearrange("p (t d) -> p t d", t=NT)
        w3 = part(NT * D).rearrange("p (t d) -> p t d", t=NT)
        assert at[0] <= NT * N

        ps = ctx.enter_context(nc.psum_tensor("ps", [P, 8, HALF], F32))
        psb = ps[:, :, :].rearrange("p b n -> p (b n)").bitcast(BF16).rearrange("p (b n) -> p b n", b=8)

        split_d = nc.dram_tensor("split_scratch", [NQ, PARTS, N], BF16, kind="Internal").ap()
        split2_d = nc.dram_tensor("split2_scratch", [4, PARTS, N], BF16, kind="Internal").ap()
        m_d = nc.dram_tensor("max_scratch", [H, N], F32, kind="Internal").ap()
        m2_d = nc.dram_tensor("max2_scratch", [1, N], F32, kind="Internal").ap()
        vp_d = nc.dram_tensor("value_scratch", [H, P, NT * DA], F32, kind="Internal").ap()

        names = """x_in w_in a_in l12_in rows_in staged0 staged1 rows_out split_out m_out vp_out
            out_done ids ids2 ones dve_chain act_chain pool_chain
            adj_turned adj_copied adj_copied_b ln_var ln_std h_ready h_turned hT_ready
            w_turned w_copied wa_done wall_ready s_done s_read mx_done mx_read mxrow mxb m_ready split_ready
            split_turned split_copied m_turned m_copied vw_done vw_ready vp_done vp_read vp_ones
            scores scores_seen selected relus leaked shifted weights products acc_free
            out_turned out_taken x_ready norm_sq norm_rt kq_done kq_ready kqn_done kqn_read big_ready
            kq_t big_b big_s big_bias e_scores e_exp e_masked e_products y_read y_turned y_ready y_products
            ops2 wh_done wh_ready s2_done x2 den dis den_c dis_c logs ratio ratioc un l1 l2 art scl scl_e wgt wm3 sums
            z_read z_turned z_ready v_sq v_rt th_in th sec_done g_ready g_turned g_read""".split()
        s = {n: ctx.enter_context(nc.semaphore(n)) for n in names}
        adj_in = [ctx.enter_context(nc.semaphore(f"adj_in{n}")) for n in range(NADJ)]
        staged = [s["staged0"], s["staged1"]]
        STAGED = 16 * (4 * 2 + 2)

        def bc(v, n=D):
            return v.unsqueeze(2).to_broadcast([P, NT, n])

        def row_group(op, b, g, r0, n):
            return op[32 * g + r0:32 * g + r0 + n, b, :]

        block = ctx.enter_context(nc.Block())

        @block.sync
        def _(sp):
            def stage(b, sq, s2q, m_row, v_src):
                for g in range(4):
                    sp.dma_start(row_group(op_l, b, g, 0, PARTS), s2q(g // 2)).then_inc(staged[b], 16)
                    sp.dma_start(row_group(op_r, b, g, PARTS, PARTS), sq(g // 2)).then_inc(staged[b], 16)
                sp.dma_start(mrow[:, b, :], m_row.to_broadcast([P, N])).then_inc(staged[b], 16)
                sp.dma_start(vst[:, b, :, :].rearrange("p t d -> p (t d)"), v_src).then_inc(staged[b], 16)

            sp.dma_start(x[:, :, :], x_d.rearrange("(t p) d -> p t d", p=P)).then_inc(s["x_in"], 16)
            for n, (w, b) in enumerate(((Qw, Qb), (Kw, Kb), (Vw, Vb))):
                sp.dma_start(wload[0:D, n, :], w).then_inc(s["w_in"], 16)
                sp.dma_start(wload[D:DA, n, :], b.rearrange("(o n) -> o n", o=1)).then_inc(s["w_in"], 16)
            for r in range(REL):
                sp.dma_start(arel[:, r, :, :], a_rel[r, :, :].rearrange("(c p) h -> p c h", p=P))\
                    .then_inc(s["a_in"], 16)
            sp.dma_start(pw[:, :, :], Pw.rearrange("(c p) n -> p c n", p=P)).then_inc(s["a_in"], 16)
            sp.dma_start(pb[:, :], Pb.rearrange("(o n) -> o n", o=1).to_broadcast([P, D])).then_inc(s["l12_in"], 16)
            sp.dma_start(wkq[:, 0:E], w_k).then_inc(s["l12_in"], 16)
            sp.dma_start(wkq[:, E:2 * E], w_q).then_inc(s["l12_in"], 16)
            sp.dma_start(w2[:, :], W2).then_inc(s["l12_in"], 16)
            with nc.allow_non_contiguous_dma(reason="128 values"):
                sp.dma_start(a12[:, :], a2.rearrange("(c p) o -> p (c o)", c=2)).then_inc(s["l12_in"], 16)
            sp.wait_ge(s["split_copied"], 1)
            for c in range(NQ * PARTS * NT // P):
                sp.dma_start(split_d.rearrange("q c (t n) -> (q c t) n", n=P)[c * P:(c + 1) * P, :],
                             splitT[:, c * P:(c + 1) * P]).then_inc(s["rows_out"], 16)
            sp.wait_ge(s["m_copied"], 1)
            sp.dma_start(m_d.rearrange("h (t n) -> (h t) n", n=P), mT[:, :]).then_inc(s["m_out"], 16)
            sp.wait_ge(s["vp_ones"], 1)
            sp.wait_ge(s["vp_read"], NT)
            sp.dma_start(vp_d.rearrange("h p n -> p h n"), vp.rearrange("p h t d -> p h (t d)"))\
                .then_inc(s["vp_out"], 16)
            sp.wait_ge(s["rows_out"], 16 * (NQ * PARTS * NT // P))
            sp.wait_ge(s["m_out"], 16)
            sp.wait_ge(s["vp_out"], 16)
            sp.wait_ge(s["ones"], 3)

            def stage_head(b, head):
                stage(b, lambda r: split_d[bass.ds(head + r * H, 1), :, :].rearrange("o c n -> (o c) n"),
                      lambda r: split_d[bass.ds(head + (REL + r) * H, 1), :, :].rearrange("o c n -> (o c) n"),
                      m_d[bass.ds(head, 1), :], vp_d[bass.ds(head, 1), :, :].rearrange("o p n -> (o p) n"))

            stage_head(0, 0)
            stage_head(1, 1)
            with sp.Fori(1, H // 2) as i:
                for b in range(2):
                    sp.wait_ge(s["acc_free"], i * (2 * BLOCKS) + (b - 1) * BLOCKS)
                    stage_head(b, i * 2 + b)
            sp.wait_ge(s["split_copied"], 2)
            sp.dma_start(split2_d.rearrange("q c (t n) -> (q c t) n", n=P)[0:96, :], splitT[0:96, 0:P])\
                .then_inc(s["rows_out"], 16)
            sp.dma_start(split2_d.rearrange("q c (t n) -> (q c t) n", n=P)[96:192, :], splitT[0:96, P:2 * P])\
                .then_inc(s["rows_out"], 16)
            sp.wait_ge(s["m_copied"], 2)
            sp.dma_start(m2_d.rearrange("h (t n) -> (h t) n", n=P), mT[0:NT, :]).then_inc(s["m_out"], 16)
            sp.wait_ge(s["rows_out"], 16 * (NQ * PARTS * NT // P + 2))
            sp.wait_ge(s["m_out"], 32)
            sp.wait_ge(s["ones"], 5)
            for g in range(4):
                sp.dma_start(row_group(op_l, 0, g, 0, PARTS), split2_d[2 + g // 2, :, :]).then_inc(s["ops2"], 16)
                sp.dma_start(row_group(op_r, 0, g, PARTS, PARTS), split2_d[g // 2, :, :]).then_inc(s["ops2"], 16)
            sp.dma_start(mrow[:, 0, :], m2_d[0:1, :].to_broadcast([P, N])).then_inc(s["ops2"], 16)
            sp.wait_ge(s["x_ready"], 4)
            sp.dma_start(out_d.rearrange("(t p) d -> p t d", p=P), x[:, :, :]).then_inc(s["out_done"], 16)
            sp.wait_ge(s["out_done"], 16)

        TILES0 = H * PER_HEAD
        LAG_W, LAG_P = 5, 7

        @block.gpsimd
        def _(pool):
            for t in range(NADJ):
                pool.dma_start(adjb[:, t, :], adj_d[t * P:(t + 1) * P, :]).then_inc(adj_in[t], 16)
            pool.memset(ident[:, :], 0.0).then_inc(s["ids"], 1)
            pool.memset(identb[:, :], 0.0).then_inc(s["ids"], 1)
            pool.wait_ge(s["ids"], 2)
            for m in (ident, identb):
                pool.affine_select(out=m[:, :], in_=m[:, :], compare_op=ALU.not_equal, fill=1.0, base=0,
                                   pattern=[[-1, P]], channel_multiplier=1).then_inc(s["ids2"], 1)
            pool.memset(op_l[:, :, :], 1.0).then_inc(s["ones"], 1)
            pool.memset(op_r[:, :, :], 1.0).then_inc(s["ones"], 1)
            pool.memset(onesf[:, :], 1.0).then_inc(s["ones"], 1)
            for t in range(NADJ, NT):
                pool.wait_ge(s["adj_turned"], 2 * (t - NADJ) + 2)
                pool.dma_start(adjb[:, t % NADJ, :], adj_d[t * P:(t + 1) * P, :])\
                    .then_inc(adj_in[t % NADJ], 16)

            def shift(k, kk, b):
                i0 = kk // NT % BLOCKS * HALF
                pool.wait_ge(s["leaked"], k + 1)
                pool.tensor_tensor(ring[:, kk % RING, :], ring[:, kk % RING, :], mrow[:, b, i0:i0 + HALF],
                                   ALU.subtract).then_inc(s["shifted"], 1)

            with pool.Fori(0, H // 2) as i:
                for kk in range(PAIR):
                    shift(i * PAIR + kk, kk, kk // PER_HEAD)
            pool.wait_ge(s["big_bias"], 1)
            pool.wait_ge(s["e_products"], NB * NT)
            pool.memset(op_l[:, :, :], 1.0).then_inc(s["ones"], 1)
            pool.memset(op_r[:, :, :], 1.0).then_inc(s["ones"], 1)
            for kk in range(PER_HEAD):
                shift(TILES0 + kk, kk, 0)
            for k in range(NB * NT + 1):
                if k < NB * NT:
                    u = k % NW
                    pool.wait_ge(s["logs"], 2 * k + 2)
                    pool.tensor_tensor(wB[:, u, :], wB[:, u, :], wA[:, u, :], ALU.subtract).then_inc(s["ratio"], 1)
                if k >= 1:
                    u = (k - 1) % NW
                    pool.wait_ge(s["l2"], k)
                    pool.tensor_tensor(wD[:, u, :], wD[:, u, :], wC[:, u, :], ALU.subtract).then_inc(s["art"], 1)

        @block.vector
        def _(dve):
            chain = [0]

            def link(ins):
                chain[0] += 1
                ins.then_inc(s["dve_chain"], 1)
                dve.wait_ge(s["dve_chain"], chain[0])

            def ts(out, in_, s1, s2, o0, o1=None):
                if o1 is None:
                    return dve.tensor_scalar(out, in_, s1, None, o0)
                return dve.tensor_scalar(out, in_, s1, s2, o0, o1)

            def tt(out, a, b, op):
                return dve.tensor_tensor(out, a, b, op)

            roots = [0]

            def root(dst, var):
                ts(stat[:, 4, :], var, 1.0, None, ALU.mult).then_inc(s["ln_var"], 1)
                roots[0] += 1
                dve.wait_ge(s["ln_std"], roots[0])
                link(dve.reciprocal(stat[:, 6, :], stat[:, 5, :]))
                link(tt(stat[:, 6, :], stat[:, 6, :], var, ALU.mult))
                link(tt(stat[:, 6, :], stat[:, 6, :], stat[:, 5, :], ALU.add))
                link(ts(stat[:, 6, :], stat[:, 6, :], 0.5, None, ALU.mult))
                link(dve.reciprocal(dst, stat[:, 6, :]))

            def center(v):
                link(dve.reduce_sum(stat[:, 0, :], v, AX.X))
                link(ts(stat[:, 0, :], stat[:, 0, :], 1.0 / D, None, ALU.mult))
                link(tt(work[:, :, :], v, bc(stat[:, 0, :]), ALU.subtract))

            def sum_squares(dst, v, scratch):
                link(tt(scratch, v, v, ALU.mult))
                link(dve.reduce_sum(dst, scratch, AX.X))

            def layer_norm(last=True):
                center(x[:, :, :])
                sum_squares(stat[:, 1, :], work[:, :, :], h[:, :, 0:D])
                link(ts(stat[:, 1, :], stat[:, 1, :], 1.0 / D, LN_EPS, ALU.mult, ALU.add))
                root(stat[:, 2, :], stat[:, 1, :])
                link(tt(work[:, :, :], work[:, :, :], bc(stat[:, 2, :]), ALU.mult))
                r = ts(h[:, :, 0:D], work[:, :, :], 0.0, None, ALU.max)
                if last:
                    r.then_inc(s["h_ready"], 1)
                else:
                    link(r)

            def split3(src, rem, dst):
                link(dve.tensor_copy(dst[:, :, 0, :], src))
                link(tt(rem, src, dst[:, :, 0, :], ALU.subtract))
                link(dve.tensor_copy(dst[:, :, 1, :], rem))
                link(tt(rem, rem, dst[:, :, 1, :], ALU.subtract))
                dve.tensor_copy(dst[:, :, 2, :], rem).then_inc(s["split_ready"], 1)

            def copy_h(n, rows):
                dve.wait_ge(s["h_turned"], n)
                dve.tensor_copy(hT[0:rows, 0:N // 2], ps[0:rows, 0:2, :].rearrange("p b n -> p (b n)"))\
                    .then_inc(s["hT_ready"], 1)

            dve.memset(h[:, :, D:DA], 1.0)
            dve.memset(vp[:, :, :, D:DA], 1.0).then_inc(s["vp_ones"], 1)
            dve.wait_ge(s["x_in"], 16)
            layer_norm()
            copy_h(1, DA)
            dve.wait_ge(s["w_turned"], 1)
            for n in range(3):
                r = dve.tensor_copy(wT[:, n, :, :], ps[:, 4 + n, 0:DC * P].rearrange("p (c n) -> p c n", c=DC)[:, :, 0:DA])
            r.then_inc(s["w_copied"], 1)
            dve.wait_ge(s["wa_done"], 1)
            dve.tensor_copy(wall[:, :], ps[0:DA, 7, 0:NQ]).then_inc(s["wall_ready"], 1)
            dve.wait_ge(s["vw_done"], 1)
            for w in range(2):
                r = dve.tensor_copy(wload[:, 2, :].rearrange("p (c w d) -> p w c d", w=2, d=D)[:, w, :, :],
                                    ps[0:DA, 5 + w, 0:DC * D].rearrange("p (c d) -> p c d", d=D))
            r.then_inc(s["vw_ready"], 1)
            dve.wait_ge(s["s_done"], 1)
            link(dve.tensor_copy(s_nat, ps[:, 4, :].rearrange("p (t q) -> p q t", q=NQ)))
            split3(s_nat, s_rem, split)
            RH = REL * H
            dve.reduce_max(small[:, 0:RH], s_nat[:, RH:2 * RH, :], AX.X).then_inc(s["mx_done"], 1)
            dve.wait_ge(s["mx_read"], 1)
            link(dve.reduce_max(small[0:RH, 20:21], ps[0:RH, 7, 0:P], AX.X))
            ts(small[0:RH, 24:24 + RH], ident[0:RH, 0:RH], small[0:RH, 20:21], None, ALU.mult).then_inc(s["mxrow"], 1)
            dve.wait_ge(s["mxb"], 1)
            link(dve.tensor_copy(small[:, 40:40 + RH], ps[:, 7, P:P + RH]))
            link(tt(m_nat, s_nat[:, 0:RH, :], small[:, 40:40 + RH].unsqueeze(2).to_broadcast([P, RH, NT]), ALU.add))
            link(ts(m_tmp, m_nat, SLOPE, None, ALU.mult))
            link(tt(m_nat, m_nat, m_tmp, ALU.max))
            tt(m_tmp[:, 0:H, :], m_nat[:, 0:H, :], m_nat[:, H:RH, :], ALU.max).then_inc(s["m_ready"], 1)
            dve.wait_ge(s["split_turned"], 1)
            dve.tensor_copy(splitT[:, :], psb[:, 0:2, 0:NQ * PARTS * NT // 2].rearrange("p b n -> p b n"))\
                .then_inc(s["split_copied"], 1)
            dve.wait_ge(s["m_turned"], 1)
            dve.tensor_copy(mT[:, :], ps[:, 7, 0:P]).then_inc(s["m_copied"], 1)
            HB = NT // 2
            for t in range(NT):
                dve.wait_ge(s["adj_turned"], 2 * t + 1)
                dve.tensor_copy(mask[:, 0:HB, t * P:(t + 1) * P],
                                psb[:, 0 + 2 * (t % 2), :].rearrange("p (j n) -> p j n", n=P)).then_inc(s["adj_copied"], 1)

            def select(k, kk):
                jt, i0 = kk % NT, kk // NT % BLOCKS * HALF
                dve.wait_ge(s["scores"], k + 1)
                dve.sem_inc(s["scores_seen"], 1)
                dve.copy_predicated(ps[:, kk % SLOTS, :], mask[:, jt, i0:i0 + HALF], ps[:, 4 + kk % 2, :])\
                    .then_inc(s["selected"], 1)

            def leak(k, kk):
                r = ring[:, kk % RING, :]
                dve.wait_ge(s["relus"], k + 1)
                dve.scalar_tensor_tensor(r, ps[:, kk % SLOTS, :], SLOPE, r, ALU.mult, ALU.add)\
                    .then_inc(s["leaked"], 1)

            def take_sums(k, kk, head):
                blk = kk // NT
                dve.wait_ge(s["products"], k + 1)
                dst = outT[0:DA, bass.ds(head, 1), :] if not isinstance(head, int) else outT[0:DA, head:head + 1, :]
                i0 = blk % BLOCKS * HALF
                dve.tensor_copy(dst.rearrange("p o n -> p (o n)")[:, i0:i0 + HALF], ps[0:DA, 6 + blk % 2, :])\
                    .then_inc(s["acc_free"], 1)

            def tiles(base, n, head0, carried, drain):
                for kk in range(n + (LAG_P + 2 if drain else 0)):
                    if kk < n:
                        select(base + kk, kk)
                    if (kk >= 1 or carried) and kk - 1 < n:
                        leak(base + kk - 1, kk - 1)
                    e = kk - LAG_P - 1
                    if e % NT == NT - 1 and (e >= 0 or carried) and e < n:
                        take_sums(base + e, e, head0 + e // PER_HEAD)

            tiles(0, PAIR, 0, False, False)
            with dve.Fori(1, H // 2) as i:
                tiles(i * PAIR, PAIR, i * 2, True, False)
            tiles(TILES0, 0, H, True, True)

            dve.wait_ge(s["l12_in"], 16 * 5)
            link(tt(x[:, :, :], x[:, :, :], pb[:, :].unsqueeze(1).to_broadcast([P, NT, D]), ALU.add))
            for t in range(NT):
                q = 2 * (t % 2)
                dve.wait_ge(s["out_turned"], t + 1)
                pv = ps[:, q:q + 2, :].rearrange("p b (h d) -> p (b h) d", d=P)
                den = stat[:, 6:7, 0:H].rearrange("p o h -> p (o h)")
                link(dve.reciprocal(den, pv[:, :, D]))
                yv = work[:, 0:H, :]
                dve.tensor_tensor(yv, pv[:, :, 0:D], den.unsqueeze(2).to_broadcast([P, H, D]), ALU.mult)\
                    .then_inc(s["out_taken"], 1)
                dve.wait_ge(s["out_taken"], t + 1)
                link(dve.reduce_sum(y[:, t, :], yv.rearrange("p h d -> p d h"), AX.X))
            link(tt(x[:, :, :], x[:, :, :], y[:, :, :], ALU.add))

            layer_norm(last=False)
            center(h[:, :, 0:D])
            sum_squares(stat[:, 1, :], work[:, :, :], h[:, :, 0:D])
            link(ts(stat[:, 1, :], stat[:, 1, :], NORM_EPS ** 2, None, ALU.max))
            root(stat[:, 2, :], stat[:, 1, :])
            link(ts(stat[:, 2, :], stat[:, 2, :], 1.0 / NORM_EPS, None, ALU.min))
            tt(h[:, :, 0:D], work[:, :, :], bc(stat[:, 2, :]), ALU.mult).then_inc(s["h_ready"], 1)
            copy_h(2, DA)
            dve.wait_ge(s["kq_done"], 1)
            dve.tensor_copy(kqT[0:E, :], ps[0:E, 0:4, :].rearrange("p b n -> p (b n)")).then_inc(s["kq_ready"], 1)
            dve.wait_ge(s["kqn_done"], 1)
            kq = ps[:, 4, 0:NT * 2 * E]
            v = work[:, :, :].rearrange("p a d -> p (a d)")[:, 0:NT * 2 * E]
            link(dve.tensor_copy(v, kq))
            link(tt(v, v, v, ALU.mult))
            link(dve.reduce_sum(stat[:, 0:2, :].rearrange("p a t -> p (a t)"), v.rearrange("p (m e) -> p m e", e=E), AX.X))
            dve.reduce_max(small[:, 0:2], stat[:, 0:2, :].rearrange("p a t -> p (a t)").rearrange("p (t w) -> p w t", w=2),
                           AX.X).then_inc(s["mx_done"], 1)
            dve.wait_ge(s["big_ready"], 1)
            link(dve.reduce_max(small[0:1, 2:4], ps[0:1, 5, 0:2 * P].rearrange("p (w n) -> p w n", w=2), AX.X))
            tt(small[0:1, 4:5], small[0:1, 2:3], small[0:1, 3:4], ALU.mult).then_inc(s["big_b"], 1)
            dve.wait_ge(s["big_s"], 1)
            ts(small[:, 6:7], ps[:, 5, 2 * P:2 * P + 1], -1.0, None, ALU.mult).then_inc(s["big_bias"], 1)
            for k in range(NB * NT):
                jt, b = k // NB, k % NB
                e = eT[:, jt, b * TW:(b + 1) * TW]
                dve.wait_ge(s["e_exp"], k + 1)
                tt(e, e, mask[:, jt, b * TW:(b + 1) * TW], ALU.mult).then_inc(s["e_masked"], 1)

            def take_y(n, halves):
                dve.wait_ge(s["e_products"] if n == 0 else s["y_products"], NB * NT if n == 0 else n)
                rows = DA if n == 0 else P
                dve.tensor_copy(yT[0:rows, 0:TW], ps[0:rows, 4:6, :].rearrange("p b n -> p (b n)")).then_inc(s["y_read"], 1)
                dve.wait_ge(s["y_turned"], n + 1)
                v = ps[:, 0:4, :].rearrange("p b (t d) -> p (b t) d", d=P)
                if n == 0:
                    link(dve.reciprocal(stat[:, 3, :], v[:, :, D]))
                    tt(y[:, :, :], v[:, :, 0:D], bc(stat[:, 3, :]), ALU.mult).then_inc(s["y_ready"], 1)
                else:
                    link(dve.reduce_sum(work[:, :, :], v.rearrange("p t (w d) -> p t d w", w=2), AX.X))
                    tt(y[:, :, :], work[:, :, :], bc(stat[:, 3, :]), ALU.mult).then_inc(s["y_ready"], 1)
                dve.wait_ge(s["y_ready"], n + 1)

            for n in range(4):
                take_y(n, n > 0)
                c = (1.0, 0.5, None, 1.0 / 6.0)[n]
                if c is not None:
                    link(dve.scalar_tensor_tensor(x[:, :, :], y[:, :, :], c, x[:, :, :], ALU.mult, ALU.add))

            layer_norm()
            copy_h(3, DA)
            dve.wait_ge(s["w_turned"], 2)
            dve.tensor_copy(w2T[:, :], ps[0:D, 4, 0:D]).then_inc(s["w_copied"], 1)
            dve.wait_ge(s["wa_done"], 2)
            dve.tensor_copy(w2a[:, :], ps[0:D, 5, 0:2]).then_inc(s["wall_ready"], 1)
            dve.wait_ge(s["wh_done"], 1)
            dve.memset(vst[:, 0, :, D:DA], 1.0)
            dve.tensor_copy(vst[:, 0, :, 0:D], ps[:, 6:8, :].rearrange("p b (t d) -> p (b t) d", d=D))\
                .then_inc(s["wh_ready"], 1)
            dve.wait_ge(s["s2_done"], 1)
            s2v = s_nat[:, 0:4, :]
            dve.memset(s2v[:, 0:1, :], 0.0)
            dve.memset(s2v[:, 2:3, :], MASKED / SLOPE)
            link(dve.tensor_copy(s2v.rearrange("p (r w) t -> p r w t", w=2)[:, :, 1, :],
                                 ps[:, 5, 16:16 + 2 * NT].rearrange("p (t q) -> p q t", q=2)))
            split3(s2v, s_rem[:, 0:4, :], split[:, 0:4, :, :])
            dve.reduce_max(small[:, 0:1], s_nat[:, 3, :], AX.X).then_inc(s["mx_done"], 1)
            dve.wait_ge(s["mx_read"], 2)
            dve.reduce_max(small[0:1, 20:21], ps[0:1, 4, 0:P], AX.X).then_inc(s["mxrow"], 1)
            dve.wait_ge(s["mxb"], 2)
            link(dve.tensor_copy(small[:, 40:41], ps[:, 4, P:P + 1]))
            link(ts(m_nat[:, 0, :], s_nat[:, 1, :], small[:, 40:41], None, ALU.add))
            link(ts(m_tmp[:, 1, :], m_nat[:, 0, :], SLOPE, None, ALU.mult))
            tt(m_tmp[:, 0, :], m_nat[:, 0, :], m_tmp[:, 1, :], ALU.max).then_inc(s["m_ready"], 1)
            dve.wait_ge(s["split_turned"], 2)
            dve.tensor_copy(splitT[0:96, 0:2 * P], psb[0:96, 0, 0:2 * P]).then_inc(s["split_copied"], 1)
            dve.wait_ge(s["m_turned"], 2)
            dve.tensor_copy(mT[0:NT, :], ps[0:NT, 4, 0:P]).then_inc(s["m_copied"], 1)
            tiles(TILES0, PER_HEAD, 0, False, True)
            dve.wait_ge(s["out_turned"], NT + 1)
            v = ps[:, 0:4, :].rearrange("p b (t d) -> p (b t) d", d=P)
            link(dve.reciprocal(stat[:, 3, :], v[:, :, D]))
            link(tt(y[:, :, :], v[:, :, 0:D], bc(stat[:, 3, :]), ALU.mult))
            ts(work[:, :, :], y[:, :, :], 0.0, None, ALU.min).then_inc(s["x2"], 1)
            link(dve.scalar_tensor_tensor(x[:, :, :], y[:, :, :], 0.0, x[:, :, :], ALU.max, ALU.add))
            dve.wait_ge(s["x2"], 2)
            link(dve.scalar_tensor_tensor(x[:, :, :], work[:, :, :], 1.0, x[:, :, :], ALU.subtract, ALU.add))

            layer_norm(last=False)
            link(tt(work[:, :, :], h[:, :, 0:D], h[:, :, 0:D], ALU.mult))
            link(dve.reduce_sum(h[:, :, DA:DX].rearrange("p t o -> p (t o)"), work[:, :, :], AX.X))
            for v in range(2):
                ts(g3[:, v, :, 0:D], h[:, :, 0:D], -2.0, None, ALU.mult)
                dve.memset(g3[:, v, :, D + v:D + v + 1], 1.0)
                r = dve.tensor_copy(g3[:, v, :, D + 1 - v:D + 2 - v], h[:, :, DA:DX])
            r.then_inc(s["h_ready"], 1)
            dve.wait_ge(s["h_turned"], 4)
            dve.tensor_copy(lhs3[0:DX, :], ps[0:DX, 0:4, :].rearrange("p b n -> p (b n)")).then_inc(s["g_read"], 1)
            dve.wait_ge(s["g_turned"], 2)
            dve.tensor_copy(rdis[0:DX, :], ps[0:DX, 0:4, :].rearrange("p b n -> p (b n)")).then_inc(s["g_read"], 1)
            LO, HI = 2.0 * math.log(BALL_EPS), 2.0 * math.log(1.0 - 1e-5)
            n3 = NB * NT
            for k in range(n3 + 3):
                if k < n3:
                    u = k % NW
                    if k >= NW:
                        dve.wait_ge(s["sums"], k - NW + 1)
                    dve.wait_ge(s["den"], k + 1)
                    ts(wA[:, u, :], ps[:, 0:2, :].rearrange("p b n -> p (b n)"), BALL_EPS, None, ALU.max)\
                        .then_inc(s["den_c"], 1)
                    dve.wait_ge(s["dis"], k + 1)
                    ts(wB[:, u, :], ps[:, 2:4, :].rearrange("p b n -> p (b n)"), BALL_EPS, None, ALU.max)\
                        .then_inc(s["dis_c"], 1)
                if 2 <= k < n3 + 2:
                    u = (k - 2) % NW
                    dve.wait_ge(s["un"], k - 1)
                    dve.wait_ge(s["ratioc"], k - 1)
                    dve.scalar_tensor_tensor(wB[:, u, :], wB[:, u, :], -0.5, wA[:, u, :], ALU.mult, ALU.subtract)\
                        .then_inc(s["scl"], 1)
                if 1 <= k <= n3:
                    u = (k - 1) % NW
                    dve.wait_ge(s["ratio"], k)
                    ts(wB[:, u, :], wB[:, u, :], LO, HI, ALU.max, ALU.min).then_inc(s["ratioc"], 1)
                if k >= 3:
                    m = k - 3
                    u, jt, b = m % NW, m // NB, m % NB
                    dve.wait_ge(s["scl_e"], m + 1)
                    dve.wait_ge(s["art"], m + 1)
                    tt(wD[:, u, :], wD[:, u, :], wB[:, u, :], ALU.mult).then_inc(s["wgt"], 1)
                    dve.wait_ge(s["wgt"], m + 1)
                    tt(wD[:, u, :], wD[:, u, :], mask[:, jt, b * TW:(b + 1) * TW], ALU.mult).then_inc(s["wm3"], 1)
            dve.wait_ge(s["sums"], n3)
            dve.tensor_copy(yT[0:DX, 0:TW], ps[0:DX, 4:6, :].rearrange("p b n -> p (b n)")).then_inc(s["y_read"], 1)
            dve.wait_ge(s["z_turned"], 1)
            link(dve.tensor_copy(z[:, :, :], ps[:, 0:4, :].rearrange("p b (t d) -> p (b t) d", d=P)[:, :, 0:DX]))
            hf, n2 = h[:, :, 0:D], h[:, :, DA:DX].rearrange("p t o -> p (t o)")
            S2, S1, S3 = z[:, :, 0:D], z[:, :, D], z[:, :, DA]

            def dot(dst, a, b):
                link(tt(w3[:, :, :], a, b, ALU.mult))
                link(dve.reduce_sum(dst, w3[:, :, :], AX.X))

            beta, c2 = stat[:, 0, :], stat[:, 1, :]
            link(ts(beta, n2, -1.0, 1.0, ALU.mult, ALU.add))
            link(ts(c2, beta, BALL_EPS, None, ALU.max))
            dot(stat[:, 2, :], hf, S2)
            link(dve.scalar_tensor_tensor(stat[:, 2, :], stat[:, 2, :], -2.0, S1, ALU.mult, ALU.add))
            link(tt(stat[:, 2, :], stat[:, 2, :], S3, ALU.add))
            link(tt(work[:, :, :], hf, bc(stat[:, 2, :]), ALU.mult))
            link(tt(y[:, :, :], S2, bc(beta), ALU.mult))
            link(tt(y[:, :, :], y[:, :, :], work[:, :, :], ALU.subtract))
            link(ts(y[:, :, :], y[:, :, :], 0.5, None, ALU.mult))
            dot(stat[:, 3, :], y[:, :, :], y[:, :, :])
            link(ts(stat[:, 3, :], stat[:, 3, :], 1e-30, None, ALU.max))
            root(stat[:, 7, :], stat[:, 3, :])
            link(tt(stat[:, 6, :], stat[:, 6, :], c2, ALU.mult))
            link(ts(stat[:, 6, :], stat[:, 6, :], BALL_EPS, None, ALU.max))
            link(dve.reciprocal(stat[:, 7, :], stat[:, 6, :]))
            link(tt(stat[:, 7, :], stat[:, 7, :], c2, ALU.mult))
            dve.reciprocal(stat[:, 3, :], stat[:, 7, :]).then_inc(s["th_in"], 1)
            dve.wait_ge(s["th"], 1)
            link(tt(stat[:, 5, :], stat[:, 5, :], stat[:, 7, :], ALU.mult))
            link(tt(y[:, :, :], y[:, :, :], bc(stat[:, 5, :]), ALU.mult))
            dot(stat[:, 2, :], hf, y[:, :, :])
            dot(stat[:, 3, :], y[:, :, :], y[:, :, :])
            link(ts(stat[:, 2, :], stat[:, 2, :], 2.0, 1.0, ALU.mult, ALU.add))
            link(tt(stat[:, 4, :], stat[:, 2, :], stat[:, 3, :], ALU.add))
            link(tt(stat[:, 3, :], stat[:, 3, :], n2, ALU.mult))
            link(tt(stat[:, 2, :], stat[:, 2, :], stat[:, 3, :], ALU.add))
            link(ts(stat[:, 2, :], stat[:, 2, :], BALL_EPS, None, ALU.max))
            link(dve.reciprocal(stat[:, 2, :], stat[:, 2, :]))
            link(tt(stat[:, 4, :], stat[:, 4, :], stat[:, 2, :], ALU.mult))
            link(tt(stat[:, 2, :], beta, stat[:, 2, :], ALU.mult))
            link(tt(work[:, :, :], hf, bc(stat[:, 4, :]), ALU.mult))
            link(tt(y[:, :, :], y[:, :, :], bc(stat[:, 2, :]), ALU.mult))
            link(tt(x[:, :, :], x[:, :, :], work[:, :, :], ALU.add))
            tt(x[:, :, :], x[:, :, :], y[:, :, :], ALU.add).then_inc(s["x_ready"], 4)

        @block.scalar
        def _(act):
            def root(n):
                act.wait_ge(s["ln_var"], n)
                act.activation(stat[:, 5, :], stat[:, 4, :], ACT.Sqrt).then_inc(s["ln_std"], 1)

            def copy_h(n, rows):
                act.wait_ge(s["h_turned"], n)
                act.activation(hT[0:rows, N // 2:N], ps[0:rows, 2:4, :].rearrange("p b n -> p (b n)"), ACT.Copy)\
                    .then_inc(s["hT_ready"], 1)

            root(1)
            copy_h(1, DA)
            for t in range(NT):
                act.wait_ge(s["vp_done"], t + 1)
                act.activation(vp[:, :, t, 0:D], ps[:, 4 + t % 2, :].rearrange("p (h d) -> p h d", h=H), ACT.Copy)\
                    .then_inc(s["vp_read"], 1)
            HB = NT // 2
            for t in range(NT):
                act.wait_ge(s["adj_turned"], 2 * t + 2)
                act.activation(mask[:, HB:NT, t * P:(t + 1) * P],
                               psb[:, 1 + 2 * (t % 2), :].rearrange("p (j n) -> p j n", n=P), ACT.Copy)\
                    .then_inc(s["adj_copied_b"], 1)

            def tiles(base, n, carried, drain):
                for kk in range(n + (LAG_W if drain else 0)):
                    if kk < n:
                        k = base + kk
                        act.wait_ge(s["selected"], k + 1)
                        if kk >= RING or carried:
                            act.wait_ge(s["products"], k - RING + 1)
                        act.activation(ring[:, kk % RING, :], ps[:, kk % SLOTS, :], ACT.Relu, scale=1.0 - SLOPE)\
                            .then_inc(s["relus"], 1)
                    m = kk - LAG_W
                    if m >= 0 or carried:
                        act.wait_ge(s["shifted"], base + m + 1)
                        act.activation(ring[:, m % RING, :], ring[:, m % RING, :], ACT.Exp).then_inc(s["weights"], 1)

            tiles(0, PAIR, False, False)
            with act.Fori(1, H // 2) as i:
                tiles(i * PAIR, PAIR, True, False)
            tiles(TILES0, 0, True, True)
            root(2)
            root(3)
            copy_h(2, DA)
            act.wait_ge(s["kq_t"], 1)
            act.activation(qT[0:E, :], ps[0:E, 4:8, :].rearrange("p b n -> p (b n)"), ACT.Copy).then_inc(s["kq_ready"], 1)
            act.wait_ge(s["big_b"], 1)
            act.activation(small[0:1, 5:6], small[0:1, 4:5], ACT.Sqrt, scale=1.0 / E).then_inc(s["big_b"], 1)
            act.wait_ge(s["big_bias"], 1)
            for k in range(NB * NT):
                jt, b, p2 = k // NB, k % NB, k % 2
                act.wait_ge(s["e_scores"], k + 1)
                act.activation(eT[:, jt, b * TW:(b + 1) * TW], ps[:, 2 * p2:2 * p2 + 2, :].rearrange("p b n -> p (b n)"),
                               ACT.Exp, bias=small[:, 6:7], scale=1.0 / math.sqrt(E)).then_inc(s["e_exp"], 1)
            for n in range(4):
                act.wait_ge(s["e_products"] if n == 0 else s["y_products"], NB * NT if n == 0 else n)
                rows = DA if n == 0 else P
                act.activation(yT[0:rows, TW:N], ps[0:rows, 6:8, :].rearrange("p b n -> p (b n)"), ACT.Copy)\
                    .then_inc(s["y_read"], 1)
            root(4)
            copy_h(3, DA)
            tiles(TILES0, PER_HEAD, False, True)
            act.wait_ge(s["x2"], 1)
            act.activation(work[:, :, :], work[:, :, :], ACT.Exp).then_inc(s["x2"], 1)
            root(5)
            act.preload_act_table_set("natural_log_exp_and_others")
            act.wait_ge(s["g_turned"], 1)
            act.activation(rden[0:DX, :], ps[0:DX, 4:8, :].rearrange("p b n -> p (b n)"), ACT.Copy)\
                .then_inc(s["g_read"], 1)
            n3 = NB * NT
            for k in range(n3 + 2):
                if k < n3:
                    u = k % NW
                    act.wait_ge(s["den_c"], k + 1)
                    act.activation(wA[:, u, :], wA[:, u, :], ACT.Ln).then_inc(s["logs"], 1)
                    act.wait_ge(s["dis_c"], k + 1)
                    act.activation(wB[:, u, :], wB[:, u, :], ACT.Ln).then_inc(s["logs"], 1)
                if 1 <= k <= n3:
                    u = (k - 1) % NW
                    act.wait_ge(s["ratioc"], k)
                    act.activation(wC[:, u, :], wB[:, u, :], ACT.Exp, scale=0.5).then_inc(s["un"], 1)
                    act.wait_ge(s["un"], k)
                    act.activation(wD[:, u, :], wC[:, u, :], ACT.Ln, bias=1.0).then_inc(s["l1"], 1)
                    act.wait_ge(s["l1"], k)
                    act.activation(wC[:, u, :], wC[:, u, :], ACT.Ln, bias=1.0, scale=-1.0).then_inc(s["l2"], 1)
                if k >= 2:
                    u = (k - 2) % NW
                    act.wait_ge(s["scl"], k - 1)
                    act.activation(wB[:, u, :], wB[:, u, :], ACT.Exp).then_inc(s["scl_e"], 1)
            act.wait_ge(s["sums"], n3)
            act.activation(yT[0:DX, TW:N], ps[0:DX, 6:8, :].rearrange("p b n -> p (b n)"), ACT.Copy).then_inc(s["y_read"], 1)
            root(6)
            act.wait_ge(s["th_in"], 1)
            act.activation(stat[:, 5, :], stat[:, 3, :], ACT.Tanh).then_inc(s["th"], 1)

        @block.tensor
        def _(pe):
            def turn(dst_bank, src, rows, sem, n=NT):
                for t in range(n):
                    r = pe.transpose(ps[0:rows, dst_bank + t // 4, t % 4 * P:(t % 4 + 1) * P], src(t), ident[:, :])
                r.then_inc(sem, 1)

            pe.wait_ge(s["ids2"], 2)
            pe.wait_ge(s["w_in"], 16 * 6)
            for n in range(3):
                for c in range(DC):
                    r = pe.transpose(ps[:, 4 + n, c * P:c * P + DA], wload[:, n, c * P:(c + 1) * P], ident[0:DA, 0:DA])
            r.then_inc(s["w_turned"], 1)
            pe.wait_ge(s["h_ready"], 1)
            turn(0, lambda t: h[:, t, 0:DA], DA, s["h_turned"])
            pe.wait_ge(s["w_copied"], 1)
            pe.wait_ge(s["a_in"], 16 * 3)
            for n in range(2):
                for r in range(REL):
                    for c in range(DC):
                        o = (n * REL + r) * H
                        m = pe.matmul(ps[0:DA, 7, o:o + H], wT[:, n, c, :], arel[:, r, n * DC + c, :],
                                      start=(c == 0), stop=(c == DC - 1))
            m.then_inc(s["wa_done"], 1)
            for hh in range(H):
                c, p0 = hh // 2, hh % 2 * D
                m = pe.matmul(ps[0:DA, 5 + hh % 2, c * D:(c + 1) * D], wT[p0:p0 + D, 2, c, :], pw[p0:p0 + D, c, :],
                              start=True, stop=True)
            m.then_inc(s["vw_done"], 1)
            pe.wait_ge(s["hT_ready"], 2)
            pe.wait_ge(s["wall_ready"], 1)
            for t in range(NT):
                m = pe.matmul(ps[:, 4, t * NQ:(t + 1) * NQ], hT[0:DA, t * P:(t + 1) * P], wall[:, :], start=True, stop=True)
            m.then_inc(s["s_done"], 1)
            RH = REL * H
            pe.wait_ge(s["mx_done"], 1)
            pe.transpose(ps[0:RH, 7, 0:P], small[:, 0:RH], ident[:, :]).then_inc(s["mx_read"], 1)
            pe.wait_ge(s["mxrow"], 1)
            pe.wait_ge(s["ones"], 3)
            pe.matmul(ps[:, 7, P:P + RH], onesf[0:RH, :], small[0:RH, 24:24 + RH], start=True, stop=True)\
                .then_inc(s["mxb"], 1)
            pe.wait_ge(s["split_ready"], 1)
            flat = split.rearrange("p q c t -> p (q c t)")
            nblk = NQ * PARTS * NT // P
            for c in range(nblk):
                o = c % (nblk // 2) * P
                r = pe.transpose(psb[:, c // (nblk // 2), o:o + P], flat[:, c * P:(c + 1) * P], identb[:, :])
            r.then_inc(s["split_turned"], 1)
            pe.wait_ge(s["m_ready"], 1)
            pe.transpose(ps[:, 7, 0:P], m_tmp[:, 0:H, :].rearrange("p h t -> p (h t)"), ident[:, :]).then_inc(s["m_turned"], 1)
            pe.wait_ge(s["vw_ready"], 1)
            for t in range(NT):
                if t >= 2:
                    pe.wait_ge(s["vp_read"], t - 1)
                pe.matmul(ps[:, 4 + t % 2, :], hT[0:DA, t * P:(t + 1) * P], wload[:, 2, :], start=True, stop=True)\
                    .then_inc(s["vp_done"], 1)
            HB = NT // 2
            pe.wait_ge(s["split_copied"], 1)
            for t in range(NT):
                pe.wait_ge(adj_in[t % NADJ], 16 * (t // NADJ + 1))
                if t >= 2:
                    pe.wait_ge(s["adj_copied"], t - 1)
                    pe.wait_ge(s["adj_copied_b"], t - 1)
                for w in range(2):
                    for j in range(HB):
                        r = pe.transpose(psb[:, w + 2 * (t % 2), j * P:(j + 1) * P],
                                         adjb[:, t % NADJ, (w * HB + j) * P:(w * HB + j + 1) * P], identb[:, :])
                    r.then_inc(s["adj_turned"], 1)

            def score(k, kk, carried):
                jt, i0, b = kk % NT, kk // NT % BLOCKS * HALF, kk // PER_HEAD
                if kk >= SLOTS or carried:
                    pe.wait_ge(s["leaked"], k - SLOTS + 1)
                if kk >= 2 or carried:
                    pe.wait_ge(s["selected"], k - 1)
                for r, bank in ((0, kk % SLOTS), (1, 4 + kk % 2)):
                    p0 = 32 * (2 * r + kk % 2)
                    m = pe.matmul(ps[:, bank, :], op_l[p0:p0 + 2 * PARTS, b, jt * P:(jt + 1) * P],
                                  op_r[p0:p0 + 2 * PARTS, b, i0:i0 + HALF], start=True, stop=True)
                m.then_inc(s["scores"], 1)

            def aggregate(k, kk, acc, carried):
                jt, blk, b = kk % NT, kk // NT, kk // PER_HEAD
                pe.wait_ge(s["weights"], k + 1)
                if jt == 0 and (blk >= 2 or carried):
                    pe.wait_ge(s["acc_free"], acc + blk - 1)
                pe.matmul(ps[0:DA, 6 + blk % 2, :], vst[:, b, jt, :], ring[:, kk % RING, :],
                          start=(jt == 0), stop=(jt == NT - 1)).then_inc(s["products"], 1)

            def tiles(base, n, step, acc, carried, drain):
                for kk in range(n + (LAG_P if drain else 0)):
                    if kk < n:
                        if kk % PER_HEAD == 0 and step is not None:
                            pe.wait_ge(staged[kk // PER_HEAD], (step + 1) * STAGED)
                        score(base + kk, kk, carried)
                    mm = kk - LAG_P
                    if mm >= 0:
                        aggregate(base + mm, mm, acc, carried)
                    elif carried:
                        aggregate(base + mm, mm + PAIR, acc - 2 * BLOCKS, carried)

            pe.wait_ge(s["adj_copied"], NT)
            pe.wait_ge(s["adj_copied_b"], NT)
            pe.wait_ge(s["m_copied"], 1)
            tiles(0, PAIR, 0, 0, False, False)
            with pe.Fori(1, H // 2) as i:
                tiles(i * PAIR, PAIR, i, i * (2 * BLOCKS), True, False)
            tiles(TILES0, 0, None, H * BLOCKS, True, True)
            pe.wait_ge(s["acc_free"], H * BLOCKS)
            for t in range(NT):
                if t >= 2:
                    pe.wait_ge(s["out_taken"], t - 1)
                for hh in range(H):
                    r = pe.transpose(ps[:, 2 * (t % 2) + hh // 4, hh % 4 * P:hh % 4 * P + DA],
                                     outT[0:DA, hh, t * P:(t + 1) * P], ident[0:DA, 0:DA])
                r.then_inc(s["out_turned"], 1)
            pe.wait_ge(s["h_ready"], 2)
            turn(0, lambda t: h[:, t, 0:DA], DA, s["h_turned"])
            pe.wait_ge(s["hT_ready"], 4)
            for w, sem in ((1, s["kq_t"]), (0, s["kq_done"])):
                for c in range(4):
                    m = pe.matmul(ps[0:E, 4 * w + c, :], wkq[:, w * E:(w + 1) * E], hT[0:D, c * HALF:(c + 1) * HALF],
                                  start=True, stop=True)
                m.then_inc(sem, 1)
            pe.wait_ge(s["kq_ready"], 2)
            for t in range(NT):
                m = pe.matmul(ps[:, 4, t * 2 * E:(t + 1) * 2 * E], hT[0:D, t * P:(t + 1) * P], wkq[:, :], start=True, stop=True)
            m.then_inc(s["kqn_done"], 1)
            pe.wait_ge(s["mx_done"], 2)
            for w in range(2):
                r = pe.transpose(ps[0:1, 5, w * P:(w + 1) * P], small[:, w:w + 1], ident[:, :])
            r.then_inc(s["big_ready"], 1)
            pe.wait_ge(s["big_b"], 2)
            pe.matmul(ps[:, 5, 2 * P:2 * P + 1], onesf[0:1, :], small[0:1, 5:6], start=True, stop=True).then_inc(s["big_s"], 1)
            pe.wait_ge(s["big_bias"], 1)
            for k in range(NB * NT + 3):
                if k < NB * NT:
                    jt, b, p2 = k // NB, k % NB, k % 2
                    if k >= 2:
                        pe.wait_ge(s["e_exp"], k - 1)
                    for w in range(2):
                        m = pe.matmul(ps[:, 2 * p2 + w, :], qT[0:E, jt * P:(jt + 1) * P],
                                      kqT[0:E, b * TW + w * HALF:b * TW + (w + 1) * HALF], start=True, stop=True)
                    m.then_inc(s["e_scores"], 1)
                if k >= 3:
                    mm = k - 3
                    jt, b = mm // NB, mm % NB
                    pe.wait_ge(s["e_masked"], mm + 1)
                    for w in range(2):
                        m = pe.matmul(ps[0:DA, 4 + 2 * b + w, :], h[:, jt, 0:DA], eT[:, jt, b * TW + w * HALF:b * TW + (w + 1) * HALF],
                                      start=(jt == 0), stop=(jt == NT - 1))
                    m.then_inc(s["e_products"], 1)

            def turn_y(n, rows):
                pe.wait_ge(s["y_read"], 2 * n + 2)
                for t in range(NT):
                    r = pe.transpose(ps[:, t // 4, t % 4 * P:t % 4 * P + rows], yT[0:rows, t * P:(t + 1) * P],
                                     ident[0:rows, 0:rows])
                r.then_inc(s["y_turned"], 1)

            turn_y(0, DA)
            for n in range(1, 4):
                pe.wait_ge(s["y_ready"], n)
                for jp in range(NT // 2):
                    for c in range(4):
                        for w in range(2):
                            jt = 2 * jp + w
                            m = pe.matmul(ps[w * D:(w + 1) * D, 4 + c, :], y[:, jt, :], eT[:, jt, c * HALF:(c + 1) * HALF],
                                          start=(jp == 0), stop=(jp == NT // 2 - 1))
                m.then_inc(s["y_products"], 1)
                turn_y(n, P)
            pe.wait_ge(s["h_ready"], 3)
            turn(0, lambda t: h[:, t, 0:DA], DA, s["h_turned"])
            pe.transpose(ps[0:D, 4, 0:D], w2[:, :], ident[0:D, 0:D]).then_inc(s["w_turned"], 1)
            pe.wait_ge(s["w_copied"], 2)
            pe.matmul(ps[0:D, 5, 0:2], w2T[:, :], a12[:, :], start=True, stop=True).then_inc(s["wa_done"], 1)
            pe.wait_ge(s["hT_ready"], 6)
            for t in range(NT):
                m = pe.matmul(ps[:, 6 + t // 8, t % 8 * D:(t % 8 + 1) * D], hT[0:D, t * P:(t + 1) * P], w2[:, :],
                              start=True, stop=True)
            m.then_inc(s["wh_done"], 1)
            pe.wait_ge(s["wall_ready"], 2)
            for t in range(NT):
                m = pe.matmul(ps[:, 5, 16 + 2 * t:18 + 2 * t], hT[0:D, t * P:(t + 1) * P], w2a[:, :], start=True, stop=True)
            m.then_inc(s["s2_done"], 1)
            pe.wait_ge(s["mx_done"], 3)
            pe.transpose(ps[0:1, 4, 0:P], small[:, 0:1], ident[:, :]).then_inc(s["mx_read"], 1)
            pe.wait_ge(s["mxrow"], 2)
            pe.matmul(ps[:, 4, P:P + 1], onesf[0:1, :], small[0:1, 20:21], start=True, stop=True).then_inc(s["mxb"], 1)
            pe.wait_ge(s["split_ready"], 2)
            flat2 = split[:, 0:4, :, :].rearrange("p q c t -> p (q c t)")
            for c in range(2):
                r = pe.transpose(psb[0:96, 0, c * P:(c + 1) * P], flat2[:, c * 96:(c + 1) * 96], identb[:, :])
            r.then_inc(s["split_turned"], 1)
            pe.wait_ge(s["m_ready"], 2)
            pe.transpose(ps[0:NT, 4, 0:P], m_tmp[:, 0, :], ident[:, :]).then_inc(s["m_turned"], 1)
            pe.wait_ge(s["m_copied"], 2)
            pe.wait_ge(s["ops2"], 16 * 9)
            pe.wait_ge(s["wh_ready"], 1)
            tiles(TILES0, PER_HEAD, None, H * BLOCKS, False, True)
            pe.wait_ge(s["acc_free"], (H + 1) * BLOCKS)
            for t in range(NT):
                r = pe.transpose(ps[:, t // 4, t % 4 * P:t % 4 * P + DA], outT[0:DA, 0, t * P:(t + 1) * P],
                                 ident[0:DA, 0:DA])
            r.then_inc(s["out_turned"], 1)
            pe.wait_ge(s["h_ready"], 4)
            turn(0, lambda t: h[:, t, :], DX, s["h_turned"])
            turn(4, lambda t: g3[:, 0, t, :], DX, s["g_turned"])
            pe.wait_ge(s["g_read"], 2)
            turn(0, lambda t: g3[:, 1, t, :], DX, s["g_turned"])
            pe.wait_ge(s["g_read"], 3)
            n3 = NB * NT
            for k in range(n3 + 4):
                if k < n3:
                    jt, b = k // NB, k % NB
                    for bank, rhs, sem, read in ((0, rden, s["den"], s["den_c"]), (2, rdis, s["dis"], s["dis_c"])):
                        if k >= 1:
                            pe.wait_ge(read, k)
                        for w in range(2):
                            m = pe.matmul(ps[:, bank + w, :], lhs3[0:DX, jt * P:(jt + 1) * P],
                                          rhs[0:DX, b * TW + w * HALF:b * TW + (w + 1) * HALF], start=True, stop=True)
                        m.then_inc(sem, 1)
                if k >= 4:
                    mm = k - 4
                    jt, b, u = mm // NB, mm % NB, mm % NW
                    pe.wait_ge(s["wm3"], mm + 1)
                    for w in range(2):
                        m = pe.matmul(ps[0:DX, 4 + 2 * b + w, :], h[:, jt, :], wD[:, u, w * HALF:(w + 1) * HALF],
                                      start=(jt == 0), stop=(jt == NT - 1))
                    m.then_inc(s["sums"], 1)
            pe.wait_ge(s["y_read"], 10)
            for t in range(NT):
                r = pe.transpose(ps[:, t // 4, t % 4 * P:t % 4 * P + DX], yT[0:DX, t * P:(t + 1) * P], ident[0:DX, 0:DX])
            r.then_inc(s["z_turned"], 1)


_INS = ['x', 'adj', 'L0_gnn_Qw', 'L0_gnn_Qb', 'L0_gnn_Kw', 'L0_gnn_Kb', 'L0_gnn_Vw', 'L0_gnn_Vb', 'L0_gnn_a',
        'L0_gnn_Pw', 'L0_gnn_Pb', 'L1_gnn_w_k', 'L1_gnn_w_q', 'L2_gnn_W', 'L2_gnn_a']


def kernel(**inputs):
    import numpy as _np
    import concourse.bacc as _bacc
    from concourse import mybir as _mybir
    from concourse.bass_utils import run_bass_kernel_spmd as _run

    nc = _bacc.Bacc("TRN2", target_bir_lowering=False, num_devices=1)
    arrays, args = {}, []
    for name in _INS:
        a = _np.ascontiguousarray(inputs[name])
        arrays[f"in_{name}_dram"] = a
        args.append(nc.dram_tensor(f"in_{name}_dram", a.shape, _mybir.dt.from_np(a.dtype), kind="ExternalInput").ap())
    out = nc.dram_tensor("out_dram", inputs["x"].shape, _mybir.dt.float32, kind="ExternalOutput").ap()
    gnn_stack(nc, *args, out)
    r = _run(nc, [arrays], core_ids=[0])
    return r.results[0]["out_dram"]
```

```python
import math
from contextlib import ExitStack

import concourse.bass as bass
from concourse import mybir

P = 128
ALU = mybir.AluOpType
ACT = mybir.ActivationFunctionType
AX = mybir.AxisListType
F32 = mybir.dt.float32
BF16 = mybir.dt.bfloat16
U8 = mybir.dt.uint8
I32 = mybir.dt.int32

LN_EPS = 1e-5
NORM_EPS = 1e-12
BALL_EPS = 1e-7
SLOPE = 0.2
MASKED = -9e15


def gnn_stack(nc, x_d, adj_d, Qw, Qb, Kw, Kb, Vw, Vb, a_rel, Pw, Pb, w_k, w_q, W2, a2, out_d):
    N, D = x_d.shape
    NT = N // P
    H = a_rel.shape[2]
    DM = Qw.shape[1]
    DC = DM // P
    REL = 2
    E = w_k.shape[1]
    HALF = 512
    TW = 2 * HALF
    NB = N // TW
    PARTS = 3
    DA = D + 1
    DX = D + 2
    RING = 16
    BLOCKS = N // HALF
    PER_HEAD = BLOCKS * NT
    PAIR = 2 * PER_HEAD
    SLOTS = 4
    NQ = 2 * REL * H

    ctx = ExitStack()
    with ctx:
        def sb(name, shape, dt=F32):
            return ctx.enter_context(nc.sbuf_tensor(name, shape, dt))

        big = sb("big", [P, NT * N])
        mask = sb("mask", [P, NT, N], U8)
        x = sb("x_nat", [P, NT, D])
        h = sb("h_nat", [P, NT, DX])
        hT = sb("hT", [P, N])
        work = sb("work", [P, NT, D])
        ident = sb("ident", [P, P])
        identb = sb("identb", [P, P], BF16)
        onesf = sb("onesf", [P, P])
        stat = sb("stat", [P, 8, NT])
        small = sb("small", [P, 64])
        op_l = sb("op_l", [P, 2, N], BF16)
        op_r = sb("op_r", [P, 2, N], BF16)
        wall = sb("wall", [DA, NQ])
        arel = sb("arel", [P, REL, 2 * DC, H])
        pb = sb("pb", [P, D])
        wkq = sb("wkq", [D, 2 * E])
        w2 = sb("w2", [D, D])
        w2T = sb("w2T", [D, D])
        a12 = sb("a12", [D, 2])
        w2a = sb("w2a", [D, 2])

        at = [0]

        def part(n, shape=None):
            v = big[:, at[0]:at[0] + n]
            at[0] += n
            return v
        outT = part(H * N).rearrange("p (h n) -> p h n", h=H)
        ring = part(RING * HALF).rearrange("p (r n) -> p r n", r=RING)
        mrow = part(2 * N).rearrange("p (b n) -> p b n", b=2)
        vst = part(2 * NT * DA).rearrange("p (b t d) -> p b t d", b=2, t=NT)
        used0 = at[0]
        per_head = ring.rearrange("p r n -> p (r n)").rearrange("p (t h d) -> p t h d", t=NT, h=H)
        assert used0 <= NT * N
        at[0] = 0
        vp = part(NT * H * DA).rearrange("p (h t d) -> p h t d", h=H, t=NT)
        s_nat = part(NQ * NT).rearrange("p (q t) -> p q t", q=NQ)
        s_rem = part(NQ * NT).rearrange("p (q t) -> p q t", q=NQ)
        split = part(NQ * PARTS * NT // 2).bitcast(BF16).rearrange("p (q c t) -> p q c t", q=NQ, c=PARTS)
        splitT = part(NQ * PARTS * NT // 2).bitcast(BF16)
        m_nat = part(REL * H * NT).rearrange("p (q t) -> p q t", q=REL * H)
        m_tmp = part(REL * H * NT).rearrange("p (q t) -> p q t", q=REL * H)
        mT = part(P)
        wload = part(3 * DM).rearrange("p (w n) -> p w n", w=3)[0:DA, :, :]
        wT = part(3 * DC * DA).rearrange("p (w c n) -> p w c n", w=3, c=DC)
        pw = part(DC * D).rearrange("p (c n) -> p c n", c=DC)
        assert at[0] <= H * N
        adjb = ring.rearrange("p r n -> p (r n)").bitcast(BF16).rearrange("p (r n) -> p r n", n=N)
        NADJ = RING * HALF * 2 // N
        eT = big[:, :].rearrange("p (t n) -> p t n", t=NT)
        Q_PART, K_PART = (0, 1, 0, 2, 0, 1), (0, 0, 1, 0, 2, 1)
        ER = len(Q_PART) * E
        qT, kT = op_l[:, 0, :], op_r[:, 0, :]
        y = sb("y_nat", [P, NT, D])
        wflat = work[:, :, :].rearrange("p t d -> p (t d)")
        KQ = NT * 2 * E
        kq, kq_rem = wflat[:, 0:KQ], wflat[:, KQ:2 * KQ]
        kq_part = wflat[:, 2 * KQ:2 * KQ + 3 * KQ // 2].bitcast(BF16).rearrange("p (c n) -> p c n", c=PARTS)
        kq_slot = y[:, :, :].rearrange("p t d -> p (t d)")[:, 0:NT * ER].bitcast(BF16)\
            .rearrange("p (w t e) -> p w t e", w=2, t=NT)
        yT = hT
        at[0] = 0
        lhs3 = part(N)
        rden = part(N)
        rdis = part(N)
        NW = 8
        wA = part(NW * HALF).rearrange("p (r n) -> p r n", r=NW)
        wB = part(NW * HALF).rearrange("p (r n) -> p r n", r=NW)
        wC = part(NW * HALF).rearrange("p (r n) -> p r n", r=NW)
        wD = part(NW * HALF).rearrange("p (r n) -> p r n", r=NW)
        assert at[0] <= NT * N
        at[0] = 3 * N
        g3 = part(2 * NT * DX).rearrange("p (v t d) -> p v t d", v=2, t=NT)
        at[0] = 3 * N
        z = part(NT * DX).rearrange("p (t d) -> p t d", t=NT)
        w3 = part(NT * D).rearrange("p (t d) -> p t d", t=NT)

        ps = ctx.enter_context(nc.psum_tensor("ps", [P, 8, HALF], F32))
        psb = ps[:, :, :].rearrange("p b n -> p (b n)").bitcast(BF16).rearrange("p (b n) -> p b n", b=8)

        split_d = nc.dram_tensor("split_scratch", [NQ, PARTS, N], BF16, kind="Internal").ap()
        split2_d = nc.dram_tensor("split2_scratch", [4, PARTS, N], BF16, kind="Internal").ap()
        m_d = nc.dram_tensor("max_scratch", [H, N], F32, kind="Internal").ap()
        m2_d = nc.dram_tensor("max2_scratch", [1, N], F32, kind="Internal").ap()
        vp_d = nc.dram_tensor("value_scratch", [H, P, NT * DA], F32, kind="Internal").ap()

        names = """x_in w_in a_in l12_in rows_in staged0 staged1 valued0 valued1 rows_out split_out m_out vp_out
            out_done ids ids2 ones dve_chain act_chain pool_chain
            adj_turned adj_copied adj_copied_b ln_var ln_std h_ready h_turned hT_ready
            w_turned w_copied wa_done wall_ready s_done s_read mx_done mx_read mxrow mxb m_ready split_ready
            split_turned split_copied m_turned m_copied vw_done vw_ready vp_done vp_read vp_ones
            scores scores_seen selected relus leaked shifted weights products acc_free
            out_turned out_taken half_sums quarter_sums head_sums x_ready norm_sq norm_rt kq_done kq_ready kqn_done kqn_read big_ready
            kq_t big_b big_s big_bias e_scores e_exp e_masked e_products y_read y_turned y_ready y_products
            ops2 wh_done wh_ready s2_done x2 den dis den_c dis_c logs ratio ratioc un l1 l2 art scl scl_e wgt wm3 turned3 mirrored sums
            z_read z_turned z_ready v_sq v_rt th_in th sec_done g_ready g_turned g_read""".split()
        s = {n: ctx.enter_context(nc.semaphore(n)) for n in names}
        adj_in = [ctx.enter_context(nc.semaphore(f"adj_in{n}")) for n in range(NADJ)]
        staged = [s["staged0"], s["staged1"]]
        valued = [s["valued0"], s["valued1"]]
        STAGED = 16 * (4 * 2 + 1)

        def bc(v, n=D):
            return v.unsqueeze(2).to_broadcast([P, NT, n])

        def row_group(op, b, g, r0, n):
            return op[32 * g + r0:32 * g + r0 + n, b, :]

        block = ctx.enter_context(nc.Block())

        @block.sync
        def _(sp):
            def stage(b, sq, s2q, m_row):
                sp.dma_start(mrow[:, b, :], m_row.to_broadcast([P, N])).then_inc(staged[b], 16)
                for g in range(4):
                    sp.dma_start(row_group(op_l, b, g, 0, PARTS), s2q(g // 2)).then_inc(staged[b], 16)
                    sp.dma_start(row_group(op_r, b, g, PARTS, PARTS), sq(g // 2)).then_inc(staged[b], 16)

            def stage_values(b, v_src):
                sp.dma_start(vst[:, b, :, :].rearrange("p t d -> p (t d)"), v_src).then_inc(valued[b], 16)

            sp.dma_start(x[:, :, :], x_d.rearrange("(t p) d -> p t d", p=P)).then_inc(s["x_in"], 16)
            for n, (w, b) in enumerate(((Qw, Qb), (Kw, Kb), (Vw, Vb))):
                sp.dma_start(wload[0:D, n, :], w).then_inc(s["w_in"], 16)
                sp.dma_start(wload[D:DA, n, :], b.rearrange("(o n) -> o n", o=1)).then_inc(s["w_in"], 16)
            for r in range(REL):
                sp.dma_start(arel[:, r, :, :], a_rel[r, :, :].rearrange("(c p) h -> p c h", p=P))\
                    .then_inc(s["a_in"], 16)
            sp.dma_start(pw[:, :, :], Pw.rearrange("(c p) n -> p c n", p=P)).then_inc(s["a_in"], 16)
            sp.dma_start(pb[:, :], Pb.rearrange("(o n) -> o n", o=1).to_broadcast([P, D])).then_inc(s["l12_in"], 16)
            sp.dma_start(wkq[:, 0:E], w_k).then_inc(s["l12_in"], 16)
            sp.dma_start(wkq[:, E:2 * E], w_q).then_inc(s["l12_in"], 16)
            sp.dma_start(w2[:, :], W2).then_inc(s["l12_in"], 16)
            with nc.allow_non_contiguous_dma(reason="128 values"):
                sp.dma_start(a12[:, :], a2.rearrange("(c p) o -> p (c o)", c=2)).then_inc(s["l12_in"], 16)
            sp.wait_ge(s["split_copied"], 1)
            for c in range(NQ * PARTS * NT // P):
                sp.dma_start(split_d.rearrange("q c (t n) -> (q c t) n", n=P)[c * P:(c + 1) * P, :],
                             splitT[:, c * P:(c + 1) * P]).then_inc(s["rows_out"], 16)
            sp.wait_ge(s["m_copied"], 1)
            sp.dma_start(m_d.rearrange("h (t n) -> (h t) n", n=P), mT[:, :]).then_inc(s["m_out"], 16)
            sp.wait_ge(s["rows_out"], 16 * (NQ * PARTS * NT // P))
            sp.wait_ge(s["m_out"], 16)
            sp.wait_ge(s["ones"], 3)

            def stage_head(b, head):
                stage(b, lambda r: split_d[bass.ds(head + r * H, 1), :, :].rearrange("o c n -> (o c) n"),
                      lambda r: split_d[bass.ds(head + (REL + r) * H, 1), :, :].rearrange("o c n -> (o c) n"),
                      m_d[bass.ds(head, 1), :])

            def values(head):
                return vp[:, head, :, :].rearrange("p t d -> p (t d)")

            stage_head(0, 0)
            stage_head(1, 1)
            sp.wait_ge(s["vp_ones"], 1)
            sp.wait_ge(s["vp_read"], NT)
            stage_values(0, values(0))
            stage_values(1, values(1))
            for head in range(2, H):
                sp.dma_start(vp_d[head, :, :], values(head)).then_inc(s["vp_out"], 16)
            sp.wait_ge(s["vp_out"], 16 * (H - 2))
            with sp.Fori(1, H // 2) as i:
                for b in range(2):
                    sp.wait_ge(s["acc_free"], i * (2 * BLOCKS) + (b - 1) * BLOCKS)
                    stage_head(b, i * 2 + b)
                    stage_values(b, vp_d[bass.ds(i * 2 + b, 1), :, :].rearrange("o p n -> (o p) n"))
            sp.wait_ge(s["split_copied"], 2)
            sp.dma_start(split2_d.rearrange("q c (t n) -> (q c t) n", n=P)[0:96, :], splitT[0:96, 0:P])\
                .then_inc(s["rows_out"], 16)
            sp.dma_start(split2_d.rearrange("q c (t n) -> (q c t) n", n=P)[96:192, :], splitT[0:96, P:2 * P])\
                .then_inc(s["rows_out"], 16)
            sp.wait_ge(s["m_copied"], 2)
            sp.dma_start(m2_d.rearrange("h (t n) -> (h t) n", n=P), mT[0:NT, :]).then_inc(s["m_out"], 16)
            sp.wait_ge(s["m_out"], 32)
            sp.dma_start(mrow[:, 0, :], m2_d[0:1, :].to_broadcast([P, N])).then_inc(s["ops2"], 16)
            sp.wait_ge(s["rows_out"], 16 * (NQ * PARTS * NT // P + 2))
            sp.wait_ge(s["ones"], 5)
            for g in range(4):
                sp.dma_start(row_group(op_l, 0, g, 0, PARTS), split2_d[2 + g // 2, :, :]).then_inc(s["ops2"], 16)
                sp.dma_start(row_group(op_r, 0, g, PARTS, PARTS), split2_d[g // 2, :, :]).then_inc(s["ops2"], 16)
            sp.wait_ge(s["x_ready"], 4)
            sp.dma_start(out_d.rearrange("(t p) d -> p t d", p=P), x[:, :, :]).then_inc(s["out_done"], 16)
            sp.wait_ge(s["out_done"], 16)

        TILES0 = H * PER_HEAD
        ADJ_FIRST = 3
        PROLOGUE = ([("adj", t) for t in range(ADJ_FIRST)] + [("hT", 0)]
                    + [("value", 0), ("value", 1), ("adj", 3), ("value", 2), ("value", 3), ("adj", 4), ("value", 4),
                       ("adj", 5), ("max", 0), ("value", 5), ("max", 1), ("value", 6), ("max", 2), ("value", 7)]
                    + [x for t in range(6, NT) for x in ([("value", t + 2)] if t + 2 < NT else []) + [("adj", t)]])
        TILES3 = [(jt, c) for jt in range(NT) for c in range(jt // (HALF // P), BLOCKS)[::-1 if jt else 1]]
        n3 = len(TILES3)
        MIRROR = [c > jt // (HALF // P) for jt, c in TILES3]
        MIRRORS = [sum(MIRROR[:k + 1]) for k in range(n3)]
        LAG_T, LAG_M, LAG_S = 4, 5, 6
        LAG_W, LAG_P = 5, 7

        @block.gpsimd
        def _(pool):
            for t in range(NADJ):
                pool.dma_start(adjb[:, t, :], adj_d[t * P:(t + 1) * P, :]).then_inc(adj_in[t], 16)
            pool.memset(ident[:, :], 0.0).then_inc(s["ids"], 1)
            pool.memset(identb[:, :], 0.0).then_inc(s["ids"], 1)
            pool.wait_ge(s["ids"], 2)
            for m in (ident, identb):
                pool.affine_select(out=m[:, :], in_=m[:, :], compare_op=ALU.not_equal, fill=1.0, base=0,
                                   pattern=[[-1, P]], channel_multiplier=1).then_inc(s["ids2"], 1)
            pool.memset(op_l[:, :, :], 1.0).then_inc(s["ones"], 1)
            pool.memset(op_r[:, :, :], 1.0).then_inc(s["ones"], 1)
            pool.memset(onesf[:, :], 1.0).then_inc(s["ones"], 1)
            for t in range(NADJ, NT):
                pool.wait_ge(s["adj_turned"], 2 * (t - NADJ + 1))
                pool.dma_start(adjb[:, t % NADJ, :], adj_d[t * P:(t + 1) * P, :])\
                    .then_inc(adj_in[t % NADJ], 16)

            def shift(k, kk, b):
                i0 = kk // NT % BLOCKS * HALF
                pool.wait_ge(s["leaked"], k + 1)
                pool.tensor_tensor(ring[:, kk % RING, :], ring[:, kk % RING, :], mrow[:, b, i0:i0 + HALF],
                                   ALU.subtract).then_inc(s["shifted"], 1)

            with pool.Fori(0, H // 2) as i:
                for kk in range(PAIR):
                    shift(i * PAIR + kk, kk, kk // PER_HEAD)
            for t in range(NT):
                v = per_head[:, t, :, :]
                pool.wait_ge(s["out_taken"], t + 1)
                pool.tensor_tensor(v[:, 0:4, :], v[:, 0:4, :], v[:, 4:8, :], ALU.add).then_inc(s["half_sums"], 1)
                pool.wait_ge(s["half_sums"], t + 1)
                pool.tensor_tensor(v[:, 0:2, :], v[:, 0:2, :], v[:, 2:4, :], ALU.add).then_inc(s["quarter_sums"], 1)
                pool.wait_ge(s["quarter_sums"], t + 1)
                pool.tensor_tensor(y[:, t, :], v[:, 0, :], v[:, 1, :], ALU.add).then_inc(s["head_sums"], 1)
            pool.wait_ge(s["big_bias"], 1)
            pool.wait_ge(s["e_products"], NB * NT)
            pool.memset(op_l[:, :, :], 1.0).then_inc(s["ones"], 1)
            pool.memset(op_r[:, :, :], 1.0).then_inc(s["ones"], 1)
            for kk in range(PER_HEAD):
                shift(TILES0 + kk, kk, 0)
            for k in range(n3 + 1):
                if k < n3:
                    u = k % NW
                    pool.wait_ge(s["logs"], 2 * k + 2)
                    pool.tensor_tensor(wB[:, u, :], wB[:, u, :], wA[:, u, :], ALU.subtract).then_inc(s["ratio"], 1)
                if k >= 1:
                    u = (k - 1) % NW
                    pool.wait_ge(s["l2"], k)
                    pool.tensor_tensor(wD[:, u, :], wD[:, u, :], wC[:, u, :], ALU.subtract).then_inc(s["art"], 1)

        @block.vector
        def _(dve):
            chain = [0]

            def link(ins):
                chain[0] += 1
                ins.then_inc(s["dve_chain"], 1)
                dve.wait_ge(s["dve_chain"], chain[0])

            def ts(out, in_, s1, s2, o0, o1=None):
                if o1 is None:
                    return dve.tensor_scalar(out, in_, s1, None, o0)
                return dve.tensor_scalar(out, in_, s1, s2, o0, o1)

            def tt(out, a, b, op):
                return dve.tensor_tensor(out, a, b, op)

            roots = [0]

            def root(dst, var):
                ts(stat[:, 4, :], var, 1.0, None, ALU.mult).then_inc(s["ln_var"], 1)
                roots[0] += 1
                dve.wait_ge(s["ln_std"], roots[0])
                link(dve.reciprocal(stat[:, 6, :], stat[:, 5, :]))
                link(tt(stat[:, 6, :], stat[:, 6, :], var, ALU.mult))
                link(tt(stat[:, 6, :], stat[:, 6, :], stat[:, 5, :], ALU.add))
                link(ts(stat[:, 6, :], stat[:, 6, :], 0.5, None, ALU.mult))
                link(dve.reciprocal(dst, stat[:, 6, :]))

            def center(v):
                link(dve.reduce_sum(stat[:, 0, :], v, AX.X))
                link(ts(stat[:, 0, :], stat[:, 0, :], 1.0 / D, None, ALU.mult))
                link(tt(work[:, :, :], v, bc(stat[:, 0, :]), ALU.subtract))

            def sum_squares(dst, v, scratch):
                link(tt(scratch, v, v, ALU.mult))
                link(dve.reduce_sum(dst, scratch, AX.X))

            def layer_norm(last=True):
                center(x[:, :, :])
                sum_squares(stat[:, 1, :], work[:, :, :], h[:, :, 0:D])
                link(ts(stat[:, 1, :], stat[:, 1, :], 1.0 / D, LN_EPS, ALU.mult, ALU.add))
                root(stat[:, 2, :], stat[:, 1, :])
                link(tt(work[:, :, :], work[:, :, :], bc(stat[:, 2, :]), ALU.mult))
                r = ts(h[:, :, 0:D], work[:, :, :], 0.0, None, ALU.max)
                if last:
                    r.then_inc(s["h_ready"], 1)
                else:
                    link(r)

            def split3(src, rem, dst):
                link(dve.tensor_copy(dst[:, :, 0, :], src))
                link(tt(rem, src, dst[:, :, 0, :], ALU.subtract))
                link(dve.tensor_copy(dst[:, :, 1, :], rem))
                link(tt(rem, rem, dst[:, :, 1, :], ALU.subtract))
                dve.tensor_copy(dst[:, :, 2, :], rem).then_inc(s["split_ready"], 1)

            def copy_h(n, rows):
                dve.wait_ge(s["h_turned"], n)
                dve.tensor_copy(hT[0:rows, 0:N // 2], ps[0:rows, 0:2, :].rearrange("p b n -> p (b n)"))\
                    .then_inc(s["hT_ready"], 1)

            dve.memset(h[:, :, D:DA], 1.0)
            dve.memset(vp[:, :, :, D:DA], 1.0).then_inc(s["vp_ones"], 1)
            dve.wait_ge(s["x_in"], 16)
            layer_norm()
            copy_h(1, DA)
            dve.wait_ge(s["w_turned"], 1)
            for n in range(3):
                r = dve.tensor_copy(wT[:, n, :, :], ps[:, 4 + n, 0:DC * P].rearrange("p (c n) -> p c n", c=DC)[:, :, 0:DA])
            r.then_inc(s["w_copied"], 1)
            dve.wait_ge(s["wa_done"], 1)
            dve.tensor_copy(wall[:, :], ps[0:DA, 7, 0:NQ]).then_inc(s["wall_ready"], 1)
            dve.wait_ge(s["vw_done"], 1)
            for w in range(2):
                r = dve.tensor_copy(wload[:, 2, :].rearrange("p (c w d) -> p w c d", w=2, d=D)[:, w, :, :],
                                    ps[0:DA, 5 + w, 0:DC * D].rearrange("p (c d) -> p c d", d=D))
            r.then_inc(s["vw_ready"], 1)
            dve.wait_ge(s["s_done"], 1)
            link(dve.tensor_copy(s_nat, ps[:, 4, :].rearrange("p (t q) -> p q t", q=NQ)))
            split3(s_nat, s_rem, split)
            RH = REL * H
            dve.reduce_max(small[:, 0:RH], s_nat[:, RH:2 * RH, :], AX.X).then_inc(s["mx_done"], 1)
            dve.wait_ge(s["mx_read"], 1)
            link(dve.reduce_max(small[0:RH, 20:21], ps[0:RH, 7, 0:P], AX.X))
            ts(small[0:RH, 24:24 + RH], ident[0:RH, 0:RH], small[0:RH, 20:21], None, ALU.mult).then_inc(s["mxrow"], 1)
            dve.wait_ge(s["mxb"], 1)
            link(dve.tensor_copy(small[:, 40:40 + RH], ps[:, 7, P:P + RH]))
            link(tt(m_nat, s_nat[:, 0:RH, :], small[:, 40:40 + RH].unsqueeze(2).to_broadcast([P, RH, NT]), ALU.add))
            link(ts(m_tmp, m_nat, SLOPE, None, ALU.mult))
            link(tt(m_nat, m_nat, m_tmp, ALU.max))
            tt(m_tmp[:, 0:H, :], m_nat[:, 0:H, :], m_nat[:, H:RH, :], ALU.max).then_inc(s["m_ready"], 1)
            dve.wait_ge(s["split_turned"], 1)
            dve.tensor_copy(splitT[:, 0:2 * HALF], psb[:, 4, :])
            dve.wait_ge(s["m_turned"], 1)
            dve.tensor_copy(splitT[:, 2 * HALF:], psb[:, 7, HALF:]).then_inc(s["split_copied"], 1)
            dve.tensor_copy(mT[:, :], ps[:, 7, 0:P]).then_inc(s["m_copied"], 1)
            HB = NT // 2
            for t in range(NT // 2, NT):
                dve.wait_ge(s["adj_turned"], 2 * t + 1)
                dve.tensor_copy(mask[:, 0:HB, t * P:(t + 1) * P],
                                psb[:, 2 * (t % 2), :].rearrange("p (j n) -> p j n", n=P)).then_inc(s["adj_copied"], 1)

            def select(k, kk):
                jt, i0 = kk % NT, kk // NT % BLOCKS * HALF
                dve.wait_ge(s["scores"], k + 1)
                dve.sem_inc(s["scores_seen"], 1)
                dve.copy_predicated(ps[:, kk % SLOTS, :], mask[:, jt, i0:i0 + HALF], ps[:, 4 + kk % 2, :])\
                    .then_inc(s["selected"], 1)

            def leak(k, kk):
                r = ring[:, kk % RING, :]
                dve.wait_ge(s["relus"], k + 1)
                dve.scalar_tensor_tensor(r, ps[:, kk % SLOTS, :], SLOPE, r, ALU.mult, ALU.add)\
                    .then_inc(s["leaked"], 1)

            def take_sums(k, kk, head):
                blk = kk // NT
                dve.wait_ge(s["products"], k + 1)
                dst = outT[0:DA, bass.ds(head, 1), :] if not isinstance(head, int) else outT[0:DA, head:head + 1, :]
                i0 = blk % BLOCKS * HALF
                dve.tensor_copy(dst.rearrange("p o n -> p (o n)")[:, i0:i0 + HALF], ps[0:DA, 6 + blk % 2, :])\
                    .then_inc(s["acc_free"], 1)

            def tiles(base, n, head0, carried, drain):
                for kk in range(n + (LAG_P + 2 if drain else 0)):
                    if kk < n:
                        select(base + kk, kk)
                    if (kk >= 1 or carried) and kk - 1 < n:
                        leak(base + kk - 1, kk - 1)
                    e = kk - LAG_P - 1
                    if e % NT == NT - 1 and (e >= 0 or carried) and e < n:
                        if e == NT - 1 and not carried and n == PAIR:
                            dve.wait_ge(s["vp_out"], 16 * (H - 2))
                            for b in range(2):
                                dve.wait_ge(valued[b], 16)
                        take_sums(base + e, e, head0 + e // PER_HEAD)

            tiles(0, PAIR, 0, False, False)
            with dve.Fori(1, H // 2) as i:
                tiles(i * PAIR, PAIR, i * 2, True, False)
            tiles(TILES0, 0, H, True, True)

            dve.wait_ge(s["l12_in"], 16 * 5)
            link(tt(x[:, :, :], x[:, :, :], pb[:, :].unsqueeze(1).to_broadcast([P, NT, D]), ALU.add))
            for t in range(NT):
                q = 2 * (t % 2)
                dve.wait_ge(s["out_turned"], t + 1)
                pv = ps[:, q:q + 2, :].rearrange("p b (h d) -> p (b h) d", d=P)
                if t >= 2:
                    dve.wait_ge(s["out_taken"], t - 1)
                den = stat[:, 6:7, t % 2 * H:(t % 2 + 1) * H].rearrange("p o h -> p (o h)")
                link(dve.reciprocal(den, pv[:, :, D]))
                dve.tensor_tensor(per_head[:, t, :, :], pv[:, :, 0:D], den.unsqueeze(2).to_broadcast([P, H, D]), ALU.mult)\
                    .then_inc(s["out_taken"], 1)
            dve.wait_ge(s["head_sums"], NT)
            link(tt(x[:, :, :], x[:, :, :], y[:, :, :], ALU.add))

            layer_norm(last=False)
            center(h[:, :, 0:D])
            sum_squares(stat[:, 1, :], work[:, :, :], h[:, :, 0:D])
            link(ts(stat[:, 1, :], stat[:, 1, :], NORM_EPS ** 2, None, ALU.max))
            root(stat[:, 2, :], stat[:, 1, :])
            link(ts(stat[:, 2, :], stat[:, 2, :], 1.0 / NORM_EPS, None, ALU.min))
            tt(h[:, :, 0:D], work[:, :, :], bc(stat[:, 2, :]), ALU.mult).then_inc(s["h_ready"], 1)
            copy_h(2, DA)
            dve.wait_ge(s["kqn_done"], 1)
            link(dve.tensor_copy(kq, ps[:, 4, 0:KQ]))
            link(dve.tensor_copy(kq_part[:, 0, :], kq))
            link(tt(kq_rem, kq, kq_part[:, 0, :], ALU.subtract))
            link(dve.tensor_copy(kq_part[:, 1, :], kq_rem))
            link(tt(kq_rem, kq_rem, kq_part[:, 1, :], ALU.subtract))
            link(dve.tensor_copy(kq_part[:, 2, :], kq_rem))
            for w, parts in ((1, Q_PART), (0, K_PART)):
                for n, c in enumerate(parts):
                    r = dve.tensor_copy(kq_slot[:, w, :, n * E:(n + 1) * E],
                                        kq_part[:, c, :].rearrange("p (t e) -> p t e", t=NT)[:, :, w * E:(w + 1) * E])
            r.then_inc(s["kq_done"], 1)
            link(tt(kq_rem, kq, kq, ALU.mult))
            link(dve.reduce_sum(stat[:, 0:2, :].rearrange("p a t -> p (a t)"), kq_rem.rearrange("p (m e) -> p m e", e=E), AX.X))
            dve.reduce_max(small[:, 0:2], stat[:, 0:2, :].rearrange("p a t -> p (a t)").rearrange("p (t w) -> p w t", w=2),
                           AX.X).then_inc(s["mx_done"], 1)
            dve.wait_ge(s["kq_t"], 1)
            dve.tensor_copy(qT[0:ER, :].rearrange("p (b n) -> p b n", b=2), psb[0:ER, 0:2, :]).then_inc(s["kq_ready"], 1)
            dve.wait_ge(s["big_ready"], 1)
            link(dve.reduce_max(small[0:1, 2:4], ps[0:1, 5, 0:2 * P].rearrange("p (w n) -> p w n", w=2), AX.X))
            tt(small[0:1, 4:5], small[0:1, 2:3], small[0:1, 3:4], ALU.mult).then_inc(s["big_b"], 1)
            dve.wait_ge(s["big_s"], 1)
            ts(small[:, 6:7], ps[:, 5, 2 * P:2 * P + 1], -1.0, None, ALU.mult).then_inc(s["big_bias"], 1)
            for k in range(NB * NT):
                jt, b = k // NB, k % NB
                e = eT[:, jt, b * TW:(b + 1) * TW]
                dve.wait_ge(s["e_exp"], k + 1)
                tt(e, e, mask[:, jt, b * TW:(b + 1) * TW], ALU.mult).then_inc(s["e_masked"], 1)

            def take_y(n, halves):
                dve.wait_ge(s["e_products"] if n == 0 else s["y_products"], NB * NT if n == 0 else n)
                rows = DA if n == 0 else P
                dve.tensor_copy(yT[0:rows, 0:TW], ps[0:rows, 4:6, :].rearrange("p b n -> p (b n)")).then_inc(s["y_read"], 1)
                dve.wait_ge(s["y_turned"], n + 1)
                v = ps[:, 0:4, :].rearrange("p b (t d) -> p (b t) d", d=P)
                if n == 0:
                    link(dve.reciprocal(stat[:, 3, :], v[:, :, D]))
                    tt(y[:, :, :], v[:, :, 0:D], bc(stat[:, 3, :]), ALU.mult).then_inc(s["y_ready"], 1)
                else:
                    link(dve.reduce_sum(work[:, :, :], v.rearrange("p t (w d) -> p t d w", w=2), AX.X))
                    tt(y[:, :, :], work[:, :, :], bc(stat[:, 3, :]), ALU.mult).then_inc(s["y_ready"], 1)
                dve.wait_ge(s["y_ready"], n + 1)

            for n in range(4):
                take_y(n, n > 0)
                c = (1.0, 0.5, None, 1.0 / 6.0)[n]
                if c is not None:
                    link(dve.scalar_tensor_tensor(x[:, :, :], y[:, :, :], c, x[:, :, :], ALU.mult, ALU.add))

            dve.wait_ge(s["w_turned"], 2)
            dve.tensor_copy(w2T[:, :], ps[0:D, 4, 0:D]).then_inc(s["w_copied"], 1)
            dve.wait_ge(s["wa_done"], 2)
            dve.tensor_copy(w2a[:, :], ps[0:D, 5, 0:2]).then_inc(s["wall_ready"], 1)
            layer_norm()
            copy_h(3, DA)
            dve.wait_ge(s["s2_done"], 1)
            s2v = s_nat[:, 0:4, :]
            dve.memset(s2v[:, 0:1, :], 0.0)
            dve.memset(s2v[:, 2:3, :], MASKED / SLOPE)
            link(dve.tensor_copy(s2v.rearrange("p (r w) t -> p r w t", w=2)[:, :, 1, :],
                                 ps[:, 5, 16:16 + 2 * NT].rearrange("p (t q) -> p q t", q=2)))
            split3(s2v, s_rem[:, 0:4, :], split[:, 0:4, :, :])
            dve.reduce_max(small[:, 0:1], s_nat[:, 3, :], AX.X).then_inc(s["mx_done"], 1)
            dve.wait_ge(s["mx_read"], 2)
            dve.reduce_max(small[0:1, 20:21], ps[0:1, 4, 0:P], AX.X).then_inc(s["mxrow"], 1)
            dve.wait_ge(s["mxb"], 2)
            link(dve.tensor_copy(small[:, 40:41], ps[:, 4, P:P + 1]))
            link(ts(m_nat[:, 0, :], s_nat[:, 1, :], small[:, 40:41], None, ALU.add))
            link(ts(m_tmp[:, 1, :], m_nat[:, 0, :], SLOPE, None, ALU.mult))
            tt(m_tmp[:, 0, :], m_nat[:, 0, :], m_tmp[:, 1, :], ALU.max).then_inc(s["m_ready"], 1)
            dve.wait_ge(s["split_turned"], 2)
            dve.tensor_copy(splitT[0:96, 0:2 * P], psb[0:96, 0, 0:2 * P]).then_inc(s["split_copied"], 1)
            dve.wait_ge(s["m_turned"], 2)
            dve.tensor_copy(mT[0:NT, :], ps[0:NT, 4, 0:P]).then_inc(s["m_copied"], 1)
            dve.memset(vst[:, 0, :, D:DA], 1.0)
            dve.wait_ge(s["wh_done"], 1)
            dve.tensor_copy(vst[:, 0, :, 0:D], ps[:, 6:8, :].rearrange("p b (t d) -> p (b t) d", d=D))\
                .then_inc(s["wh_ready"], 1)
            tiles(TILES0, PER_HEAD, 0, False, True)
            dve.wait_ge(s["out_turned"], NT + 1)
            v = ps[:, 0:4, :].rearrange("p b (t d) -> p (b t) d", d=P)
            link(dve.reciprocal(stat[:, 3, :], v[:, :, D]))
            link(tt(y[:, :, :], v[:, :, 0:D], bc(stat[:, 3, :]), ALU.mult))
            ts(work[:, :, :], y[:, :, :], 0.0, None, ALU.min).then_inc(s["x2"], 1)
            link(dve.scalar_tensor_tensor(x[:, :, :], y[:, :, :], 0.0, x[:, :, :], ALU.max, ALU.add))
            dve.wait_ge(s["x2"], 2)
            link(dve.scalar_tensor_tensor(x[:, :, :], work[:, :, :], 1.0, x[:, :, :], ALU.subtract, ALU.add))

            layer_norm(last=False)
            link(tt(work[:, :, :], h[:, :, 0:D], h[:, :, 0:D], ALU.mult))
            link(dve.reduce_sum(h[:, :, DA:DX].rearrange("p t o -> p (t o)"), work[:, :, :], AX.X))
            for v in range(2):
                ts(g3[:, v, :, 0:D], h[:, :, 0:D], -2.0, None, ALU.mult)
                dve.memset(g3[:, v, :, D + v:D + v + 1], 1.0)
                r = dve.tensor_copy(g3[:, v, :, D + 1 - v:D + 2 - v], h[:, :, DA:DX])
            r.then_inc(s["h_ready"], 1)
            dve.wait_ge(s["h_turned"], 4)
            dve.tensor_copy(lhs3[0:DX, :], ps[0:DX, 0:4, :].rearrange("p b n -> p (b n)")).then_inc(s["g_read"], 1)
            dve.wait_ge(s["g_turned"], 2)
            dve.tensor_copy(rdis[0:DX, :], ps[0:DX, 0:4, :].rearrange("p b n -> p (b n)")).then_inc(s["g_read"], 1)
            LO, HI = 2.0 * math.log(BALL_EPS), 2.0 * math.log(1.0 - 1e-5)
            for k in range(n3 + LAG_M):
                if k >= LAG_M and MIRROR[k - LAG_M]:
                    m = k - LAG_M
                    u, (jt, c) = m % NW, TILES3[m]
                    j0 = c * (HALF // P)
                    dve.wait_ge(s["turned3"], MIRRORS[m])
                    tt(wA[:, u, :].rearrange("p (j n) -> p j n", n=P),
                       ps[:, 2 + MIRRORS[m] % 2, :].rearrange("p (j n) -> p j n", n=P),
                       mask[:, j0:j0 + HALF // P, jt * P:(jt + 1) * P], ALU.mult).then_inc(s["mirrored"], 1)
                if k < n3:
                    u = k % NW
                    if k >= NW:
                        dve.wait_ge(s["sums"], k - NW + 1)
                    dve.wait_ge(s["den"], k + 1)
                    ts(wA[:, u, :], ps[:, 0, :], BALL_EPS, None, ALU.max).then_inc(s["den_c"], 1)
                    dve.wait_ge(s["dis"], k + 1)
                    ts(wB[:, u, :], ps[:, 1, :], BALL_EPS, None, ALU.max)\
                        .then_inc(s["dis_c"], 1)
                if 2 <= k < n3 + 2:
                    u = (k - 2) % NW
                    dve.wait_ge(s["un"], k - 1)
                    dve.wait_ge(s["ratioc"], k - 1)
                    dve.scalar_tensor_tensor(wB[:, u, :], wB[:, u, :], -0.5, wA[:, u, :], ALU.mult, ALU.subtract)\
                        .then_inc(s["scl"], 1)
                if 1 <= k <= n3:
                    u = (k - 1) % NW
                    dve.wait_ge(s["ratio"], k)
                    ts(wB[:, u, :], wB[:, u, :], LO, HI, ALU.max, ALU.min).then_inc(s["ratioc"], 1)
                if 3 <= k < n3 + 3:
                    m = k - 3
                    u, (jt, c) = m % NW, TILES3[m]
                    dve.wait_ge(s["scl_e"], m + 1)
                    dve.wait_ge(s["art"], m + 1)
                    tt(wD[:, u, :], wD[:, u, :], wB[:, u, :], ALU.mult).then_inc(s["wgt"], 1)
                    dve.wait_ge(s["wgt"], m + 1)
                    tt(wC[:, u, :], wD[:, u, :], mask[:, jt, c * HALF:(c + 1) * HALF], ALU.mult).then_inc(s["wm3"], 1)
            dve.wait_ge(s["sums"], n3)
            dve.tensor_copy(yT[0:DX, 0:TW], ps[0:DX, 4:6, :].rearrange("p b n -> p (b n)")).then_inc(s["y_read"], 1)
            dve.wait_ge(s["z_turned"], 1)
            link(dve.tensor_copy(z[:, :, :], ps[:, 0:4, :].rearrange("p b (t d) -> p (b t) d", d=P)[:, :, 0:DX]))
            hf, n2 = h[:, :, 0:D], h[:, :, DA:DX].rearrange("p t o -> p (t o)")
            S2, S1, S3 = z[:, :, 0:D], z[:, :, D], z[:, :, DA]

            def dot(dst, a, b):
                link(tt(w3[:, :, :], a, b, ALU.mult))
                link(dve.reduce_sum(dst, w3[:, :, :], AX.X))

            beta, c2 = stat[:, 0, :], stat[:, 1, :]
            link(ts(beta, n2, -1.0, 1.0, ALU.mult, ALU.add))
            link(ts(c2, beta, BALL_EPS, None, ALU.max))
            dot(stat[:, 2, :], hf, S2)
            link(dve.scalar_tensor_tensor(stat[:, 2, :], stat[:, 2, :], -2.0, S1, ALU.mult, ALU.add))
            link(tt(stat[:, 2, :], stat[:, 2, :], S3, ALU.add))
            link(tt(work[:, :, :], hf, bc(stat[:, 2, :]), ALU.mult))
            link(tt(y[:, :, :], S2, bc(beta), ALU.mult))
            link(tt(y[:, :, :], y[:, :, :], work[:, :, :], ALU.subtract))
            link(ts(y[:, :, :], y[:, :, :], 0.5, None, ALU.mult))
            dot(stat[:, 3, :], y[:, :, :], y[:, :, :])
            link(ts(stat[:, 3, :], stat[:, 3, :], 1e-30, None, ALU.max))
            root(stat[:, 7, :], stat[:, 3, :])
            link(tt(stat[:, 6, :], stat[:, 6, :], c2, ALU.mult))
            link(ts(stat[:, 6, :], stat[:, 6, :], BALL_EPS, None, ALU.max))
            link(dve.reciprocal(stat[:, 7, :], stat[:, 6, :]))
            link(tt(stat[:, 7, :], stat[:, 7, :], c2, ALU.mult))
            dve.reciprocal(stat[:, 3, :], stat[:, 7, :]).then_inc(s["th_in"], 1)
            dve.wait_ge(s["th"], 1)
            link(tt(stat[:, 5, :], stat[:, 5, :], stat[:, 7, :], ALU.mult))
            link(tt(y[:, :, :], y[:, :, :], bc(stat[:, 5, :]), ALU.mult))
            dot(stat[:, 2, :], hf, y[:, :, :])
            dot(stat[:, 3, :], y[:, :, :], y[:, :, :])
            link(ts(stat[:, 2, :], stat[:, 2, :], 2.0, 1.0, ALU.mult, ALU.add))
            link(tt(stat[:, 4, :], stat[:, 2, :], stat[:, 3, :], ALU.add))
            link(tt(stat[:, 3, :], stat[:, 3, :], n2, ALU.mult))
            link(tt(stat[:, 2, :], stat[:, 2, :], stat[:, 3, :], ALU.add))
            link(ts(stat[:, 2, :], stat[:, 2, :], BALL_EPS, None, ALU.max))
            link(dve.reciprocal(stat[:, 2, :], stat[:, 2, :]))
            link(tt(stat[:, 4, :], stat[:, 4, :], stat[:, 2, :], ALU.mult))
            link(tt(stat[:, 2, :], beta, stat[:, 2, :], ALU.mult))
            link(tt(work[:, :, :], hf, bc(stat[:, 4, :]), ALU.mult))
            link(tt(y[:, :, :], y[:, :, :], bc(stat[:, 2, :]), ALU.mult))
            link(tt(x[:, :, :], x[:, :, :], work[:, :, :], ALU.add))
            tt(x[:, :, :], x[:, :, :], y[:, :, :], ALU.add).then_inc(s["x_ready"], 4)

        @block.scalar
        def _(act):
            def root(n):
                act.wait_ge(s["ln_var"], n)
                act.activation(stat[:, 5, :], stat[:, 4, :], ACT.Sqrt).then_inc(s["ln_std"], 1)

            def copy_h(n, rows):
                act.wait_ge(s["h_turned"], n)
                act.activation(hT[0:rows, N // 2:N], ps[0:rows, 2:4, :].rearrange("p b n -> p (b n)"), ACT.Copy)\
                    .then_inc(s["hT_ready"], 1)

            HB = NT // 2

            def adj_out(t, w):
                act.wait_ge(s["adj_turned"], 2 * t + w + 1)
                act.activation(mask[:, w * HB:(w + 1) * HB, t * P:(t + 1) * P],
                               psb[:, (2 * (t % 2) if t >= ADJ_FIRST else 2) + w, :].rearrange("p (j n) -> p j n", n=P),
                               ACT.Copy).then_inc(s["adj_copied_b"], 1)

            def value_out(t):
                act.wait_ge(s["vp_done"], t + 1)
                act.activation(vp[:, :, t, 0:D], ps[:, 5 + t % 2, :].rearrange("p (h d) -> p h d", h=H), ACT.Copy)\
                    .then_inc(s["vp_read"], 1)

            for kind, t in PROLOGUE:
                if kind == "adj":
                    for w in range(2):
                        if w or t < NT // 2:
                            adj_out(t, w)
                elif kind == "value":
                    value_out(t)
                elif kind == "hT":
                    root(1)
                    copy_h(1, DA)

            def tiles(base, n, carried, drain):
                for kk in range(n + (LAG_W if drain else 0)):
                    if kk < n:
                        k = base + kk
                        act.wait_ge(s["selected"], k + 1)
                        if kk >= RING or carried:
                            act.wait_ge(s["products"], k - RING + 1)
                        act.activation(ring[:, kk % RING, :], ps[:, kk % SLOTS, :], ACT.Relu, scale=1.0 - SLOPE)\
                            .then_inc(s["relus"], 1)
                    m = kk - LAG_W
                    if m >= 0 or carried:
                        act.wait_ge(s["shifted"], base + m + 1)
                        act.activation(ring[:, m % RING, :], ring[:, m % RING, :], ACT.Exp).then_inc(s["weights"], 1)

            tiles(0, PAIR, False, False)
            with act.Fori(1, H // 2) as i:
                tiles(i * PAIR, PAIR, True, False)
            tiles(TILES0, 0, True, True)
            root(2)
            root(3)
            copy_h(2, DA)
            act.wait_ge(s["kq_t"], 2)
            act.activation(kT[0:ER, :].rearrange("p (b n) -> p b n", b=2), psb[0:ER, 2:4, :], ACT.Copy)\
                .then_inc(s["kq_ready"], 1)
            act.wait_ge(s["big_b"], 1)
            act.activation(small[0:1, 5:6], small[0:1, 4:5], ACT.Sqrt, scale=1.0 / E).then_inc(s["big_b"], 1)
            act.wait_ge(s["big_bias"], 1)
            for k in range(NB * NT):
                jt, b, p2 = k // NB, k % NB, k % 2
                act.wait_ge(s["e_scores"], k + 1)
                act.activation(eT[:, jt, b * TW:(b + 1) * TW], ps[:, 2 * p2:2 * p2 + 2, :].rearrange("p b n -> p (b n)"),
                               ACT.Exp, bias=small[:, 6:7], scale=1.0 / math.sqrt(E)).then_inc(s["e_exp"], 1)
            for n in range(4):
                act.wait_ge(s["e_products"] if n == 0 else s["y_products"], NB * NT if n == 0 else n)
                rows = DA if n == 0 else P
                act.activation(yT[0:rows, TW:N], ps[0:rows, 6:8, :].rearrange("p b n -> p (b n)"), ACT.Copy)\
                    .then_inc(s["y_read"], 1)
            root(4)
            copy_h(3, DA)
            tiles(TILES0, PER_HEAD, False, True)
            act.wait_ge(s["x2"], 1)
            act.activation(work[:, :, :], work[:, :, :], ACT.Exp).then_inc(s["x2"], 1)
            root(5)
            act.preload_act_table_set("natural_log_exp_and_others")
            act.wait_ge(s["g_turned"], 1)
            act.activation(rden[0:DX, :], ps[0:DX, 4:8, :].rearrange("p b n -> p (b n)"), ACT.Copy)\
                .then_inc(s["g_read"], 1)
            for k in range(n3 + 2):
                if k < n3:
                    u = k % NW
                    act.wait_ge(s["den_c"], k + 1)
                    act.activation(wA[:, u, :], wA[:, u, :], ACT.Ln).then_inc(s["logs"], 1)
                    act.wait_ge(s["dis_c"], k + 1)
                    act.activation(wB[:, u, :], wB[:, u, :], ACT.Ln).then_inc(s["logs"], 1)
                if 1 <= k <= n3:
                    u = (k - 1) % NW
                    act.wait_ge(s["ratioc"], k)
                    act.activation(wC[:, u, :], wB[:, u, :], ACT.Exp, scale=0.5).then_inc(s["un"], 1)
                    act.wait_ge(s["un"], k)
                    act.activation(wD[:, u, :], wC[:, u, :], ACT.Ln, bias=1.0).then_inc(s["l1"], 1)
                    act.wait_ge(s["l1"], k)
                    act.activation(wC[:, u, :], wC[:, u, :], ACT.Ln, bias=1.0, scale=-1.0).then_inc(s["l2"], 1)
                if k >= 2:
                    u = (k - 2) % NW
                    act.wait_ge(s["scl"], k - 1)
                    act.activation(wB[:, u, :], wB[:, u, :], ACT.Exp).then_inc(s["scl_e"], 1)
            act.wait_ge(s["sums"], n3)
            act.activation(yT[0:DX, TW:N], ps[0:DX, 6:8, :].rearrange("p b n -> p (b n)"), ACT.Copy).then_inc(s["y_read"], 1)
            root(6)
            act.wait_ge(s["th_in"], 1)
            act.activation(stat[:, 5, :], stat[:, 3, :], ACT.Tanh).then_inc(s["th"], 1)

        @block.tensor
        def _(pe):
            def turn(dst_bank, src, rows, sem, n=NT):
                for t in range(n):
                    r = pe.transpose(ps[0:rows, dst_bank + t // 4, t % 4 * P:(t % 4 + 1) * P], src(t), ident[:, :])
                r.then_inc(sem, 1)

            pe.wait_ge(s["ids2"], 2)
            pe.wait_ge(s["w_in"], 16 * 6)
            for n in range(3):
                for c in range(DC):
                    r = pe.transpose(ps[:, 4 + n, c * P:c * P + DA], wload[:, n, c * P:(c + 1) * P], ident[0:DA, 0:DA])
            r.then_inc(s["w_turned"], 1)
            RH = REL * H
            HB = NT // 2
            nblk = NQ * PARTS * NT // P

            def adj_in_rows(t):
                pe.wait_ge(adj_in[t % NADJ], 16 * (t // NADJ + 1))
                before = t - 1 if t <= ADJ_FIRST else t - 2
                if t == ADJ_FIRST + 1:
                    before = t - 2
                if before >= 0:
                    pe.wait_ge(s["adj_copied_b"], min(2 * (before + 1), HB + before + 1))
                    if before >= HB:
                        pe.wait_ge(s["adj_copied"], before + 1 - HB)
                for w in range(2):
                    bank = (2 * (t % 2) if t >= ADJ_FIRST else 2) + w
                    for j in range(HB):
                        r = pe.transpose(psb[:, bank, j * P:(j + 1) * P],
                                         adjb[:, t % NADJ, (w * HB + j) * P:(w * HB + j + 1) * P], identb[:, :])
                    r.then_inc(s["adj_turned"], 1)

            def features():
                pe.wait_ge(s["h_ready"], 1)
                pe.wait_ge(s["adj_copied_b"], 2 * ADJ_FIRST)
                turn(0, lambda t: h[:, t, 0:DA], DA, s["h_turned"])
                pe.wait_ge(s["w_copied"], 1)
                pe.wait_ge(s["a_in"], 16 * 3)
                for n in range(2):
                    for r in range(REL):
                        for c in range(DC):
                            o = (n * REL + r) * H
                            m = pe.matmul(ps[0:DA, 7, o:o + H], wT[:, n, c, :], arel[:, r, n * DC + c, :],
                                          start=(c == 0), stop=(c == DC - 1))
                m.then_inc(s["wa_done"], 1)
                for hh in range(H):
                    c, p0 = hh // 2, hh % 2 * D
                    m = pe.matmul(ps[0:DA, 5 + hh % 2, c * D:(c + 1) * D], wT[p0:p0 + D, 2, c, :], pw[p0:p0 + D, c, :],
                                  start=True, stop=True)
                m.then_inc(s["vw_done"], 1)
                pe.wait_ge(s["hT_ready"], 2)
                pe.wait_ge(s["wall_ready"], 1)
                for t in range(NT):
                    m = pe.matmul(ps[:, 4, t * NQ:(t + 1) * NQ], hT[0:DA, t * P:(t + 1) * P], wall[:, :],
                                  start=True, stop=True)
                m.then_inc(s["s_done"], 1)

            def value_rows(t):
                pe.wait_ge(s["vw_ready"], 1)
                if t >= 2:
                    pe.wait_ge(s["vp_read"], t - 1)
                pe.matmul(ps[:, 5 + t % 2, :], hT[0:DA, t * P:(t + 1) * P], wload[:, 2, :], start=True, stop=True)\
                    .then_inc(s["vp_done"], 1)

            def maxima(step):
                if step == 0:
                    pe.wait_ge(s["mx_done"], 1)
                    pe.transpose(ps[0:RH, 7, 0:P], small[:, 0:RH], ident[:, :]).then_inc(s["mx_read"], 1)
                elif step == 1:
                    pe.wait_ge(s["mxrow"], 1)
                    pe.wait_ge(s["ones"], 3)
                    pe.matmul(ps[:, 7, P:P + RH], onesf[0:RH, :], small[0:RH, 24:24 + RH], start=True, stop=True)\
                        .then_inc(s["mxb"], 1)
                else:
                    pe.wait_ge(s["m_ready"], 1)
                    pe.wait_ge(s["split_ready"], 1)
                    flat = split.rearrange("p q c t -> p (q c t)")
                    for c in range(nblk):
                        bank, o = (4, c * P) if c < 8 else (7, HALF + (c - 8) * P)
                        r = pe.transpose(psb[:, bank, o:o + P], flat[:, c * P:(c + 1) * P], identb[:, :])
                    r.then_inc(s["split_turned"], 1)
                    pe.transpose(ps[:, 7, 0:P], m_tmp[:, 0:H, :].rearrange("p h t -> p (h t)"), ident[:, :])\
                        .then_inc(s["m_turned"], 1)

            for kind, t in PROLOGUE:
                if kind == "adj":
                    adj_in_rows(t)
                elif kind == "value":
                    value_rows(t)
                elif kind == "max":
                    maxima(t)
                else:
                    features()

            def score(k, kk, carried):
                jt, i0, b = kk % NT, kk // NT % BLOCKS * HALF, kk // PER_HEAD
                if kk >= SLOTS or carried:
                    pe.wait_ge(s["leaked"], k - SLOTS + 1)
                if kk >= 2 or carried:
                    pe.wait_ge(s["selected"], k - 1)
                for r, bank in ((0, kk % SLOTS), (1, 4 + kk % 2)):
                    p0 = 32 * (2 * r + kk % 2)
                    m = pe.matmul(ps[:, bank, :], op_l[p0:p0 + 2 * PARTS, b, jt * P:(jt + 1) * P],
                                  op_r[p0:p0 + 2 * PARTS, b, i0:i0 + HALF], start=True, stop=True)
                m.then_inc(s["scores"], 1)

            def aggregate(k, kk, acc, carried, step):
                jt, blk, b = kk % NT, kk // NT, kk // PER_HEAD
                if kk % PER_HEAD == 0 and step is not None:
                    pe.wait_ge(valued[b], (step + 1) * 16)
                pe.wait_ge(s["weights"], k + 1)
                if jt == 0 and (blk >= 2 or carried):
                    pe.wait_ge(s["acc_free"], acc + blk - 1)
                pe.matmul(ps[0:DA, 6 + blk % 2, :], vst[:, b, jt, :], ring[:, kk % RING, :],
                          start=(jt == 0), stop=(jt == NT - 1)).then_inc(s["products"], 1)

            def tiles(base, n, step, acc, carried, drain):
                for kk in range(n + (LAG_P if drain else 0)):
                    if kk < n:
                        if kk % PER_HEAD == 0 and step is not None:
                            pe.wait_ge(staged[kk // PER_HEAD], (step + 1) * STAGED)
                        score(base + kk, kk, carried)
                    mm = kk - LAG_P
                    if mm >= 0:
                        aggregate(base + mm, mm, acc, carried, step)
                    elif carried:
                        aggregate(base + mm, mm + PAIR, acc - 2 * BLOCKS, carried, None)

            pe.wait_ge(s["adj_copied"], NT - HB)
            pe.wait_ge(s["adj_copied_b"], NT + HB)
            pe.wait_ge(s["m_copied"], 1)
            tiles(0, PAIR, 0, 0, False, False)
            with pe.Fori(1, H // 2) as i:
                tiles(i * PAIR, PAIR, i, i * (2 * BLOCKS), True, False)
            tiles(TILES0, 0, None, H * BLOCKS, True, True)
            pe.wait_ge(s["acc_free"], H * BLOCKS)
            for t in range(NT):
                if t >= 2:
                    pe.wait_ge(s["out_taken"], t - 1)
                for hh in range(H):
                    r = pe.transpose(ps[:, 2 * (t % 2) + hh // 4, hh % 4 * P:hh % 4 * P + DA],
                                     outT[0:DA, hh, t * P:(t + 1) * P], ident[0:DA, 0:DA])
                r.then_inc(s["out_turned"], 1)
            pe.wait_ge(s["h_ready"], 2)
            turn(0, lambda t: h[:, t, 0:DA], DA, s["h_turned"])
            pe.wait_ge(s["hT_ready"], 4)
            for t in range(NT):
                m = pe.matmul(ps[:, 4, t * 2 * E:(t + 1) * 2 * E], hT[0:D, t * P:(t + 1) * P], wkq[:, :], start=True, stop=True)
            m.then_inc(s["kqn_done"], 1)
            pe.wait_ge(s["kq_done"], 1)
            for bank, w in ((0, 1), (2, 0)):
                for t in range(NT):
                    r = pe.transpose(psb[0:ER, bank + t // 8, t % 8 * P:(t % 8 + 1) * P], kq_slot[:, w, t, :], identb[:, :])
                r.then_inc(s["kq_t"], 1)
            pe.wait_ge(s["mx_done"], 2)
            for w in range(2):
                r = pe.transpose(ps[0:1, 5, w * P:(w + 1) * P], small[:, w:w + 1], ident[:, :])
            r.then_inc(s["big_ready"], 1)
            pe.wait_ge(s["big_b"], 2)
            pe.matmul(ps[:, 5, 2 * P:2 * P + 1], onesf[0:1, :], small[0:1, 5:6], start=True, stop=True).then_inc(s["big_s"], 1)
            pe.wait_ge(s["kq_ready"], 2)
            for k in range(NB * NT + 3):
                if k < NB * NT:
                    jt, b, p2 = k // NB, k % NB, k % 2
                    if k >= 2:
                        pe.wait_ge(s["e_exp"], k - 1)
                    for w in range(2):
                        m = pe.matmul(ps[:, 2 * p2 + w, :], qT[0:ER, jt * P:(jt + 1) * P],
                                      kT[0:ER, b * TW + w * HALF:b * TW + (w + 1) * HALF], start=True, stop=True)
                    m.then_inc(s["e_scores"], 1)
                if k >= 3:
                    mm = k - 3
                    jt, b = mm // NB, mm % NB
                    pe.wait_ge(s["e_masked"], mm + 1)
                    for w in range(2):
                        m = pe.matmul(ps[0:DA, 4 + 2 * b + w, :], h[:, jt, 0:DA], eT[:, jt, b * TW + w * HALF:b * TW + (w + 1) * HALF],
                                      start=(jt == 0), stop=(jt == NT - 1))
                    m.then_inc(s["e_products"], 1)

            def turn_y(n, rows):
                pe.wait_ge(s["y_read"], 2 * n + 2)
                for t in range(NT):
                    r = pe.transpose(ps[:, t // 4, t % 4 * P:t % 4 * P + rows], yT[0:rows, t * P:(t + 1) * P],
                                     ident[0:rows, 0:rows])
                r.then_inc(s["y_turned"], 1)

            turn_y(0, DA)
            for n in range(1, 4):
                pe.wait_ge(s["y_ready"], n)
                for jp in range(NT // 2):
                    for c in range(4):
                        for w in range(2):
                            jt = 2 * jp + w
                            m = pe.matmul(ps[w * D:(w + 1) * D, 4 + c, :], y[:, jt, :], eT[:, jt, c * HALF:(c + 1) * HALF],
                                          start=(jp == 0), stop=(jp == NT // 2 - 1))
                m.then_inc(s["y_products"], 1)
                turn_y(n, P)
            pe.transpose(ps[0:D, 4, 0:D], w2[:, :], ident[0:D, 0:D]).then_inc(s["w_turned"], 1)
            pe.wait_ge(s["w_copied"], 2)
            pe.matmul(ps[0:D, 5, 0:2], w2T[:, :], a12[:, :], start=True, stop=True).then_inc(s["wa_done"], 1)
            pe.wait_ge(s["h_ready"], 3)
            turn(0, lambda t: h[:, t, 0:DA], DA, s["h_turned"])
            pe.wait_ge(s["hT_ready"], 6)
            pe.wait_ge(s["wall_ready"], 2)
            for t in range(NT):
                m = pe.matmul(ps[:, 5, 16 + 2 * t:18 + 2 * t], hT[0:D, t * P:(t + 1) * P], w2a[:, :], start=True, stop=True)
            m.then_inc(s["s2_done"], 1)
            pe.wait_ge(s["mx_done"], 3)
            pe.transpose(ps[0:1, 4, 0:P], small[:, 0:1], ident[:, :]).then_inc(s["mx_read"], 1)
            pe.wait_ge(s["mxrow"], 2)
            pe.matmul(ps[:, 4, P:P + 1], onesf[0:1, :], small[0:1, 20:21], start=True, stop=True).then_inc(s["mxb"], 1)
            pe.wait_ge(s["split_ready"], 2)
            flat2 = split[:, 0:4, :, :].rearrange("p q c t -> p (q c t)")
            for c in range(2):
                r = pe.transpose(psb[0:96, 0, c * P:(c + 1) * P], flat2[:, c * 96:(c + 1) * 96], identb[:, :])
            r.then_inc(s["split_turned"], 1)
            pe.wait_ge(s["m_ready"], 2)
            pe.transpose(ps[0:NT, 4, 0:P], m_tmp[:, 0, :], ident[:, :]).then_inc(s["m_turned"], 1)
            for t in range(NT):
                m = pe.matmul(ps[:, 6 + t // 8, t % 8 * D:(t % 8 + 1) * D], hT[0:D, t * P:(t + 1) * P], w2[:, :],
                              start=True, stop=True)
            m.then_inc(s["wh_done"], 1)
            pe.wait_ge(s["m_copied"], 2)
            pe.wait_ge(s["ops2"], 16 * 9)
            pe.wait_ge(s["wh_ready"], 1)
            tiles(TILES0, PER_HEAD, None, H * BLOCKS, False, True)
            pe.wait_ge(s["acc_free"], (H + 1) * BLOCKS)
            for t in range(NT):
                r = pe.transpose(ps[:, t // 4, t % 4 * P:t % 4 * P + DA], outT[0:DA, 0, t * P:(t + 1) * P],
                                 ident[0:DA, 0:DA])
            r.then_inc(s["out_turned"], 1)
            pe.wait_ge(s["h_ready"], 4)
            turn(0, lambda t: h[:, t, :], DX, s["h_turned"])
            turn(4, lambda t: g3[:, 0, t, :], DX, s["g_turned"])
            pe.wait_ge(s["g_read"], 2)
            turn(0, lambda t: g3[:, 1, t, :], DX, s["g_turned"])
            pe.wait_ge(s["g_read"], 3)
            for k in range(n3 + LAG_S):
                if k < n3:
                    jt, c = TILES3[k]
                    for bank, rhs, sem, read in ((0, rden, s["den"], s["den_c"]), (1, rdis, s["dis"], s["dis_c"])):
                        if k >= 1:
                            pe.wait_ge(read, k)
                        pe.matmul(ps[:, bank, :], lhs3[0:DX, jt * P:(jt + 1) * P], rhs[0:DX, c * HALF:(c + 1) * HALF],
                                  start=True, stop=True).then_inc(sem, 1)
                m = k - LAG_T
                if 0 <= m < n3 and MIRROR[m]:
                    pe.wait_ge(s["wgt"], m + 1)
                    if MIRRORS[m] > 2:
                        pe.wait_ge(s["mirrored"], MIRRORS[m] - 2)
                    for j in range(HALF // P):
                        r = pe.transpose(ps[:, 2 + MIRRORS[m] % 2, j * P:(j + 1) * P], wD[:, m % NW, j * P:(j + 1) * P],
                                         ident[:, :])
                    r.then_inc(s["turned3"], 1)
                m = k - LAG_S
                if m >= 0:
                    u, (jt, c) = m % NW, TILES3[m]
                    pe.wait_ge(s["wm3"], m + 1)
                    r = pe.matmul(ps[0:DX, 4 + c, :], h[:, jt, :], wC[:, u, :], start=(jt == 0),
                                  stop=(jt == (c + 1) * (HALF // P) - 1))
                    if MIRROR[m]:
                        pe.wait_ge(s["mirrored"], MIRRORS[m])
                        for j in range(HALF // P):
                            r = pe.matmul(ps[0:DX, 4 + jt * P // HALF, jt * P % HALF:jt * P % HALF + P],
                                          h[:, c * (HALF // P) + j, :], wA[:, u, j * P:(j + 1) * P],
                                          start=False, stop=False)
                    r.then_inc(s["sums"], 1)
            pe.wait_ge(s["y_read"], 10)
            for t in range(NT):
                r = pe.transpose(ps[:, t // 4, t % 4 * P:t % 4 * P + DX], yT[0:DX, t * P:(t + 1) * P], ident[0:DX, 0:DX])
            r.then_inc(s["z_turned"], 1)


_INS = ['x', 'adj', 'L0_gnn_Qw', 'L0_gnn_Qb', 'L0_gnn_Kw', 'L0_gnn_Kb', 'L0_gnn_Vw', 'L0_gnn_Vb', 'L0_gnn_a',
        'L0_gnn_Pw', 'L0_gnn_Pb', 'L1_gnn_w_k', 'L1_gnn_w_q', 'L2_gnn_W', 'L2_gnn_a']


def kernel(**inputs):
    import numpy as _np
    import concourse.bacc as _bacc
    from concourse import mybir as _mybir
    from concourse.bass_utils import run_bass_kernel_spmd as _run

    nc = _bacc.Bacc("TRN2", target_bir_lowering=False, num_devices=1)
    arrays, args = {}, []
    for name in _INS:
        a = _np.ascontiguousarray(inputs[name])
        arrays[f"in_{name}_dram"] = a
        args.append(nc.dram_tensor(f"in_{name}_dram", a.shape, _mybir.dt.from_np(a.dtype), kind="ExternalInput").ap())
    out = nc.dram_tensor("out_dram", inputs["x"].shape, _mybir.dt.float32, kind="ExternalOutput").ap()
    gnn_stack(nc, *args, out)
    r = _run(nc, [arrays], core_ids=[0])
    return r.results[0]["out_dram"]
```

```python
import math
from contextlib import ExitStack

import concourse.bass as bass
from concourse import mybir

P = 128
ALU = mybir.AluOpType
ACT = mybir.ActivationFunctionType
AX = mybir.AxisListType
F32 = mybir.dt.float32
BF16 = mybir.dt.bfloat16
U8 = mybir.dt.uint8
I32 = mybir.dt.int32

LN_EPS = 1e-5
NORM_EPS = 1e-12
BALL_EPS = 1e-7
SLOPE = 0.2
MASKED = -9e15


def gnn_stack(nc, x_d, adj_d, Qw, Qb, Kw, Kb, Vw, Vb, a_rel, Pw, Pb, w_k, w_q, W2, a2, out_d):
    N, D = x_d.shape
    NT = N // P
    H = a_rel.shape[2]
    DM = Qw.shape[1]
    DC = DM // P
    REL = 2
    E = w_k.shape[1]
    HALF = 512
    TW = 2 * HALF
    NB = N // TW
    PARTS = 3
    DA = D + 1
    DX = D + 2
    RING = 16
    BLOCKS = N // HALF
    PER_HEAD = BLOCKS * NT
    PAIR = 2 * PER_HEAD
    SLOTS = 4
    NQ = 2 * REL * H

    ctx = ExitStack()
    with ctx:
        def sb(name, shape, dt=F32):
            return ctx.enter_context(nc.sbuf_tensor(name, shape, dt))

        big = sb("big", [P, NT * N])
        mask = sb("mask", [P, NT, N], U8)
        x = sb("x_nat", [P, NT, D])
        h = sb("h_nat", [P, NT, DX])
        hT = sb("hT", [P, N])
        work = sb("work", [P, NT, D])
        ident = sb("ident", [P, P])
        identb = sb("identb", [P, P], BF16)
        onesf = sb("onesf", [P, P])
        stat = sb("stat", [P, 8, NT])
        small = sb("small", [P, 64])
        op_l = sb("op_l", [P, 2, N], BF16)
        op_r = sb("op_r", [P, 2, N], BF16)
        wall = sb("wall", [DA, NQ])
        arel = sb("arel", [P, REL, 2 * DC, H])
        pb = sb("pb", [P, D])
        wkq = sb("wkq", [D, 2 * E])
        w2 = sb("w2", [D, D])
        w2T = sb("w2T", [D, D])
        a12 = sb("a12", [D, 2])
        w2a = sb("w2a", [D, 2])

        at = [0]

        def part(n, shape=None):
            v = big[:, at[0]:at[0] + n]
            at[0] += n
            return v
        outT = part(H * N).rearrange("p (h n) -> p h n", h=H)
        ring = part(RING * HALF).rearrange("p (r n) -> p r n", r=RING)
        mrow = part(2 * N).rearrange("p (b n) -> p b n", b=2)
        vst = part(2 * NT * DA).rearrange("p (b t d) -> p b t d", b=2, t=NT)
        per_head = ring.rearrange("p r n -> p (r n)").rearrange("p (t h d) -> p t h d", t=NT, h=H)
        assert at[0] <= NT * N
        at[0] = 0
        vp = part(NT * H * DA).rearrange("p (h t d) -> p h t d", h=H, t=NT)
        s_nat = part(NQ * NT).rearrange("p (q t) -> p q t", q=NQ)
        s_rem = part(NQ * NT).rearrange("p (q t) -> p q t", q=NQ)
        split = part(NQ * PARTS * NT // 2).bitcast(BF16).rearrange("p (q c t) -> p q c t", q=NQ, c=PARTS)
        splitT = part(NQ * PARTS * NT // 2).bitcast(BF16)
        m_nat = part(REL * H * NT).rearrange("p (q t) -> p q t", q=REL * H)
        m_tmp = part(REL * H * NT).rearrange("p (q t) -> p q t", q=REL * H)
        mT = part(P)
        wload = part(3 * DM).rearrange("p (w n) -> p w n", w=3)[0:DA, :, :]
        wT = part(3 * DC * DA).rearrange("p (w c n) -> p w c n", w=3, c=DC)
        pw = part(DC * D).rearrange("p (c n) -> p c n", c=DC)
        assert at[0] <= H * N
        adjb = ring.rearrange("p r n -> p (r n)").bitcast(BF16).rearrange("p (r n) -> p r n", n=N)
        NADJ = RING * HALF * 2 // N
        eT = big[:, :].rearrange("p (t n) -> p t n", t=NT)
        Q_PART, K_PART = (0, 1, 0, 2, 0, 1), (0, 0, 1, 0, 2, 1)
        ER = len(Q_PART) * E
        qT, kT = op_l[:, 0, :], op_r[:, 0, :]
        y = sb("y_nat", [P, NT, D])
        wflat = work[:, :, :].rearrange("p t d -> p (t d)")
        KQ = NT * 2 * E
        kq, kq_rem = wflat[:, 0:KQ], wflat[:, KQ:2 * KQ]
        kq_part = wflat[:, 2 * KQ:2 * KQ + 3 * KQ // 2].bitcast(BF16).rearrange("p (c n) -> p c n", c=PARTS)
        kq_slot = y[:, :, :].rearrange("p t d -> p (t d)")[:, 0:NT * ER].bitcast(BF16)\
            .rearrange("p (w t e) -> p w t e", w=2, t=NT)
        yT = hT
        Y = [y[:, :, :], h[:, :, 0:D], y[:, :, :], h[:, :, 0:D]]
        APPS = len(Y)
        TB = HALF // P
        at[0] = 0
        lhs3 = part(N)
        rden = part(N)
        rdis = part(N)
        NW = 8
        wA = part(NW * HALF).rearrange("p (r n) -> p r n", r=NW)
        wB = part(NW * HALF).rearrange("p (r n) -> p r n", r=NW)
        wC = part(NW * HALF).rearrange("p (r n) -> p r n", r=NW)
        wD = part(NW * HALF).rearrange("p (r n) -> p r n", r=NW)
        assert at[0] <= NT * N
        at[0] = 3 * N
        g3 = part(2 * NT * DX).rearrange("p (v t d) -> p v t d", v=2, t=NT)
        at[0] = 3 * N
        z = part(NT * DX).rearrange("p (t d) -> p t d", t=NT)
        w3 = part(NT * D).rearrange("p (t d) -> p t d", t=NT)

        ps = ctx.enter_context(nc.psum_tensor("ps", [P, 8, HALF], F32))
        psb = ps[:, :, :].rearrange("p b n -> p (b n)").bitcast(BF16).rearrange("p (b n) -> p b n", b=8)

        split_d = nc.dram_tensor("split_scratch", [NQ, PARTS, N], BF16, kind="Internal").ap()
        split2_d = nc.dram_tensor("split2_scratch", [4, PARTS, N], BF16, kind="Internal").ap()
        m_d = nc.dram_tensor("max_scratch", [H, N], F32, kind="Internal").ap()
        m2_d = nc.dram_tensor("max2_scratch", [1, N], F32, kind="Internal").ap()
        vp_d = nc.dram_tensor("value_scratch", [H, P, NT * DA], F32, kind="Internal").ap()

        names = """x_in w_in a_in l12_in staged0 staged1 valued0 valued1 rows_out m_out vp_out out_done ids ids2
            ones dve_chain adj_turned adj_copied adj_copied_b ln_var ln_std h_ready h_turned hT_ready
            w_turned w_copied wa_done wall_ready s_done mx_done mx_read mxrow mxb m_ready split_ready
            split_turned split_copied m_turned m_copied vw_done vw_ready vp_done vp_read vp_ones scores
            scores_seen selected relus leaked shifted weights products acc_free out_turned out_taken
            half_sums quarter_sums head_sums x_ready kq_done kq_ready kqn_done big_ready kq_t big_b big_s
            big_bias e_scores e_exp e_masked e_products y_read y_turned y_ready y_products ops2 wh_done
            wh_ready s2_done x2 den dis den_c dis_c logs ratio ratioc un l1 l2 art scl scl_e wgt wm3 turned3
            mirrored sums z_turned th_in th h3_ready h2_ready beta_ready s2_scaled v_ready h_dot coef_ready
            h_scaled g_turned g_read g_read_b""".split()
        s = {n: ctx.enter_context(nc.semaphore(n)) for n in names}
        adj_in = [ctx.enter_context(nc.semaphore(f"adj_in{n}")) for n in range(NADJ)]
        staged = [s["staged0"], s["staged1"]]
        valued = [s["valued0"], s["valued1"]]
        STAGED = 16 * (4 * 2 + 1)

        def bc(v, n=D):
            return v.unsqueeze(2).to_broadcast([P, NT, n])

        def row_group(op, b, g, r0, n):
            return op[32 * g + r0:32 * g + r0 + n, b, :]

        block = ctx.enter_context(nc.Block())

        @block.sync
        def _(sp):
            def stage(b, sq, s2q, m_row):
                sp.dma_start(mrow[:, b, :], m_row.to_broadcast([P, N])).then_inc(staged[b], 16)
                for g in range(4):
                    sp.dma_start(row_group(op_l, b, g, 0, PARTS), s2q(g // 2)).then_inc(staged[b], 16)
                    sp.dma_start(row_group(op_r, b, g, PARTS, PARTS), sq(g // 2)).then_inc(staged[b], 16)

            def stage_values(b, v_src):
                sp.dma_start(vst[:, b, :, :].rearrange("p t d -> p (t d)"), v_src).then_inc(valued[b], 16)

            sp.dma_start(x[:, :, :], x_d.rearrange("(t p) d -> p t d", p=P)).then_inc(s["x_in"], 16)
            for n, (w, b) in enumerate(((Qw, Qb), (Kw, Kb), (Vw, Vb))):
                sp.dma_start(wload[0:D, n, :], w).then_inc(s["w_in"], 16)
                sp.dma_start(wload[D:DA, n, :], b.rearrange("(o n) -> o n", o=1)).then_inc(s["w_in"], 16)
            for r in range(REL):
                sp.dma_start(arel[:, r, :, :], a_rel[r, :, :].rearrange("(c p) h -> p c h", p=P))\
                    .then_inc(s["a_in"], 16)
            sp.dma_start(pw[:, :, :], Pw.rearrange("(c p) n -> p c n", p=P)).then_inc(s["a_in"], 16)
            sp.dma_start(pb[:, :], Pb.rearrange("(o n) -> o n", o=1).to_broadcast([P, D])).then_inc(s["l12_in"], 16)
            sp.dma_start(wkq[:, 0:E], w_k).then_inc(s["l12_in"], 16)
            sp.dma_start(wkq[:, E:2 * E], w_q).then_inc(s["l12_in"], 16)
            sp.dma_start(w2[:, :], W2).then_inc(s["l12_in"], 16)
            with nc.allow_non_contiguous_dma(reason="128 values"):
                sp.dma_start(a12[:, :], a2.rearrange("(c p) o -> p (c o)", c=2)).then_inc(s["l12_in"], 16)
            sp.wait_ge(s["split_copied"], 1)
            for c in range(NQ * PARTS * NT // P):
                sp.dma_start(split_d.rearrange("q c (t n) -> (q c t) n", n=P)[c * P:(c + 1) * P, :],
                             splitT[:, c * P:(c + 1) * P]).then_inc(s["rows_out"], 16)
            sp.wait_ge(s["m_copied"], 1)
            sp.dma_start(m_d.rearrange("h (t n) -> (h t) n", n=P), mT[:, :]).then_inc(s["m_out"], 16)
            sp.wait_ge(s["rows_out"], 16 * (NQ * PARTS * NT // P))
            sp.wait_ge(s["m_out"], 16)
            sp.wait_ge(s["ones"], 3)

            def stage_head(b, head):
                stage(b, lambda r: split_d[bass.ds(head + r * H, 1), :, :].rearrange("o c n -> (o c) n"),
                      lambda r: split_d[bass.ds(head + (REL + r) * H, 1), :, :].rearrange("o c n -> (o c) n"),
                      m_d[bass.ds(head, 1), :])

            def values(head):
                return vp[:, head, :, :].rearrange("p t d -> p (t d)")

            stage_head(0, 0)
            stage_head(1, 1)
            sp.wait_ge(s["vp_ones"], 1)
            sp.wait_ge(s["vp_read"], NT)
            stage_values(0, values(0))
            stage_values(1, values(1))
            for head in range(2, H):
                sp.dma_start(vp_d[head, :, :], values(head)).then_inc(s["vp_out"], 16)
            sp.wait_ge(s["vp_out"], 16 * (H - 2))
            with sp.Fori(1, H // 2) as i:
                for b in range(2):
                    sp.wait_ge(s["acc_free"], i * (2 * BLOCKS) + (b - 1) * BLOCKS)
                    stage_head(b, i * 2 + b)
                    stage_values(b, vp_d[bass.ds(i * 2 + b, 1), :, :].rearrange("o p n -> (o p) n"))
            sp.wait_ge(s["split_copied"], 2)
            sp.dma_start(split2_d.rearrange("q c (t n) -> (q c t) n", n=P)[0:96, :], splitT[0:96, 0:P])\
                .then_inc(s["rows_out"], 16)
            sp.dma_start(split2_d.rearrange("q c (t n) -> (q c t) n", n=P)[96:192, :], splitT[0:96, P:2 * P])\
                .then_inc(s["rows_out"], 16)
            sp.wait_ge(s["m_copied"], 2)
            sp.dma_start(m2_d.rearrange("h (t n) -> (h t) n", n=P), mT[0:NT, :]).then_inc(s["m_out"], 16)
            sp.wait_ge(s["m_out"], 32)
            sp.dma_start(mrow[:, 0, :], m2_d[0:1, :].to_broadcast([P, N])).then_inc(s["ops2"], 16)
            sp.wait_ge(s["rows_out"], 16 * (NQ * PARTS * NT // P + 2))
            sp.wait_ge(s["ones"], 5)
            for g in range(4):
                sp.dma_start(row_group(op_l, 0, g, 0, PARTS), split2_d[2 + g // 2, :, :]).then_inc(s["ops2"], 16)
                sp.dma_start(row_group(op_r, 0, g, PARTS, PARTS), split2_d[g // 2, :, :]).then_inc(s["ops2"], 16)
            sp.wait_ge(s["x_ready"], 4)
            sp.dma_start(out_d.rearrange("(t p) d -> p t d", p=P), x[:, :, :]).then_inc(s["out_done"], 16)
            sp.wait_ge(s["out_done"], 16)

        TILES0 = H * PER_HEAD
        PROLOGUE = [("hT", 0), ("fold", 0), ("adj", 0), ("s", 0), ("adj", 1), ("value", 0), ("adj", 2), ("value", 1),
                    ("adj", 3), ("max", 0), ("value", 2), ("adj", 4), ("max", 1), ("value", 3), ("adj", 5), ("max", 2),
                    ("value", 4), ("value", 5), ("value", 6)]
        PROLOGUE += [x for t in range(6, NT) for x in [("adj", t)] + ([("value", t + 1)] if t + 1 < NT else [])]
        TILES1 = [(2 * jp + w, b) for jp in range(NT // 2) for b in range(NB) for w in range(2)]
        n1 = len(TILES1)
        POOL_SUMS = [t for t in range(NT) if t % 4 != 3]
        TILES3 = [(jt, c) for jt in range(NT) for c in range(jt // (HALF // P), BLOCKS)[::-1 if jt else 1]]
        n3 = len(TILES3)
        MIRROR = [c > jt // (HALF // P) for jt, c in TILES3]
        MIRRORS = [sum(MIRROR[:k + 1]) for k in range(n3)]
        LAG_T, LAG_M, LAG_S = 4, 5, 6
        LAG_E = 3
        LAG_W, LAG_P = 5, 7

        @block.gpsimd
        def _(pool):
            pool.memset(ident[:, :], 0.0).then_inc(s["ids"], 1)
            pool.memset(identb[:, :], 0.0).then_inc(s["ids"], 1)
            pool.wait_ge(s["ids"], 2)
            for m in (ident, identb):
                pool.affine_select(out=m[:, :], in_=m[:, :], compare_op=ALU.not_equal, fill=1.0, base=0,
                                   pattern=[[-1, P]], channel_multiplier=1).then_inc(s["ids2"], 1)
            for t in range(NADJ):
                pool.dma_start(adjb[:, t, :], adj_d[t * P:(t + 1) * P, :]).then_inc(adj_in[t], 16)
            pool.memset(op_l[:, :, :], 1.0).then_inc(s["ones"], 1)
            pool.memset(op_r[:, :, :], 1.0).then_inc(s["ones"], 1)
            pool.memset(onesf[:, :], 1.0).then_inc(s["ones"], 1)
            for t in range(NADJ, NT):
                pool.wait_ge(s["adj_turned"], 2 * (t - NADJ + 1))
                pool.dma_start(adjb[:, t % NADJ, :], adj_d[t * P:(t + 1) * P, :])\
                    .then_inc(adj_in[t % NADJ], 16)

            def shift(k, kk, b):
                i0 = kk // NT % BLOCKS * HALF
                pool.wait_ge(s["leaked"], k + 1)
                pool.tensor_tensor(ring[:, kk % RING, :], ring[:, kk % RING, :], mrow[:, b, i0:i0 + HALF],
                                   ALU.subtract).then_inc(s["shifted"], 1)

            with pool.Fori(0, H // 2) as i:
                for kk in range(PAIR):
                    shift(i * PAIR + kk, kk, kk // PER_HEAD)
            for t in POOL_SUMS:
                v = per_head[:, t, :, :]
                n = POOL_SUMS.index(t)
                pool.wait_ge(s["out_taken"], t + 1)
                pool.tensor_tensor(v[:, 0:4, :], v[:, 0:4, :], v[:, 4:8, :], ALU.add).then_inc(s["half_sums"], 1)
                pool.wait_ge(s["half_sums"], n + 1)
                pool.tensor_tensor(v[:, 0:2, :], v[:, 0:2, :], v[:, 2:4, :], ALU.add).then_inc(s["quarter_sums"], 1)
                pool.wait_ge(s["quarter_sums"], n + 1)
                pool.tensor_tensor(y[:, t, :], v[:, 0, :], v[:, 1, :], ALU.add).then_inc(s["head_sums"], 1)
            pool.wait_ge(s["big_bias"], 1)
            pool.wait_ge(s["e_products"], n1 // 2)
            pool.memset(op_l[:, :, :], 1.0).then_inc(s["ones"], 1)
            pool.memset(op_r[:, :, :], 1.0).then_inc(s["ones"], 1)
            for kk in range(PER_HEAD):
                shift(TILES0 + kk, kk, 0)
            for k in range(n3 + 1):
                if k < n3:
                    u = k % NW
                    pool.wait_ge(s["logs"], 2 * k + 2)
                    pool.tensor_tensor(wB[:, u, :], wB[:, u, :], wA[:, u, :], ALU.subtract).then_inc(s["ratio"], 1)
                if k >= 1:
                    u = (k - 1) % NW
                    pool.wait_ge(s["l2"], k)
                    pool.tensor_tensor(wD[:, u, :], wD[:, u, :], wC[:, u, :], ALU.subtract).then_inc(s["art"], 1)
            hf = h[:, :, 0:D]
            pool.wait_ge(s["beta_ready"], 1)
            pool.tensor_tensor(y[:, :, :], z[:, :, 0:D], bc(stat[:, 0, :]), ALU.mult).then_inc(s["s2_scaled"], 1)
            pool.wait_ge(s["v_ready"], 1)
            pool.tensor_tensor(work[:, :, :], hf, y[:, :, :], ALU.mult).then_inc(s["h_dot"], 1)
            pool.wait_ge(s["coef_ready"], 1)
            pool.tensor_tensor(work[:, :, :], hf, bc(stat[:, 4, :]), ALU.mult).then_inc(s["h_scaled"], 1)

        @block.vector
        def _(dve):
            chain = [0]

            def link(ins):
                chain[0] += 1
                ins.then_inc(s["dve_chain"], 1)
                dve.wait_ge(s["dve_chain"], chain[0])

            def ts(out, in_, s1, s2, o0, o1=None):
                if o1 is None:
                    return dve.tensor_scalar(out, in_, s1, None, o0)
                return dve.tensor_scalar(out, in_, s1, s2, o0, o1)

            def tt(out, a, b, op):
                return dve.tensor_tensor(out, a, b, op)

            roots = [0]

            def root(dst, var):
                ts(stat[:, 4, :], var, 1.0, None, ALU.mult).then_inc(s["ln_var"], 1)
                roots[0] += 1
                dve.wait_ge(s["ln_std"], roots[0])
                link(dve.reciprocal(stat[:, 6, :], stat[:, 5, :]))
                link(tt(stat[:, 6, :], stat[:, 6, :], var, ALU.mult))
                link(tt(stat[:, 6, :], stat[:, 6, :], stat[:, 5, :], ALU.add))
                link(ts(stat[:, 6, :], stat[:, 6, :], 0.5, None, ALU.mult))
                link(dve.reciprocal(dst, stat[:, 6, :]))

            def center(v):
                link(dve.reduce_sum(stat[:, 0, :], v, AX.X))
                link(dve.scalar_tensor_tensor(work[:, :, :], bc(stat[:, 0, :]), -1.0 / D, v, ALU.mult, ALU.add))

            def sum_squares(dst, v, scratch):
                link(tt(scratch, v, v, ALU.mult))
                link(dve.reduce_sum(dst, scratch, AX.X))

            def layer_norm(signal=None):
                center(x[:, :, :])
                sum_squares(stat[:, 1, :], work[:, :, :], h[:, :, 0:D])
                link(ts(stat[:, 1, :], stat[:, 1, :], 1.0 / D, LN_EPS, ALU.mult, ALU.add))
                root(stat[:, 2, :], stat[:, 1, :])
                r = dve.scalar_tensor_tensor(h[:, :, 0:D], work[:, :, :], 0.0, bc(stat[:, 2, :]), ALU.max, ALU.mult)
                if signal:
                    r.then_inc(s[signal], 1)
                else:
                    link(r)

            def split3(src, rem, dst):
                link(dve.tensor_copy(dst[:, :, 0, :], src))
                link(tt(rem, src, dst[:, :, 0, :], ALU.subtract))
                link(dve.tensor_copy(dst[:, :, 1, :], rem))
                link(tt(rem, rem, dst[:, :, 1, :], ALU.subtract))
                dve.tensor_copy(dst[:, :, 2, :], rem).then_inc(s["split_ready"], 1)

            def copy_h(n, rows):
                dve.wait_ge(s["h_turned"], n)
                dve.tensor_copy(hT[0:rows, 0:N // 2], ps[0:rows, 0:2, :].rearrange("p b n -> p (b n)"))\
                    .then_inc(s["hT_ready"], 1)

            dve.memset(h[:, :, D:DA], 1.0)
            dve.memset(vp[:, :, :, D:DA], 1.0).then_inc(s["vp_ones"], 1)
            dve.wait_ge(s["x_in"], 16)
            layer_norm("h_ready")
            dve.wait_ge(s["w_turned"], 1)
            for n in range(3):
                r = dve.tensor_copy(wT[:, n, :, :], ps[:, 4 + n, 0:DC * P].rearrange("p (c n) -> p c n", c=DC)[:, :, 0:DA])
            r.then_inc(s["w_copied"], 1)
            copy_h(1, DA)
            dve.wait_ge(s["wa_done"], 1)
            dve.tensor_copy(wall[:, :], ps[0:DA, 7, 0:NQ]).then_inc(s["wall_ready"], 1)
            dve.wait_ge(s["vw_done"], 1)
            for w in range(2):
                r = dve.tensor_copy(wload[:, 2, :].rearrange("p (c w d) -> p w c d", w=2, d=D)[:, w, :, :],
                                    ps[0:DA, 5 + w, 0:DC * D].rearrange("p (c d) -> p c d", d=D))
            r.then_inc(s["vw_ready"], 1)
            dve.wait_ge(s["s_done"], 1)
            link(dve.tensor_copy(s_nat, ps[:, 4, :].rearrange("p (t q) -> p q t", q=NQ)))
            split3(s_nat, s_rem, split)
            RH = REL * H
            dve.reduce_max(small[:, 0:RH], s_nat[:, RH:2 * RH, :], AX.X).then_inc(s["mx_done"], 1)
            dve.wait_ge(s["mx_read"], 1)
            link(dve.reduce_max(small[0:RH, 20:21], ps[0:RH, 7, 0:P], AX.X))
            ts(small[0:RH, 24:24 + RH], ident[0:RH, 0:RH], small[0:RH, 20:21], None, ALU.mult).then_inc(s["mxrow"], 1)
            dve.wait_ge(s["mxb"], 1)
            link(dve.tensor_copy(small[:, 40:40 + RH], ps[:, 7, P:P + RH]))
            link(tt(m_nat, s_nat[:, 0:RH, :], small[:, 40:40 + RH].unsqueeze(2).to_broadcast([P, RH, NT]), ALU.add))
            link(ts(m_tmp, m_nat, SLOPE, None, ALU.mult))
            link(tt(m_nat, m_nat, m_tmp, ALU.max))
            tt(m_tmp[:, 0:H, :], m_nat[:, 0:H, :], m_nat[:, H:RH, :], ALU.max).then_inc(s["m_ready"], 1)
            dve.wait_ge(s["split_turned"], 1)
            dve.tensor_copy(splitT[:, 0:2 * HALF], psb[:, 4, :])
            dve.wait_ge(s["m_turned"], 1)
            dve.tensor_copy(splitT[:, 2 * HALF:], psb[:, 7, HALF:]).then_inc(s["split_copied"], 1)
            dve.tensor_copy(mT[:, :], ps[:, 7, 0:P]).then_inc(s["m_copied"], 1)
            HB = NT // 2
            for t in range(NT // 2, NT):
                dve.wait_ge(s["adj_turned"], 2 * t + 1)
                dve.tensor_copy(mask[:, 0:HB, t * P:(t + 1) * P],
                                psb[:, 2 * (t % 2), :].rearrange("p (j n) -> p j n", n=P)).then_inc(s["adj_copied"], 1)

            def select(k, kk):
                jt, i0 = kk % NT, kk // NT % BLOCKS * HALF
                dve.wait_ge(s["scores"], k + 1)
                dve.sem_inc(s["scores_seen"], 1)
                dve.copy_predicated(ps[:, kk % SLOTS, :], mask[:, jt, i0:i0 + HALF], ps[:, 4 + kk % 2, :])\
                    .then_inc(s["selected"], 1)

            def leak(k, kk):
                r = ring[:, kk % RING, :]
                dve.wait_ge(s["relus"], k + 1)
                dve.scalar_tensor_tensor(r, ps[:, kk % SLOTS, :], SLOPE, r, ALU.mult, ALU.add)\
                    .then_inc(s["leaked"], 1)

            def take_sums(k, kk, head):
                blk = kk // NT
                dve.wait_ge(s["products"], k + 1)
                dst = outT[0:DA, bass.ds(head, 1), :] if not isinstance(head, int) else outT[0:DA, head:head + 1, :]
                i0 = blk % BLOCKS * HALF
                dve.tensor_copy(dst.rearrange("p o n -> p (o n)")[:, i0:i0 + HALF], ps[0:DA, 6 + blk % 2, :])\
                    .then_inc(s["acc_free"], 1)

            def tiles(base, n, head0, carried, drain):
                for kk in range(n + (LAG_P + 2 if drain else 0)):
                    if kk < n:
                        select(base + kk, kk)
                    if (kk >= 1 or carried) and kk - 1 < n:
                        leak(base + kk - 1, kk - 1)
                    e = kk - LAG_P - 1
                    if e % NT == NT - 1 and (e >= 0 or carried) and e < n:
                        if e == NT - 1 and not carried and n == PAIR:
                            dve.wait_ge(s["vp_out"], 16 * (H - 2))
                            for b in range(2):
                                dve.wait_ge(valued[b], 16)
                        take_sums(base + e, e, head0 + e // PER_HEAD)

            tiles(0, PAIR, 0, False, False)
            with dve.Fori(1, H // 2) as i:
                tiles(i * PAIR, PAIR, i * 2, True, False)
            tiles(TILES0, 0, H, True, True)

            dve.wait_ge(s["l12_in"], 16 * 5)
            link(tt(x[:, :, :], x[:, :, :], pb[:, :].unsqueeze(1).to_broadcast([P, NT, D]), ALU.add))
            for t in range(NT):
                q = 2 * (t % 2)
                dve.wait_ge(s["out_turned"], t + 1)
                pv = ps[:, q:q + 2, :].rearrange("p b (h d) -> p (b h) d", d=P)
                if t >= 2:
                    dve.wait_ge(s["out_taken"], t - 1)
                den = stat[:, 6:7, t % 2 * H:(t % 2 + 1) * H].rearrange("p o h -> p (o h)")
                link(dve.reciprocal(den, pv[:, :, D]))
                dve.tensor_tensor(per_head[:, t, :, :], pv[:, :, 0:D], den.unsqueeze(2).to_broadcast([P, H, D]), ALU.mult)\
                    .then_inc(s["out_taken"], 1)
                if t not in POOL_SUMS:
                    dve.wait_ge(s["out_taken"], t + 1)
                    link(dve.reduce_sum(y[:, t, :], per_head[:, t, :, :].rearrange("p h d -> p d h"), AX.X))
            dve.wait_ge(s["head_sums"], len(POOL_SUMS))
            link(tt(x[:, :, :], x[:, :, :], y[:, :, :], ALU.add))

            layer_norm()
            center(h[:, :, 0:D])
            sum_squares(stat[:, 1, :], work[:, :, :], h[:, :, 0:D])
            link(ts(stat[:, 1, :], stat[:, 1, :], NORM_EPS ** 2, None, ALU.max))
            root(stat[:, 2, :], stat[:, 1, :])
            link(ts(stat[:, 2, :], stat[:, 2, :], 1.0 / NORM_EPS, None, ALU.min))
            tt(h[:, :, 0:D], work[:, :, :], bc(stat[:, 2, :]), ALU.mult).then_inc(s["h_ready"], 1)
            copy_h(2, DA)
            dve.wait_ge(s["kqn_done"], 1)
            link(dve.tensor_copy(kq, ps[:, 4, 0:KQ]))
            link(dve.tensor_copy(kq_part[:, 0, :], kq))
            link(tt(kq_rem, kq, kq_part[:, 0, :], ALU.subtract))
            link(dve.tensor_copy(kq_part[:, 1, :], kq_rem))
            link(tt(kq_rem, kq_rem, kq_part[:, 1, :], ALU.subtract))
            link(dve.tensor_copy(kq_part[:, 2, :], kq_rem))
            for w, parts in ((1, Q_PART), (0, K_PART)):
                for n, c in enumerate(parts):
                    r = dve.tensor_copy(kq_slot[:, w, :, n * E:(n + 1) * E],
                                        kq_part[:, c, :].rearrange("p (t e) -> p t e", t=NT)[:, :, w * E:(w + 1) * E])
            r.then_inc(s["kq_done"], 1)
            link(tt(kq_rem, kq, kq, ALU.mult))
            link(dve.reduce_sum(stat[:, 0:2, :].rearrange("p a t -> p (a t)"), kq_rem.rearrange("p (m e) -> p m e", e=E), AX.X))
            dve.reduce_max(small[:, 0:2], stat[:, 0:2, :].rearrange("p a t -> p (a t)").rearrange("p (t w) -> p w t", w=2),
                           AX.X).then_inc(s["mx_done"], 1)
            dve.wait_ge(s["kq_t"], 1)
            dve.tensor_copy(qT[0:ER, :].rearrange("p (b n) -> p b n", b=2), psb[0:ER, 0:2, :]).then_inc(s["kq_ready"], 1)
            dve.wait_ge(s["big_ready"], 1)
            link(dve.reduce_max(small[0:1, 2:4], ps[0:1, 5, 0:2 * P].rearrange("p (w n) -> p w n", w=2), AX.X))
            tt(small[0:1, 4:5], small[0:1, 2:3], small[0:1, 3:4], ALU.mult).then_inc(s["big_b"], 1)
            dve.wait_ge(s["big_s"], 1)
            ts(small[:, 6:7], ps[:, 5, 2 * P:2 * P + 1], -1.0, None, ALU.mult).then_inc(s["big_bias"], 1)
            for k in range(n1):
                jt, b = TILES1[k]
                e = eT[:, jt, b * TW:(b + 1) * TW]
                dve.wait_ge(s["e_exp"], k + 1)
                tt(e, e, mask[:, jt, b * TW:(b + 1) * TW], ALU.mult).then_inc(s["e_masked"], 1)

            def take_y(n, c):
                dve.wait_ge(s["y_turned"], n * BLOCKS + c + 1)
                v = ps[:, c, :].rearrange("p (t d) -> p t d", d=P)
                of = slice(c * TB, (c + 1) * TB)
                per_row = stat[:, 3, of]
                link(dve.reduce_sum(work[:, of, :], v.rearrange("p t (w d) -> p t d w", w=2), AX.X))
                if n == 0:
                    link(dve.reciprocal(per_row, work[:, of, D - 1]))
                    link(tt(Y[0][:, of, 1:D], work[:, of, 0:D - 1], per_row.unsqueeze(2).to_broadcast([P, TB, D - 1]),
                            ALU.mult))
                    link(dve.reduce_sum(stat[:, 2, of], Y[0][:, of, 1:D], AX.X))
                    ts(Y[0][:, of, 0:1].rearrange("p t o -> p (t o)"), stat[:, 2, of], -1.0, None, ALU.mult)\
                        .then_inc(s["y_ready"], 1)
                else:
                    tt(Y[n][:, of, :], work[:, of, :], per_row.unsqueeze(2).to_broadcast([P, TB, D]), ALU.mult)\
                        .then_inc(s["y_ready"], 1)

            for n in range(APPS):
                for c in range(BLOCKS):
                    take_y(n, c)
                weight = (1.0, 0.5, None, 1.0 / 6.0)[n]
                if weight is not None:
                    dve.wait_ge(s["y_ready"], (n + 1) * BLOCKS)
                    link(dve.scalar_tensor_tensor(x[:, :, :], Y[n], weight, x[:, :, :], ALU.mult, ALU.add))

            dve.wait_ge(s["w_turned"], 2)
            dve.tensor_copy(w2T[:, :], ps[0:D, 4, 0:D]).then_inc(s["w_copied"], 1)
            dve.wait_ge(s["wa_done"], 2)
            dve.tensor_copy(w2a[:, :], ps[0:D, 5, 0:2]).then_inc(s["wall_ready"], 1)
            layer_norm("h_ready")
            copy_h(3, DA)
            dve.wait_ge(s["s2_done"], 1)
            s2v = s_nat[:, 0:4, :]
            dve.memset(s2v[:, 0:1, :], 0.0)
            dve.memset(s2v[:, 2:3, :], MASKED / SLOPE)
            link(dve.tensor_copy(s2v.rearrange("p (r w) t -> p r w t", w=2)[:, :, 1, :],
                                 ps[:, 5, 16:16 + 2 * NT].rearrange("p (t q) -> p q t", q=2)))
            split3(s2v, s_rem[:, 0:4, :], split[:, 0:4, :, :])
            dve.reduce_max(small[:, 0:1], s_nat[:, 3, :], AX.X).then_inc(s["mx_done"], 1)
            dve.wait_ge(s["mx_read"], 2)
            dve.reduce_max(small[0:1, 20:21], ps[0:1, 4, 0:P], AX.X).then_inc(s["mxrow"], 1)
            dve.wait_ge(s["mxb"], 2)
            link(dve.tensor_copy(small[:, 40:41], ps[:, 4, P:P + 1]))
            link(ts(m_nat[:, 0, :], s_nat[:, 1, :], small[:, 40:41], None, ALU.add))
            link(ts(m_tmp[:, 1, :], m_nat[:, 0, :], SLOPE, None, ALU.mult))
            tt(m_tmp[:, 0, :], m_nat[:, 0, :], m_tmp[:, 1, :], ALU.max).then_inc(s["m_ready"], 1)
            dve.wait_ge(s["split_turned"], 2)
            dve.tensor_copy(splitT[0:96, 0:2 * P], psb[0:96, 0, 0:2 * P]).then_inc(s["split_copied"], 1)
            dve.wait_ge(s["m_turned"], 2)
            dve.tensor_copy(mT[0:NT, :], ps[0:NT, 4, 0:P]).then_inc(s["m_copied"], 1)
            dve.memset(vst[:, 0, :, D:DA], 1.0)
            dve.wait_ge(s["wh_done"], 1)
            dve.tensor_copy(vst[:, 0, :, 0:D], ps[:, 6:8, :].rearrange("p b (t d) -> p (b t) d", d=D))\
                .then_inc(s["wh_ready"], 1)
            tiles(TILES0, PER_HEAD, 0, False, True)
            dve.wait_ge(s["out_turned"], NT + 1)
            v = ps[:, 0:4, :].rearrange("p b (t d) -> p (b t) d", d=P)
            link(dve.reciprocal(stat[:, 3, :], v[:, :, D]))
            link(tt(y[:, :, :], v[:, :, 0:D], bc(stat[:, 3, :]), ALU.mult))
            ts(work[:, :, :], y[:, :, :], 0.0, None, ALU.min).then_inc(s["x2"], 1)
            link(dve.scalar_tensor_tensor(x[:, :, :], y[:, :, :], 0.0, x[:, :, :], ALU.max, ALU.add))
            dve.wait_ge(s["x2"], 2)
            link(dve.scalar_tensor_tensor(x[:, :, :], work[:, :, :], 1.0, x[:, :, :], ALU.subtract, ALU.add))

            layer_norm("h3_ready")
            dve.wait_ge(s["h3_ready"], 1)
            link(tt(work[:, :, :], h[:, :, 0:D], h[:, :, 0:D], ALU.mult))
            link(dve.reduce_sum(h[:, :, DA:DX].rearrange("p t o -> p (t o)"), work[:, :, :], AX.X))
            for v in range(2):
                dve.memset(g3[:, v, :, D + v:D + v + 1], 1.0)
                r = dve.tensor_copy(g3[:, v, :, D + 1 - v:D + 2 - v], h[:, :, DA:DX])
            r.then_inc(s["h_ready"], 1)
            for dst, bank, sem, n in ((lhs3, 0, s["h_turned"], 4), (rden, 4, s["g_turned"], 1), (rdis, 0, s["g_turned"], 2)):
                dve.wait_ge(sem, n)
                dve.tensor_copy(dst[0:DX, 0:TW], ps[0:DX, bank:bank + 2, :].rearrange("p b n -> p (b n)"))\
                    .then_inc(s["g_read"], 1)
            LO, HI = 2.0 * math.log(BALL_EPS), 2.0 * math.log(1.0 - 1e-5)
            for k in range(n3 + LAG_M):
                if k >= LAG_M and MIRROR[k - LAG_M]:
                    m = k - LAG_M
                    u, (jt, c) = m % NW, TILES3[m]
                    j0 = c * (HALF // P)
                    dve.wait_ge(s["turned3"], MIRRORS[m])
                    tt(wA[:, u, :].rearrange("p (j n) -> p j n", n=P),
                       ps[:, 2 + MIRRORS[m] % 2, :].rearrange("p (j n) -> p j n", n=P),
                       mask[:, j0:j0 + HALF // P, jt * P:(jt + 1) * P], ALU.mult).then_inc(s["mirrored"], 1)
                if k < n3:
                    u = k % NW
                    if k >= NW:
                        dve.wait_ge(s["sums"], k - NW + 1)
                    dve.wait_ge(s["den"], k + 1)
                    ts(wA[:, u, :], ps[:, 0, :], BALL_EPS, None, ALU.max).then_inc(s["den_c"], 1)
                    dve.wait_ge(s["dis"], k + 1)
                    ts(wB[:, u, :], ps[:, 1, :], BALL_EPS, None, ALU.max)\
                        .then_inc(s["dis_c"], 1)
                if 2 <= k < n3 + 2:
                    u = (k - 2) % NW
                    dve.wait_ge(s["un"], k - 1)
                    dve.wait_ge(s["ratioc"], k - 1)
                    dve.scalar_tensor_tensor(wB[:, u, :], wB[:, u, :], -0.5, wA[:, u, :], ALU.mult, ALU.subtract)\
                        .then_inc(s["scl"], 1)
                if 1 <= k <= n3:
                    u = (k - 1) % NW
                    dve.wait_ge(s["ratio"], k)
                    ts(wB[:, u, :], wB[:, u, :], LO, HI, ALU.max, ALU.min).then_inc(s["ratioc"], 1)
                if 3 <= k < n3 + 3:
                    m = k - 3
                    u, (jt, c) = m % NW, TILES3[m]
                    dve.wait_ge(s["scl_e"], m + 1)
                    dve.wait_ge(s["art"], m + 1)
                    tt(wD[:, u, :], wD[:, u, :], wB[:, u, :], ALU.mult).then_inc(s["wgt"], 1)
                    dve.wait_ge(s["wgt"], m + 1)
                    tt(wC[:, u, :], wD[:, u, :], mask[:, jt, c * HALF:(c + 1) * HALF], ALU.mult).then_inc(s["wm3"], 1)
            dve.wait_ge(s["sums"], n3)
            dve.tensor_copy(yT[0:DX, 0:TW], ps[0:DX, 4:6, :].rearrange("p b n -> p (b n)")).then_inc(s["y_read"], 1)
            dve.wait_ge(s["z_turned"], 1)
            link(dve.tensor_copy(z[:, :, :], ps[:, 0:4, :].rearrange("p b (t d) -> p (b t) d", d=P)[:, :, 0:DX]))
            hf, n2 = h[:, :, 0:D], h[:, :, DA:DX].rearrange("p t o -> p (t o)")
            S2, S1, S3 = z[:, :, 0:D], z[:, :, D], z[:, :, DA]

            def dot(dst, a, b):
                link(tt(w3[:, :, :], a, b, ALU.mult))
                link(dve.reduce_sum(dst, w3[:, :, :], AX.X))

            beta, c2 = stat[:, 0, :], stat[:, 1, :]
            yy = small[:, 40:40 + NT]
            ts(beta, n2, -1.0, 1.0, ALU.mult, ALU.add).then_inc(s["beta_ready"], 1)
            dve.wait_ge(s["beta_ready"], 1)
            link(ts(c2, beta, BALL_EPS, None, ALU.max))
            dot(stat[:, 2, :], hf, S2)
            link(dve.scalar_tensor_tensor(stat[:, 2, :], stat[:, 2, :], -2.0, S1, ALU.mult, ALU.add))
            link(tt(stat[:, 2, :], stat[:, 2, :], S3, ALU.add))
            link(tt(work[:, :, :], hf, bc(stat[:, 2, :]), ALU.mult))
            dve.wait_ge(s["s2_scaled"], 1)
            link(tt(y[:, :, :], y[:, :, :], work[:, :, :], ALU.subtract))
            ts(y[:, :, :], y[:, :, :], 0.5, None, ALU.mult).then_inc(s["v_ready"], 1)
            dve.wait_ge(s["v_ready"], 1)
            dot(yy, y[:, :, :], y[:, :, :])
            link(ts(stat[:, 3, :], yy, 1e-30, None, ALU.max))
            root(stat[:, 7, :], stat[:, 3, :])
            link(tt(stat[:, 6, :], stat[:, 6, :], c2, ALU.mult))
            link(ts(stat[:, 6, :], stat[:, 6, :], BALL_EPS, None, ALU.max))
            link(dve.reciprocal(stat[:, 7, :], stat[:, 6, :]))
            link(tt(stat[:, 7, :], stat[:, 7, :], c2, ALU.mult))
            dve.reciprocal(stat[:, 3, :], stat[:, 7, :]).then_inc(s["th_in"], 1)
            dve.wait_ge(s["h_dot"], 1)
            link(dve.reduce_sum(stat[:, 2, :], work[:, :, :], AX.X))
            dve.wait_ge(s["th"], 1)
            link(tt(stat[:, 5, :], stat[:, 5, :], stat[:, 7, :], ALU.mult))
            link(tt(stat[:, 2, :], stat[:, 2, :], stat[:, 5, :], ALU.mult))
            link(tt(stat[:, 3, :], yy, stat[:, 5, :], ALU.mult))
            link(tt(stat[:, 3, :], stat[:, 3, :], stat[:, 5, :], ALU.mult))
            link(ts(stat[:, 2, :], stat[:, 2, :], 2.0, 1.0, ALU.mult, ALU.add))
            link(tt(stat[:, 4, :], stat[:, 2, :], stat[:, 3, :], ALU.add))
            link(tt(stat[:, 3, :], stat[:, 3, :], n2, ALU.mult))
            link(tt(stat[:, 2, :], stat[:, 2, :], stat[:, 3, :], ALU.add))
            link(ts(stat[:, 2, :], stat[:, 2, :], BALL_EPS, None, ALU.max))
            link(dve.reciprocal(stat[:, 2, :], stat[:, 2, :]))
            tt(stat[:, 4, :], stat[:, 4, :], stat[:, 2, :], ALU.mult).then_inc(s["coef_ready"], 1)
            link(tt(stat[:, 2, :], beta, stat[:, 2, :], ALU.mult))
            link(tt(stat[:, 2, :], stat[:, 2, :], stat[:, 5, :], ALU.mult))
            link(tt(y[:, :, :], y[:, :, :], bc(stat[:, 2, :]), ALU.mult))
            link(tt(x[:, :, :], x[:, :, :], y[:, :, :], ALU.add))
            dve.wait_ge(s["h_scaled"], 1)
            tt(x[:, :, :], x[:, :, :], work[:, :, :], ALU.add).then_inc(s["x_ready"], 4)

        @block.scalar
        def _(act):
            def root(n):
                act.wait_ge(s["ln_var"], n)
                act.activation(stat[:, 5, :], stat[:, 4, :], ACT.Sqrt).then_inc(s["ln_std"], 1)

            def copy_h(n, rows):
                act.wait_ge(s["h_turned"], n)
                act.activation(hT[0:rows, N // 2:N], ps[0:rows, 2:4, :].rearrange("p b n -> p (b n)"), ACT.Copy)\
                    .then_inc(s["hT_ready"], 1)

            HB = NT // 2

            def adj_out(t, w):
                act.wait_ge(s["adj_turned"], 2 * t + w + 1)
                act.activation(mask[:, w * HB:(w + 1) * HB, t * P:(t + 1) * P],
                               psb[:, 2 * (t % 2) + w, :].rearrange("p (j n) -> p j n", n=P),
                               ACT.Copy).then_inc(s["adj_copied_b"], 1)

            def value_out(t):
                act.wait_ge(s["vp_done"], t + 1)
                act.activation(vp[:, :, t, 0:D], ps[:, 5 + t % 2, :].rearrange("p (h d) -> p h d", h=H), ACT.Copy)\
                    .then_inc(s["vp_read"], 1)

            root(1)
            for kind, t in PROLOGUE:
                if kind == "adj":
                    for w in range(2):
                        if w or t < NT // 2:
                            adj_out(t, w)
                elif kind == "value":
                    value_out(t)
                elif kind == "hT":
                    copy_h(1, DA)

            def tiles(base, n, carried, drain):
                for kk in range(n + (LAG_W if drain else 0)):
                    if kk < n:
                        k = base + kk
                        act.wait_ge(s["selected"], k + 1)
                        if kk >= RING or carried:
                            act.wait_ge(s["products"], k - RING + 1)
                        act.activation(ring[:, kk % RING, :], ps[:, kk % SLOTS, :], ACT.Relu, scale=1.0 - SLOPE)\
                            .then_inc(s["relus"], 1)
                    m = kk - LAG_W
                    if m >= 0 or carried:
                        act.wait_ge(s["shifted"], base + m + 1)
                        act.activation(ring[:, m % RING, :], ring[:, m % RING, :], ACT.Exp).then_inc(s["weights"], 1)

            tiles(0, PAIR, False, False)
            with act.Fori(1, H // 2) as i:
                tiles(i * PAIR, PAIR, True, False)
            tiles(TILES0, 0, True, True)
            root(2)
            root(3)
            copy_h(2, DA)
            act.wait_ge(s["kq_t"], 2)
            act.activation(kT[0:ER, :].rearrange("p (b n) -> p b n", b=2), psb[0:ER, 2:4, :], ACT.Copy)\
                .then_inc(s["kq_ready"], 1)
            act.wait_ge(s["big_b"], 1)
            act.activation(small[0:1, 5:6], small[0:1, 4:5], ACT.Sqrt, scale=1.0 / E).then_inc(s["big_b"], 1)
            act.preload_act_table_set("natural_log_exp_and_others")
            act.wait_ge(s["big_bias"], 1)
            for k in range(n1):
                (jt, b), p2 = TILES1[k], k % 2
                act.wait_ge(s["e_scores"], k + 1)
                act.activation(eT[:, jt, b * TW:(b + 1) * TW], ps[:, 2 * p2:2 * p2 + 2, :].rearrange("p b n -> p (b n)"),
                               ACT.Exp, bias=small[:, 6:7], scale=1.0 / math.sqrt(E)).then_inc(s["e_exp"], 1)
            for n in range(APPS):
                for c in range(BLOCKS):
                    if n == 0:
                        act.wait_ge(s["e_products"], n1 // 2)
                    else:
                        act.wait_ge(s["y_products"], (n - 1) * BLOCKS + c + 1)
                    act.activation(yT[:, c * HALF:(c + 1) * HALF], ps[:, 4 + c, :], ACT.Copy)\
                        .then_inc(s["y_read"], 1)
            root(4)
            act.preload_act_table_set("natural_log_exp_and_others")
            copy_h(3, DA)
            tiles(TILES0, PER_HEAD, False, True)
            act.wait_ge(s["x2"], 1)
            act.activation(work[:, :, :], work[:, :, :], ACT.Exp).then_inc(s["x2"], 1)
            root(5)
            act.preload_act_table_set("natural_log_exp_and_others")
            act.wait_ge(s["h3_ready"], 1)
            for v in range(2):
                act.activation(g3[:, v, :, 0:D], h[:, :, 0:D], ACT.Copy, scale=-2.0).then_inc(s["h2_ready"], 1)
            for dst, bank, sem, n in ((lhs3, 2, s["h_turned"], 4), (rden, 6, s["g_turned"], 1), (rdis, 2, s["g_turned"], 2)):
                act.wait_ge(sem, n)
                act.activation(dst[0:DX, TW:N], ps[0:DX, bank:bank + 2, :].rearrange("p b n -> p (b n)"), ACT.Copy)\
                    .then_inc(s["g_read_b"], 1)
            for k in range(n3 + 2):
                if k < n3:
                    u = k % NW
                    act.wait_ge(s["den_c"], k + 1)
                    act.activation(wA[:, u, :], wA[:, u, :], ACT.Ln).then_inc(s["logs"], 1)
                    act.wait_ge(s["dis_c"], k + 1)
                    act.activation(wB[:, u, :], wB[:, u, :], ACT.Ln).then_inc(s["logs"], 1)
                if 1 <= k <= n3:
                    u = (k - 1) % NW
                    act.wait_ge(s["ratioc"], k)
                    act.activation(wC[:, u, :], wB[:, u, :], ACT.Exp, scale=0.5).then_inc(s["un"], 1)
                    act.wait_ge(s["un"], k)
                    act.activation(wD[:, u, :], wC[:, u, :], ACT.Ln, bias=1.0).then_inc(s["l1"], 1)
                    act.wait_ge(s["l1"], k)
                    act.activation(wC[:, u, :], wC[:, u, :], ACT.Ln, bias=1.0, scale=-1.0).then_inc(s["l2"], 1)
                if k >= 2:
                    u = (k - 2) % NW
                    act.wait_ge(s["scl"], k - 1)
                    act.activation(wB[:, u, :], wB[:, u, :], ACT.Exp).then_inc(s["scl_e"], 1)
            act.wait_ge(s["sums"], n3)
            act.activation(yT[0:DX, TW:N], ps[0:DX, 6:8, :].rearrange("p b n -> p (b n)"), ACT.Copy).then_inc(s["y_read"], 1)
            root(6)
            act.wait_ge(s["th_in"], 1)
            act.activation(stat[:, 5, :], stat[:, 3, :], ACT.Tanh).then_inc(s["th"], 1)

        @block.tensor
        def _(pe):
            def turn(dst_bank, src, rows, sem, n=NT):
                for t in range(n):
                    r = pe.transpose(ps[0:rows, dst_bank + t // 4, t % 4 * P:(t % 4 + 1) * P], src(t), ident[:, :])
                r.then_inc(sem, 1)

            pe.wait_ge(s["ids2"], 2)
            pe.wait_ge(s["w_in"], 16 * 6)
            for n in range(3):
                for c in range(DC):
                    r = pe.transpose(ps[:, 4 + n, c * P:c * P + DA], wload[:, n, c * P:(c + 1) * P], ident[0:DA, 0:DA])
            r.then_inc(s["w_turned"], 1)
            RH = REL * H
            HB = NT // 2
            nblk = NQ * PARTS * NT // P

            def adj_in_rows(t):
                pe.wait_ge(adj_in[t % NADJ], 16 * (t // NADJ + 1))
                before = t - 2
                if before < 0:
                    pe.wait_ge(s["hT_ready"], 2)
                else:
                    pe.wait_ge(s["adj_copied_b"], min(2 * (before + 1), HB + before + 1))
                    if before >= HB:
                        pe.wait_ge(s["adj_copied"], before + 1 - HB)
                for w in range(2):
                    bank = 2 * (t % 2) + w
                    for j in range(HB):
                        r = pe.transpose(psb[:, bank, j * P:(j + 1) * P],
                                         adjb[:, t % NADJ, (w * HB + j) * P:(w * HB + j + 1) * P], identb[:, :])
                    r.then_inc(s["adj_turned"], 1)

            def features():
                pe.wait_ge(s["h_ready"], 1)
                turn(0, lambda t: h[:, t, 0:DA], DA, s["h_turned"])

            def fold():
                pe.wait_ge(s["w_copied"], 1)
                pe.wait_ge(s["a_in"], 16 * 3)
                for n in range(2):
                    for r in range(REL):
                        for c in range(DC):
                            o = (n * REL + r) * H
                            m = pe.matmul(ps[0:DA, 7, o:o + H], wT[:, n, c, :], arel[:, r, n * DC + c, :],
                                          start=(c == 0), stop=(c == DC - 1))
                m.then_inc(s["wa_done"], 1)
                for hh in range(H):
                    c, p0 = hh // 2, hh % 2 * D
                    m = pe.matmul(ps[0:DA, 5 + hh % 2, c * D:(c + 1) * D], wT[p0:p0 + D, 2, c, :], pw[p0:p0 + D, c, :],
                                  start=True, stop=True)
                m.then_inc(s["vw_done"], 1)

            def score_vectors():
                pe.wait_ge(s["hT_ready"], 2)
                pe.wait_ge(s["wall_ready"], 1)
                for t in range(NT):
                    m = pe.matmul(ps[:, 4, t * NQ:(t + 1) * NQ], hT[0:DA, t * P:(t + 1) * P], wall[:, :],
                                  start=True, stop=True)
                m.then_inc(s["s_done"], 1)

            def value_rows(t):
                pe.wait_ge(s["vw_ready"], 1)
                if t >= 2:
                    pe.wait_ge(s["vp_read"], t - 1)
                pe.matmul(ps[:, 5 + t % 2, :], hT[0:DA, t * P:(t + 1) * P], wload[:, 2, :], start=True, stop=True)\
                    .then_inc(s["vp_done"], 1)

            def maxima(step):
                if step == 0:
                    pe.wait_ge(s["mx_done"], 1)
                    pe.transpose(ps[0:RH, 7, 0:P], small[:, 0:RH], ident[:, :]).then_inc(s["mx_read"], 1)
                elif step == 1:
                    pe.wait_ge(s["mxrow"], 1)
                    pe.wait_ge(s["ones"], 3)
                    pe.matmul(ps[:, 7, P:P + RH], onesf[0:RH, :], small[0:RH, 24:24 + RH], start=True, stop=True)\
                        .then_inc(s["mxb"], 1)
                else:
                    pe.wait_ge(s["m_ready"], 1)
                    pe.wait_ge(s["split_ready"], 1)
                    flat = split.rearrange("p q c t -> p (q c t)")
                    for c in range(nblk):
                        bank, o = (4, c * P) if c < 8 else (7, HALF + (c - 8) * P)
                        r = pe.transpose(psb[:, bank, o:o + P], flat[:, c * P:(c + 1) * P], identb[:, :])
                    r.then_inc(s["split_turned"], 1)
                    pe.transpose(ps[:, 7, 0:P], m_tmp[:, 0:H, :].rearrange("p h t -> p (h t)"), ident[:, :])\
                        .then_inc(s["m_turned"], 1)

            for kind, t in PROLOGUE:
                if kind == "adj":
                    adj_in_rows(t)
                elif kind == "value":
                    value_rows(t)
                elif kind == "max":
                    maxima(t)
                elif kind == "hT":
                    features()
                elif kind == "fold":
                    fold()
                else:
                    score_vectors()

            def score(k, kk, carried):
                jt, i0, b = kk % NT, kk // NT % BLOCKS * HALF, kk // PER_HEAD
                if kk >= SLOTS or carried:
                    pe.wait_ge(s["leaked"], k - SLOTS + 1)
                if kk >= 2 or carried:
                    pe.wait_ge(s["selected"], k - 1)
                for r, bank in ((0, kk % SLOTS), (1, 4 + kk % 2)):
                    p0 = 32 * (2 * r + kk % 2)
                    m = pe.matmul(ps[:, bank, :], op_l[p0:p0 + 2 * PARTS, b, jt * P:(jt + 1) * P],
                                  op_r[p0:p0 + 2 * PARTS, b, i0:i0 + HALF], start=True, stop=True)
                m.then_inc(s["scores"], 1)

            def aggregate(k, kk, acc, carried, step):
                jt, blk, b = kk % NT, kk // NT, kk // PER_HEAD
                if kk % PER_HEAD == 0 and step is not None:
                    pe.wait_ge(valued[b], (step + 1) * 16)
                pe.wait_ge(s["weights"], k + 1)
                if jt == 0 and (blk >= 2 or carried):
                    pe.wait_ge(s["acc_free"], acc + blk - 1)
                pe.matmul(ps[0:DA, 6 + blk % 2, :], vst[:, b, jt, :], ring[:, kk % RING, :],
                          start=(jt == 0), stop=(jt == NT - 1)).then_inc(s["products"], 1)

            def tiles(base, n, step, acc, carried, drain):
                for kk in range(n + (LAG_P if drain else 0)):
                    if kk < n:
                        if kk % PER_HEAD == 0 and step is not None:
                            pe.wait_ge(staged[kk // PER_HEAD], (step + 1) * STAGED)
                        score(base + kk, kk, carried)
                    mm = kk - LAG_P
                    if mm >= 0:
                        aggregate(base + mm, mm, acc, carried, step)
                    elif carried:
                        aggregate(base + mm, mm + PAIR, acc - 2 * BLOCKS, carried, None)

            pe.wait_ge(s["adj_copied"], NT - HB)
            pe.wait_ge(s["adj_copied_b"], NT + HB)
            pe.wait_ge(s["m_copied"], 1)
            tiles(0, PAIR, 0, 0, False, False)
            with pe.Fori(1, H // 2) as i:
                tiles(i * PAIR, PAIR, i, i * (2 * BLOCKS), True, False)
            tiles(TILES0, 0, None, H * BLOCKS, True, True)
            pe.wait_ge(s["acc_free"], H * BLOCKS)
            for t in range(NT):
                if t >= 2:
                    pe.wait_ge(s["out_taken"], t - 1)
                for hh in range(H):
                    r = pe.transpose(ps[:, 2 * (t % 2) + hh // 4, hh % 4 * P:hh % 4 * P + DA],
                                     outT[0:DA, hh, t * P:(t + 1) * P], ident[0:DA, 0:DA])
                r.then_inc(s["out_turned"], 1)
            pe.wait_ge(s["h_ready"], 2)
            turn(0, lambda t: h[:, t, 0:DA], DA, s["h_turned"])
            pe.wait_ge(s["hT_ready"], 4)
            for t in range(NT):
                m = pe.matmul(ps[:, 4, t * 2 * E:(t + 1) * 2 * E], hT[0:D, t * P:(t + 1) * P], wkq[:, :], start=True, stop=True)
            m.then_inc(s["kqn_done"], 1)
            pe.wait_ge(s["kq_done"], 1)
            for bank, w in ((0, 1), (2, 0)):
                for t in range(NT):
                    r = pe.transpose(psb[0:ER, bank + t // 8, t % 8 * P:(t % 8 + 1) * P], kq_slot[:, w, t, :], identb[:, :])
                r.then_inc(s["kq_t"], 1)
            pe.wait_ge(s["mx_done"], 2)
            for w in range(2):
                r = pe.transpose(ps[0:1, 5, w * P:(w + 1) * P], small[:, w:w + 1], ident[:, :])
            r.then_inc(s["big_ready"], 1)
            pe.wait_ge(s["big_b"], 2)
            pe.matmul(ps[:, 5, 2 * P:2 * P + 1], onesf[0:1, :], small[0:1, 5:6], start=True, stop=True).then_inc(s["big_s"], 1)
            pe.wait_ge(s["kq_ready"], 2)
            for k in range(n1 + LAG_E):
                if k < n1:
                    (jt, b), p2 = TILES1[k], k % 2
                    if k >= 2:
                        pe.wait_ge(s["e_exp"], k - 1)
                    for w in range(2):
                        m = pe.matmul(ps[:, 2 * p2 + w, :], qT[0:ER, jt * P:(jt + 1) * P],
                                      kT[0:ER, b * TW + w * HALF:b * TW + (w + 1) * HALF], start=True, stop=True)
                    m.then_inc(s["e_scores"], 1)
                mm = k - LAG_E
                if mm >= 1 and mm % 2:
                    pe.wait_ge(s["e_masked"], mm + 1)
                    b = TILES1[mm][1]
                    for c in (2 * b, 2 * b + 1):
                        for w in range(2):
                            jt = TILES1[mm - 1 + w][0]
                            m = pe.matmul(ps[w * D:(w + 1) * D, 4 + c, :], h[:, jt, 1:DA], eT[:, jt, c * HALF:(c + 1) * HALF],
                                          start=(jt < 2), stop=(jt >= NT - 2))
                    m.then_inc(s["e_products"], 1)

            def turn_y(n, c):
                pe.wait_ge(s["y_read"], n * BLOCKS + c + 1)
                if n >= 1:
                    pe.wait_ge(s["y_ready"], (n - 1) * BLOCKS + c + 1)
                for j in range(TB):
                    r = pe.transpose(ps[:, c, j * P:(j + 1) * P], yT[:, (c * TB + j) * P:(c * TB + j + 1) * P], ident[:, :])
                r.then_inc(s["y_turned"], 1)

            for n in range(1, APPS):
                for c in range(BLOCKS):
                    pe.wait_ge(s["y_read"], (n - 1) * BLOCKS + c + 1)
                    for jp in range(NT // 2):
                        if c == 0:
                            for b in {1: {0: (0, 1), 2: (2,), 4: (3,)}}.get(n, {2: (3,)}).get(jp, ()):
                                turn_y(n - 1, b)
                            pe.wait_ge(s["y_ready"], (n - 1) * BLOCKS + jp * 2 // TB + 1)
                        elif jp == 2:
                            turn_y(n, c - 1)
                        for w in range(2):
                            jt = 2 * jp + w
                            m = pe.matmul(ps[w * D:(w + 1) * D, 4 + c, :], Y[n - 1][:, jt, :],
                                          eT[:, jt, c * HALF:(c + 1) * HALF],
                                          start=(jp == 0), stop=(jp == NT // 2 - 1))
                    m.then_inc(s["y_products"], 1)
            turn_y(APPS - 1, BLOCKS - 1)
            pe.transpose(ps[0:D, 4, 0:D], w2[:, :], ident[0:D, 0:D]).then_inc(s["w_turned"], 1)
            pe.wait_ge(s["w_copied"], 2)
            pe.matmul(ps[0:D, 5, 0:2], w2T[:, :], a12[:, :], start=True, stop=True).then_inc(s["wa_done"], 1)
            pe.wait_ge(s["h_ready"], 3)
            turn(0, lambda t: h[:, t, 0:DA], DA, s["h_turned"])
            pe.wait_ge(s["hT_ready"], 6)
            pe.wait_ge(s["wall_ready"], 2)
            for t in range(NT):
                m = pe.matmul(ps[:, 5, 16 + 2 * t:18 + 2 * t], hT[0:D, t * P:(t + 1) * P], w2a[:, :], start=True, stop=True)
            m.then_inc(s["s2_done"], 1)
            pe.wait_ge(s["mx_done"], 3)
            pe.transpose(ps[0:1, 4, 0:P], small[:, 0:1], ident[:, :]).then_inc(s["mx_read"], 1)
            pe.wait_ge(s["mxrow"], 2)
            pe.matmul(ps[:, 4, P:P + 1], onesf[0:1, :], small[0:1, 20:21], start=True, stop=True).then_inc(s["mxb"], 1)
            pe.wait_ge(s["split_ready"], 2)
            flat2 = split[:, 0:4, :, :].rearrange("p q c t -> p (q c t)")
            for c in range(2):
                r = pe.transpose(psb[0:96, 0, c * P:(c + 1) * P], flat2[:, c * 96:(c + 1) * 96], identb[:, :])
            r.then_inc(s["split_turned"], 1)
            pe.wait_ge(s["m_ready"], 2)
            pe.transpose(ps[0:NT, 4, 0:P], m_tmp[:, 0, :], ident[:, :]).then_inc(s["m_turned"], 1)
            for t in range(NT):
                m = pe.matmul(ps[:, 6 + t // 8, t % 8 * D:(t % 8 + 1) * D], hT[0:D, t * P:(t + 1) * P], w2[:, :],
                              start=True, stop=True)
            m.then_inc(s["wh_done"], 1)
            pe.wait_ge(s["m_copied"], 2)
            pe.wait_ge(s["ops2"], 16 * 9)
            pe.wait_ge(s["wh_ready"], 1)
            tiles(TILES0, PER_HEAD, None, H * BLOCKS, False, True)
            pe.wait_ge(s["acc_free"], (H + 1) * BLOCKS)
            for t in range(NT):
                r = pe.transpose(ps[:, t // 4, t % 4 * P:t % 4 * P + DA], outT[0:DA, 0, t * P:(t + 1) * P],
                                 ident[0:DA, 0:DA])
            r.then_inc(s["out_turned"], 1)
            pe.wait_ge(s["h_ready"], 4)
            pe.wait_ge(s["h2_ready"], 2)
            turn(0, lambda t: h[:, t, :], DX, s["h_turned"])
            turn(4, lambda t: g3[:, 0, t, :], DX, s["g_turned"])
            pe.wait_ge(s["g_read"], 1)
            pe.wait_ge(s["g_read_b"], 1)
            turn(0, lambda t: g3[:, 1, t, :], DX, s["g_turned"])
            pe.wait_ge(s["g_read"], 3)
            pe.wait_ge(s["g_read_b"], 3)
            for k in range(n3 + LAG_S):
                if k < n3:
                    jt, c = TILES3[k]
                    for bank, rhs, sem, read in ((0, rden, s["den"], s["den_c"]), (1, rdis, s["dis"], s["dis_c"])):
                        if k >= 1:
                            pe.wait_ge(read, k)
                        pe.matmul(ps[:, bank, :], lhs3[0:DX, jt * P:(jt + 1) * P], rhs[0:DX, c * HALF:(c + 1) * HALF],
                                  start=True, stop=True).then_inc(sem, 1)
                m = k - LAG_T
                if 0 <= m < n3 and MIRROR[m]:
                    pe.wait_ge(s["wgt"], m + 1)
                    if MIRRORS[m] > 2:
                        pe.wait_ge(s["mirrored"], MIRRORS[m] - 2)
                    for j in range(HALF // P):
                        r = pe.transpose(ps[:, 2 + MIRRORS[m] % 2, j * P:(j + 1) * P], wD[:, m % NW, j * P:(j + 1) * P],
                                         ident[:, :])
                    r.then_inc(s["turned3"], 1)
                m = k - LAG_S
                if m >= 0:
                    u, (jt, c) = m % NW, TILES3[m]
                    pe.wait_ge(s["wm3"], m + 1)
                    r = pe.matmul(ps[0:DX, 4 + c, :], h[:, jt, :], wC[:, u, :], start=(jt == 0),
                                  stop=(jt == (c + 1) * (HALF // P) - 1))
                    if MIRROR[m]:
                        pe.wait_ge(s["mirrored"], MIRRORS[m])
                        for j in range(HALF // P):
                            r = pe.matmul(ps[0:DX, 4 + jt * P // HALF, jt * P % HALF:jt * P % HALF + P],
                                          h[:, c * (HALF // P) + j, :], wA[:, u, j * P:(j + 1) * P],
                                          start=False, stop=False)
                    r.then_inc(s["sums"], 1)
            pe.wait_ge(s["y_read"], APPS * BLOCKS + 2)
            for t in range(NT):
                r = pe.transpose(ps[:, t // 4, t % 4 * P:t % 4 * P + DX], yT[0:DX, t * P:(t + 1) * P], ident[0:DX, 0:DX])
            r.then_inc(s["z_turned"], 1)


_INS = ['x', 'adj', 'L0_gnn_Qw', 'L0_gnn_Qb', 'L0_gnn_Kw', 'L0_gnn_Kb', 'L0_gnn_Vw', 'L0_gnn_Vb', 'L0_gnn_a',
        'L0_gnn_Pw', 'L0_gnn_Pb', 'L1_gnn_w_k', 'L1_gnn_w_q', 'L2_gnn_W', 'L2_gnn_a']


def kernel(**inputs):
    import numpy as _np
    import concourse.bacc as _bacc
    from concourse import mybir as _mybir
    from concourse.bass_utils import run_bass_kernel_spmd as _run

    nc = _bacc.Bacc("TRN2", target_bir_lowering=False, num_devices=1)
    arrays, args = {}, []
    for name in _INS:
        a = _np.ascontiguousarray(inputs[name])
        arrays[f"in_{name}_dram"] = a
        args.append(nc.dram_tensor(f"in_{name}_dram", a.shape, _mybir.dt.from_np(a.dtype), kind="ExternalInput").ap())
    out = nc.dram_tensor("out_dram", inputs["x"].shape, _mybir.dt.float32, kind="ExternalOutput").ap()
    gnn_stack(nc, *args, out)
    r = _run(nc, [arrays], core_ids=[0])
    return r.results[0]["out_dram"]
```
